# Optimizing a Trainium2 kernel written in Bass

```python
import numpy as np
import jax
import jax.numpy as jnp

def _softmax(x, axis=-1):
    return jax.nn.softmax(x, axis=axis)

def _gelu(x):
    return jax.nn.gelu(x, approximate=True)

def _silu(x):
    return jax.nn.silu(x)

def _sigmoid(x):
    return jax.nn.sigmoid(x)

def _layernorm(x, axis=-1, eps=1e-05):
    m = jnp.mean(x, axis=axis, keepdims=True)
    v = jnp.var(x, axis=axis, keepdims=True)
    return (x - m) / jnp.sqrt(v + eps)

def _scatter_add(tgt, idx, src, axis=0):
    return tgt.at[idx].add(src)

def _segment_sum(src, seg, n):
    return jax.ops.segment_sum(src, seg, n)
kernel_name = 'mk_gnn_resnorm_d4_gnn_r32_54eb95'

def setup_inputs(seed: int=0):
    np.random.seed(seed)
    _w = jnp.asarray

    def _rec_inputs():
        import jax
        import jax.numpy as jnp
        _gk = jax.random.key(seed)
        x = -0.0003713 + 1 * jax.random.normal(jax.random.fold_in(_gk, 1), (3125, 128), jnp.float32)
        src = jax.random.randint(jax.random.fold_in(_gk, 2), (100000,), 0, 3125, jnp.int32)
        dst = jax.random.randint(jax.random.fold_in(_gk, 3), (100000,), 0, 3125, jnp.int32)
        _o = jnp.argsort(dst, stable=True)
        src = src[_o]
        dst = dst[_o]
        edge_type_8 = jax.random.randint(jax.random.fold_in(_gk, 12), (100000,), 0, 8, jnp.int32)
        edge_weight = jax.random.uniform(jax.random.fold_in(_gk, 13), (100000,), jnp.float32, 0.0, 0.999998)
        return (x, src, dst, edge_type_8, edge_weight)
    x, src, dst, edge_type_8, edge_weight = _rec_inputs()

    def _L0_gnn_setup():
        import jax, jax.numpy as jnp
        import numpy as np
        K = 3
        key = jax.random.key(seed)
        k1, k2 = jax.random.split(key)
        N, E, D = (3125, 100000, 128)
        h_local = jax.random.normal(k1, (N, D), dtype=jnp.float32)
        edge_list = jax.random.randint(k2, (2, E), 0, N, dtype=jnp.int64)
        return {'h_local': h_local, 'edge_list': edge_list, 'num_nodes': N}
    _L0_gnn_all = _L0_gnn_setup()
    _L0_gnn_in = {k: v for k, v in _L0_gnn_all.items() if k in ()}
    del _L0_gnn_all

    def _L1_gnn_setup():
        import jax, jax.numpy as jnp
        from jax import lax
        import numpy as np
        N_NODES = 50000
        N_EDGES = 25000
        IN_CH = 128
        HEADS = 4
        OUT_CH = 32
        TOP_K = 8

        def _topk_mask_1h(e_h, row, k):
            E = e_h.shape[0]
            order = jnp.lexsort((-e_h, row))
            srow = row[order]
            seg_start = jnp.searchsorted(srow, srow, side='left')
            pos_in_seg = jnp.arange(E, dtype=seg_start.dtype) - seg_start
            keep_sorted = pos_in_seg < k
            return jnp.zeros((E,), jnp.bool_).at[order].set(keep_sorted)
        key = jax.random.key(seed)
        k1, k2, k3, k4 = jax.random.split(key, 4)
        x = jax.random.normal(k1, (N_NODES, IN_CH), jnp.float32)
        edge_index = jax.random.randint(k2, (2, N_EDGES), 0, N_NODES, dtype=jnp.int32)
        scale = float(np.sqrt(2.0 / (IN_CH + HEADS * OUT_CH)))
        W = jax.random.normal(k3, (IN_CH, HEADS * OUT_CH), jnp.float32) * scale
        att = jax.random.normal(k4, (HEADS, 2 * OUT_CH), jnp.float32) * 0.1
        return {'x': x, 'W': W, 'att': att, 'edge_index': edge_index}
    _L1_gnn_all = _L1_gnn_setup()
    _L1_gnn_in = {k: v for k, v in _L1_gnn_all.items() if k in ('W', 'att')}
    del _L1_gnn_all

    def _L2_gnn_setup():
        import jax, jax.numpy as jnp
        import numpy as np
        N_NODES = 3125
        N_EDGES = 18750
        IN_C = 128
        OUT_C = 128
        key = jax.random.key(seed)
        k1, k2, k3, k4, k5, k6 = jax.random.split(key, 6)
        x = jax.random.normal(k1, (N_NODES, IN_C), dtype=jnp.float32)
        edge_index = jax.random.randint(k2, (2, N_EDGES), 0, N_NODES, dtype=jnp.int64)
        edge_weight = jax.random.uniform(k3, (N_EDGES,), dtype=jnp.float32)
        W_neigh = jax.random.normal(k4, (IN_C, OUT_C), dtype=jnp.float32) / np.sqrt(IN_C)
        W_self = jax.random.normal(k5, (IN_C, OUT_C), dtype=jnp.float32) / np.sqrt(IN_C)
        b_self = jax.random.normal(k6, (OUT_C,), dtype=jnp.float32) * 0.01
        return {'x': x, 'edge_index': edge_index, 'edge_weight': edge_weight, 'W_neigh': W_neigh, 'W_self': W_self, 'b_self': b_self}
    _L2_gnn_all = _L2_gnn_setup()
    _L2_gnn_in = {k: v for k, v in _L2_gnn_all.items() if k in ('W_neigh', 'W_self', 'b_self')}
    del _L2_gnn_all

    def _L3_gnn_setup():
        import jax, jax.numpy as jnp
        import numpy as np
        N, E, D_IN, D_OUT, R = (50000, 25000, 128, 128, 8)
        key = jax.random.key(seed)
        ks = jax.random.split(key, 6)
        x = jax.random.normal(ks[0], (N, D_IN), dtype=jnp.float32)
        W_rel = jax.random.normal(ks[1], (R, D_IN, D_OUT), dtype=jnp.float32) * (1.0 / np.sqrt(D_IN))
        W_self_w = jax.random.normal(ks[2], (D_OUT, D_IN), dtype=jnp.float32) * (1.0 / np.sqrt(D_IN))
        W_self_b = jax.random.normal(ks[3], (D_OUT,), dtype=jnp.float32) * 0.01
        edge_index = jax.random.randint(ks[4], (2, E), 0, N, dtype=jnp.int32)
        edge_type = jax.random.randint(ks[5], (E,), 0, R, dtype=jnp.int32)
        return {'x': x, 'W_rel': W_rel, 'W_self_w': W_self_w, 'W_self_b': W_self_b, 'edge_index': edge_index, 'edge_type': edge_type}
    _L3_gnn_all = _L3_gnn_setup()
    _L3_gnn_in = {k: v for k, v in _L3_gnn_all.items() if k in ('W_rel', 'W_self_w', 'W_self_b')}
    del _L3_gnn_all
    return {'x': x, 'src': src, 'dst': dst, 'edge_type_8': edge_type_8, 'edge_weight': edge_weight, 'L1_gnn_W': _L1_gnn_in['W'], 'L1_gnn_att': _L1_gnn_in['att'], 'L2_gnn_W_neigh': _L2_gnn_in['W_neigh'], 'L2_gnn_W_self': _L2_gnn_in['W_self'], 'L2_gnn_b_self': _L2_gnn_in['b_self'], 'L3_gnn_W_rel': _L3_gnn_in['W_rel'], 'L3_gnn_W_self_w': _L3_gnn_in['W_self_w'], 'L3_gnn_W_self_b': _L3_gnn_in['W_self_b']}

def reference(x, src, dst, edge_type_8, edge_weight, L1_gnn_W, L1_gnn_att, L2_gnn_W_neigh, L2_gnn_W_self, L2_gnn_b_self, L3_gnn_W_rel, L3_gnn_W_self_w, L3_gnn_W_self_b):
    import jax
    import jax.numpy as jnp

    def _L0_gnn_ref(h_local, edge_list, num_nodes):
        import jax, jax.numpy as jnp
        import numpy as np
        K = 3
        N = num_nodes
        loops = jnp.broadcast_to(jnp.arange(N, dtype=edge_list.dtype)[None, :], (2, N))
        ei = jnp.concatenate([edge_list, loops], axis=1)
        row, col = (ei[0], ei[1])
        deg = jax.ops.segment_sum(jnp.ones_like(row, dtype=h_local.dtype), row, num_segments=N)
        deg_inv_sqrt = jnp.where(deg > 0, jax.lax.rsqrt(jnp.maximum(deg, 1.0)), 0.0)
        w = deg_inv_sqrt[row] * deg_inv_sqrt[col]

        def spmm(H):
            return jax.ops.segment_sum(w[:, None] * H[col], row, num_segments=N)
        H = h_local
        for _ in range(K):
            H = spmm(H)
        return H

    def _L1_gnn_ref(x, W, att, edge_index):
        import jax, jax.numpy as jnp
        from jax import lax
        import numpy as np
        N_NODES = 50000
        N_EDGES = 25000
        IN_CH = 128
        HEADS = 4
        OUT_CH = 32
        TOP_K = 8

        def _topk_mask_1h(e_h, row, k):
            E = e_h.shape[0]
            order = jnp.lexsort((-e_h, row))
            srow = row[order]
            seg_start = jnp.searchsorted(srow, srow, side='left')
            pos_in_seg = jnp.arange(E, dtype=seg_start.dtype) - seg_start
            keep_sorted = pos_in_seg < k
            return jnp.zeros((E,), jnp.bool_).at[order].set(keep_sorted)
        N = x.shape[0]
        H, C = (HEADS, OUT_CH)
        h = (x @ W).reshape(N, H, C)
        loops = jnp.arange(N, dtype=edge_index.dtype)
        ei = jnp.concatenate([edge_index, jnp.stack([loops, loops])], axis=1)
        row, col = (ei[0], ei[1])
        x_i = h[row]
        x_j = h[col]
        a_i, a_j = (att[:, :C], att[:, C:])
        e = jnp.einsum('ehc,hc->eh', x_i, a_i) + jnp.einsum('ehc,hc->eh', x_j, a_j)
        e = jax.nn.leaky_relu(e, negative_slope=0.2)
        mask = jax.vmap(lambda eh: _topk_mask_1h(eh, row, TOP_K), in_axes=1, out_axes=1)(e)
        e = jnp.where(mask, e, -jnp.inf)
        seg_max = jax.ops.segment_max(e, row, num_segments=N)
        ez = jnp.exp(e - lax.stop_gradient(seg_max)[row])
        denom = jax.ops.segment_sum(ez, row, num_segments=N)
        alpha = ez / denom[row]
        out = jax.ops.segment_sum(alpha[:, :, None] * x_j, row, num_segments=N)
        out = out.reshape(N, H * C)
        return jax.nn.elu(out)

    def _L2_gnn_ref(x, edge_index, edge_weight, W_neigh, W_self, b_self):
        import jax, jax.numpy as jnp
        import numpy as np
        N_NODES = 3125
        N_EDGES = 18750
        IN_C = 128
        OUT_C = 128
        src_idx = edge_index[0]
        dst_idx = edge_index[1]
        msg = x[src_idx] @ W_neigh * edge_weight[:, None]
        agg = jax.ops.segment_sum(msg, dst_idx, num_segments=x.shape[0])
        return agg + x @ W_self + b_self

    def _L3_gnn_ref(x, W_rel, W_self_w, W_self_b, edge_index, edge_type):
        import jax, jax.numpy as jnp
        import numpy as np
        N, E, D_IN, D_OUT, R = (50000, 25000, 128, 128, 8)
        n = x.shape[0]
        out = x @ W_self_w.T + W_self_b
        src = edge_index[0]
        dst = edge_index[1]
        h = jnp.einsum('nd,rdo->rno', x, W_rel)
        msg = h[edge_type, src]
        agg = jax.ops.segment_sum(msg, dst, num_segments=n)
        deg = jax.ops.segment_sum(jnp.ones_like(dst, dtype=x.dtype), dst, num_segments=n)
        deg = jnp.maximum(deg, 1.0)[:, None]
        out = jax.nn.relu(out + agg / deg)
        return out
    edge_index = jnp.stack([src, dst])
    x = _layernorm(x + _L0_gnn_ref(x, edge_index, 3125), axis=-1)
    x = _layernorm(x + _L1_gnn_ref(x, L1_gnn_W, L1_gnn_att, edge_index), axis=-1)
    x = _layernorm(x + _L2_gnn_ref(x, edge_index, edge_weight, L2_gnn_W_neigh, L2_gnn_W_self, L2_gnn_b_self), axis=-1)
    x = _layernorm(x + _L3_gnn_ref(x, L3_gnn_W_rel, L3_gnn_W_self_w, L3_gnn_W_self_b, edge_index, edge_type_8), axis=-1)
    return x

_drawn_inputs = setup_inputs


def setup_inputs(seed=0):
    import zlib

    import numpy as np

    out = dict(_drawn_inputs(seed))
    spreads = {}
    factors = {'L2_gnn_b_self': 8.0, 'L3_gnn_W_self_b': 8.0}
    for name, (base, spread) in spreads.items():
        noise = np.random.default_rng([zlib.crc32(name.encode()), seed]).standard_normal(out[name].shape)
        drawn = base * np.exp(spread * noise) if base else spread * noise
        out[name] = jnp.asarray(drawn.astype(out[name].dtype))
    for name, factor in factors.items():
        out[name] = (out[name] * factor).astype(out[name].dtype)
    return out
```

```python
from contextlib import ExitStack

import concourse.bass as bass
from concourse import mybir

F32, BF16 = mybir.dt.float32, mybir.dt.bfloat16
I32, U32, U16, I16 = mybir.dt.int32, mybir.dt.uint32, mybir.dt.uint16, mybir.dt.int16
ALU, ACT, AX = mybir.AluOpType, mybir.ActivationFunctionType, mybir.AxisListType
ds = bass.ds

P = 128
NODES, D, EDGES, HEADS, CH, TOPK, TYPES = 3125, 128, 100000, 4, 32, 8, 8
TILES = -(-NODES // P)
NP = TILES * P
FULL, REST = NODES // P, NODES % P
CHUNKS = 3
GE = CHUNKS * P
GROUPS = -(-EDGES // GE)
GT = -(-GROUPS // P)
LOADS = EDGES // GE // P + 2
WIN = 18
WINDOWS = -(-NODES // WIN)
KEYS = TILES * WIN
OFF = 20000.0
EPS = 1e-5
PARTS = 3


class Steps:

    def __init__(self, eng, sem):
        self.eng, self.sem, self.base, self.n = eng, sem, 0, 0

    def __call__(self, ins, tick=None):
        ins.then_inc(self.sem, 1)
        self.n += 1
        self.eng.wait_ge(self.sem, self.base + self.n)
        if tick is not None:
            self.eng.sem_inc(tick, 1)

    def enter(self, i, per):
        self.start, self.per = self.base + self.n, per
        self.base, self.n = self.start + i * per, 0

    def leave(self, count):
        assert self.n == self.per, (self.n, self.per)
        self.base, self.n = self.start + count * self.per, 0


class Graph:
    def __init__(self, nc, ctx, src, dst, etype, weight):
        self.nc, self.names = nc, 0
        self.src, self.dst, self.etype, self.weight = src, dst, etype, weight
        sb = lambda name, shape, dt: ctx.enter_context(nc.sbuf_tensor(name, shape, dt))
        self.ident = sb("ident", [P, P], F32)
        self.identb = sb("identb", [P, P], BF16)
        self.base = sb("base", [P, GT], F32)
        self.next_base = sb("next_base", [P, GT], F32)
        self.wide = sb("wide", [1, 1], I32)

    def phase(self):
        ctx = ExitStack()
        self.sems = []
        ctx.callback(self.clear, self.sems)
        return ctx

    def clear(self, sems):
        for sem in sems:
            self.nc.gpsimd.sem_clear(sem)
        if sems:
            self.nc.all_engine_barrier()

    def sem(self, ctx, name):
        self.names += 1
        self.sems.append(ctx.enter_context(self.nc.semaphore(f"{name}_{self.names}")))
        return self.sems[-1]

    def sbuf(self, ctx, name, shape, dt):
        self.names += 1
        return ctx.enter_context(self.nc.sbuf_tensor(f"{name}_{self.names}", shape, dt))

    def psum(self, ctx, name, shape, dt):
        self.names += 1
        return ctx.enter_context(self.nc.psum_tensor(f"{name}_{self.names}", shape, dt))


def load_edges(eng, dram, tile, sem):
    whole, full = EDGES // GE, EDGES // GE // P
    for t in range(full):
        eng.dma_start(tile[:, t, :], dram[t * P * GE:(t + 1) * P * GE].rearrange("(g e) -> g e", e=GE)).then_inc(sem, 16)
    eng.dma_start(tile[0:whole - full * P, full, :],
                  dram[full * P * GE:whole * GE].rearrange("(g e) -> g e", e=GE)).then_inc(sem, 16)
    eng.dma_start(tile[whole - full * P:whole - full * P + 1, full, 0:EDGES - whole * GE],
                  dram[whole * GE:EDGES].rearrange("(g e) -> g e", g=1)).then_inc(sem, 16)


def constants(g):
    nc = g.nc
    with g.phase() as ctx:
        zeroed, made = g.sem(ctx, "zeroed"), g.sem(ctx, "made")
        block = ctx.enter_context(nc.Block())

        @block.gpsimd
        def _(pool):
            pool.memset(g.ident[:, :], 0.0).then_inc(zeroed, 1)
            pool.memset(g.identb[:, :], 0.0).then_inc(zeroed, 1)
            pool.wait_ge(zeroed, 2)
            for m in (g.ident, g.identb):
                pool.affine_select(out=m[:, :], in_=m[:, :], compare_op=ALU.not_equal, fill=1.0, base=0,
                                   pattern=[[-1, P]], channel_multiplier=1).then_inc(made, 1)
            pool.wait_ge(made, 2)


def window_bases(g):
    nc = g.nc
    with g.phase() as ctx:
        dst_i = g.sbuf(ctx, "dst_i", [P, GT, GE], I32)
        dst_f = g.sbuf(ctx, "dst_f", [P, GT, GE], F32)
        dst_m = g.sbuf(ctx, "dst_m", [P, GT, GE], F32)
        hi = g.sbuf(ctx, "hi", [P, GT], F32)
        over = g.sbuf(ctx, "over", [P, 1], F32)
        ones = g.sbuf(ctx, "ones", [P, 1], F32)
        total = g.psum(ctx, "total", [1, 1], F32)
        filled, loaded, counted = g.sem(ctx, "filled"), g.sem(ctx, "loaded"), g.sem(ctx, "counted")
        vec = g.sem(ctx, "vec")
        block = ctx.enter_context(nc.Block())

        @block.sync
        def _(sp):
            sp.wait_ge(filled, 1)
            load_edges(sp, g.dst, dst_i, loaded)

        @block.vector
        def _(dve):
            step = Steps(dve, vec)
            nc.vector.memset(dst_i[:, :, :], int(OFF)).then_inc(filled, 1)
            step(nc.vector.memset(ones[:, :], 1.0))
            step(nc.vector.memset(g.next_base[:, :], 0.0))
            dve.wait_ge(loaded, 16 * LOADS)
            step(nc.vector.tensor_copy(dst_f[:, :, :], dst_i[:, :, :]))
            step(nc.vector.tensor_reduce(g.base[:, :], dst_f[:, :, :], AX.X, ALU.min))
            step(nc.vector.tensor_scalar(g.base[:, :], g.base[:, :], float(NODES - WIN), None, ALU.min))
            step(nc.vector.scalar_tensor_tensor(dst_m[:, :, :], dst_f[:, :, :], OFF, dst_f[:, :, :],
                                                ALU.is_lt, ALU.mult))
            step(nc.vector.tensor_reduce(hi[:, :], dst_m[:, :, :], AX.X, ALU.max))
            step(nc.vector.tensor_tensor(hi[:, :], hi[:, :], g.base[:, :], ALU.subtract))
            step(nc.vector.tensor_reduce(over[:, :], hi[:, :], AX.X, ALU.max))
            step(nc.vector.tensor_scalar(over[:, :], over[:, :], float(WIN), None, ALU.is_ge))
            dve.wait_ge(counted, 1)
            step(nc.vector.tensor_scalar(g.wide[:, :], total[:, :], 1.0, None, ALU.min))
            assert step.n == 11

        @block.tensor
        def _(pe):
            pe.wait_ge(vec, 10)
            nc.tensor.matmul(total[:, :], over[:, :], ones[:, :], start=True, stop=True).then_inc(counted, 1)


def edge_columns(g, ctx, kinds):
    g.keys_row = g.sbuf(ctx, "keys_row", [P, 512], I16)
    g.base_row = g.sbuf(ctx, "base_row", [1, GT * P], I32)
    sel = {kind: g.sbuf(ctx, kind, [P, GROUPS, CHUNKS], U32 if kind == "source" else F32) for kind in kinds}
    group_keys(g, sel)
    return sel


def group_keys(g, sel):
    nc = g.nc
    with g.phase() as ctx:
        raw, val = {}, {}
        for name in ("dst", "src", "etype", "weight"):
            if name == "etype" and "typed" not in sel or name == "weight" and "weight" not in sel:
                continue
            raw[name] = g.sbuf(ctx, name + "_raw", [P, GT, GE], F32 if name == "weight" else I32)
        place = g.sbuf(ctx, "place", [P, GT, GE], F32)
        bad = g.sbuf(ctx, "bad", [P, GT, GE], F32)
        for kind in sel:
            if kind not in ("place", "weight"):
                val[kind] = g.sbuf(ctx, kind + "_val", [P, GT, GE], F32)
        val["place"] = place
        if "weight" in sel:
            val["weight"] = raw["weight"]
        ps = [g.psum(ctx, "turned", [P, GE], F32) for _ in range(2)]
        filled, loaded, vec = g.sem(ctx, "filled"), g.sem(ctx, "loaded"), g.sem(ctx, "vec")
        turned, copied = g.sem(ctx, "turned"), g.sem(ctx, "copied")
        based = g.sem(ctx, "based")
        base_ps = g.psum(ctx, "base_ps", [1, GT * P], F32)
        jobs = [(kind, t) for kind in sel for t in range(GT)]
        dram = dict(dst=g.dst, src=g.src, etype=g.etype, weight=g.weight)
        counted = g.sem(ctx, "counted")
        block = ctx.enter_context(nc.Block())

        @block.gpsimd
        def _(pool):
            pool.iota(g.keys_row[:, :], [[1, 512]], base=0, channel_multiplier=0).then_inc(counted, 1)
            pool.wait_ge(counted, 1)

        @block.sync
        def _(sp):
            sp.wait_ge(filled, len(raw))
            for name in raw:
                load_edges(sp, dram[name], raw[name], loaded)

        @block.vector
        def _(dve):
            step = Steps(dve, vec)
            for name in raw:
                nc.vector.memset(raw[name][:, :, :], int(OFF) if name == "dst" else 0).then_inc(filled, 1)
            dve.wait_ge(based, 1)
            step(nc.vector.tensor_copy(g.base_row[:, :], base_ps[:, :]))
            dve.wait_ge(loaded, 16 * LOADS * len(raw))
            step(nc.vector.tensor_copy(place[:, :, :], raw["dst"][:, :, :]))
            for t in range(GT):
                step(nc.vector.tensor_scalar(place[:, t, :], place[:, t, :], g.base[:, t:t + 1], None,
                                             ALU.subtract))
            step(nc.vector.tensor_scalar(bad[:, :, :], place[:, :, :], float(WIN), OFF, ALU.is_ge, ALU.mult))
            step(nc.vector.tensor_tensor(bad[:, :, :], bad[:, :, :], place[:, :, :], ALU.add))
            step(nc.vector.tensor_scalar(place[:, :, :], place[:, :, :], 0.0, OFF, ALU.is_lt, ALU.mult))
            step(nc.vector.tensor_tensor(place[:, :, :], place[:, :, :], bad[:, :, :], ALU.add))
            if "source" in sel:
                step(nc.vector.tensor_copy(val["source"][:, :, :], raw["src"][:, :, :]))
            if "typed" in sel:
                step(nc.vector.tensor_copy(val["typed"][:, :, :], raw["etype"][:, :, :]))
                step(nc.vector.scalar_tensor_tensor(val["typed"][:, :, :], val["typed"][:, :, :], float(WIN),
                                                    place[:, :, :], ALU.mult, ALU.add))
            if "low" in sel:
                low, high = raw["dst"], raw["src"]
                step(nc.vector.tensor_scalar(low[:, :, :], raw["src"][:, :, :], P - 1, None, ALU.bitwise_and))
                step(nc.vector.tensor_scalar(high[:, :, :], raw["src"][:, :, :], 7, None,
                                             ALU.arith_shift_right))
                step(nc.vector.tensor_copy(val["low"][:, :, :], low[:, :, :]))
                step(nc.vector.tensor_copy(bad[:, :, :], high[:, :, :]))
                step(nc.vector.scalar_tensor_tensor(val["key"][:, :, :], bad[:, :, :], float(WIN),
                                                    place[:, :, :], ALU.mult, ALU.add))
            for n, (kind, t) in enumerate(jobs):
                dve.wait_ge(turned, n + 1)
                rows = min(GROUPS - P * t, P)
                nc.vector.tensor_copy(
                    sel[kind][:, P * t:P * t + rows, :],
                    ps[n % 2][:, :].rearrange("p (c g) -> p g c", g=P)[:, 0:rows, :]).then_inc(copied, 1)
            dve.wait_ge(copied, len(jobs))

        @block.tensor
        def _(pe):
            for t in range(GT):
                ins = nc.tensor.transpose(base_ps[:, t * P:(t + 1) * P], g.base[:, t:t + 1], g.ident[:, :])
            ins.then_inc(based, 1)
            n_vec = 6 + GT + ("source" in sel) + 2 * ("typed" in sel) + 5 * ("low" in sel)
            pe.wait_ge(vec, n_vec)
            for n, (kind, t) in enumerate(jobs):
                if n >= 2:
                    pe.wait_ge(copied, n - 1)
                for c in range(CHUNKS):
                    ins = nc.tensor.transpose(ps[n % 2][:, c * P:(c + 1) * P],
                                              val[kind][:, t, c * P:(c + 1) * P], g.ident[:, :])
                ins.then_inc(turned, 1)


def add_edges(g, adj, low, key):
    nc = g.nc
    UN = 3
    with g.phase() as ctx:
        hot_key = g.sbuf(ctx, "hot_key", [P, UN, CHUNKS, KEYS], BF16)
        hot_low = g.sbuf(ctx, "hot_low", [P, UN, CHUNKS, P], BF16)
        count = [g.psum(ctx, "count", [P, KEYS], F32) for _ in range(UN)]
        keys_made = g.sem(ctx, "keys_made")
        counted, added = g.sem(ctx, "counted"), g.sem(ctx, "added")
        block = ctx.enter_context(nc.Block())

        @block.vector
        def _(dve):
            dve.sem_inc(counted, UN)
            dve.sem_inc(added, UN)

            with dve.Fori(0, GROUPS // UN) as i:
                def make_keys(b):
                    dve.wait_ge(counted, i * UN + b + 1)
                    for c in range(CHUNKS):
                        ins = nc.vector.tensor_scalar(hot_key[:, b, c, :], g.keys_row[:, 0:KEYS],
                                                      key[:, ds(i * UN + b, 1), c], None, ALU.is_equal)
                        ins = nc.vector.tensor_scalar(hot_low[:, b, c, :], g.keys_row[:, 0:P],
                                                      low[:, ds(i * UN + b, 1), c], None, ALU.is_equal)
                    ins.then_inc(keys_made, 1)

                def add(b):
                    base = nc.vector.value_load(g.base_row[0:1, ds(i * UN + b, 1)], min_val=0,
                                                max_val=NP - WIN)
                    dve.wait_ge(counted, i * UN + b + UN + 1)
                    dve.wait_ge(added, i * UN + b + UN)
                    nc.vector.tensor_tensor(adj[:, :, ds(base, WIN)], adj[:, :, ds(base, WIN)],
                                            count[b][:, :].rearrange("p (t w) -> p t w", w=WIN),
                                            ALU.add).then_inc(added, 1)

                make_keys(0)
                for b in range(1, UN):
                    make_keys(b)
                    add(b - 1)
                add(UN - 1)

        @block.tensor
        def _(pe):
            with pe.Fori(0, GROUPS // UN) as i:
                for b in range(UN):
                    pe.wait_ge(keys_made, i * UN + b + 1)
                    pe.wait_ge(added, i * UN + b + 1)
                    for c in range(CHUNKS):
                        ins = nc.tensor.matmul(count[b][:, :], hot_low[:, b, c, :], hot_key[:, b, c, :],
                                               start=(c == 0), stop=(c == CHUNKS - 1))
                    ins.then_inc(counted, 1)


def in_windows(g, work):
    nc = g.nc
    flag = nc.values_load(g.wide[0:1, 0:1], min_val=0, max_val=1)
    with nc.If(flag):
        with nc.Fori(0, WINDOWS):
            with g.phase() as ctx:
                moved = g.sem(ctx, "moved")
                block = ctx.enter_context(nc.Block())

                @block.vector
                def _(dve):
                    nc.vector.tensor_copy(g.base[:, :], g.next_base[:, :]).then_inc(moved, 1)
                    dve.wait_ge(moved, 1)
                    nc.vector.tensor_scalar(g.next_base[:, :], g.next_base[:, :], float(WIN), None,
                                            ALU.add).then_inc(moved, 1)
                    dve.wait_ge(moved, 2)
            work()
    with nc.Else():
        work()


def degrees(g, adj, out):
    nc = g.nc
    with g.phase() as ctx:
        ones = g.sbuf(ctx, "ones", [P, 1], BF16)
        total = g.psum(ctx, "total", [P, TILES], F32)
        made, summed, copied = g.sem(ctx, "made"), g.sem(ctx, "summed"), g.sem(ctx, "copied")
        block = ctx.enter_context(nc.Block())

        @block.vector
        def _(dve):
            nc.vector.memset(ones[:, :], 1.0).then_inc(made, 1)
            dve.wait_ge(summed, TILES)
            nc.vector.tensor_copy(out[:, :], total[:, :]).then_inc(copied, 1)
            dve.wait_ge(copied, 1)

        @block.tensor
        def _(pe):
            pe.wait_ge(made, 1)
            with pe.Fori(0, TILES) as m:
                for k in range(TILES):
                    ins = nc.tensor.matmul(total[:, ds(m, 1)], adj[:, k, ds(m * P, P)], ones[:, :],
                                           start=(k == 0), stop=(k == TILES - 1))
                ins.then_inc(summed, 1)


def turn(g, adj):
    nc = g.nc
    SLOTS, BANK = 4, 1024
    flat = adj[:, :, :].rearrange("p k n -> p (k n)")
    pairs = [(d, TILES - d) for d in range(1, TILES)]
    with g.phase() as ctx:
        upper = g.psum(ctx, "upper", [P, SLOTS * BANK], BF16)
        lower = g.psum(ctx, "lower", [P, SLOTS * BANK], BF16)
        turned, up_put, low_put = g.sem(ctx, "turned"), g.sem(ctx, "up_put"), g.sem(ctx, "low_put")
        diag_turned, diag_put = g.sem(ctx, "diag_turned"), g.sem(ctx, "diag_put")
        block = ctx.enter_context(nc.Block())

        @block.tensor
        def _(pe):
            n = 0
            for d, count in pairs:
                with pe.Fori(0, count) as i:
                    slot = ((i + n) % SLOTS) * BANK
                    pe.wait_ge(up_put, i + n + 1)
                    pe.wait_ge(low_put, i + n + 1)
                    nc.tensor.transpose(upper[:, ds(slot, P)], flat[:, ds(i * (NP + P) + d * P, P)],
                                        g.identb[:, :])
                    nc.tensor.transpose(lower[:, ds(slot, P)], flat[:, ds(i * (NP + P) + d * NP, P)],
                                        g.identb[:, :]).then_inc(turned, 1)
                n += count
            for t in range(TILES):
                pe.wait_ge(low_put, n + SLOTS)
                if t >= 2:
                    pe.wait_ge(diag_put, t - 1)
                nc.tensor.transpose(lower[:, t % 2 * BANK:t % 2 * BANK + P], adj[:, t, t * P:(t + 1) * P],
                                    g.identb[:, :]).then_inc(diag_turned, 1)

        @block.scalar
        def _(act):
            act.sem_inc(up_put, SLOTS)
            n = 0
            for d, count in pairs:
                with act.Fori(0, count) as i:
                    act.wait_ge(turned, i + n + 1)
                    nc.scalar.copy(flat[:, ds(i * (NP + P) + d * NP, P)],
                                   upper[:, ds(((i + n) % SLOTS) * BANK, P)]).then_inc(up_put, 1)
                n += count

        @block.vector
        def _(dve):
            dve.sem_inc(low_put, SLOTS)
            n = 0
            for d, count in pairs:
                with dve.Fori(0, count) as i:
                    dve.wait_ge(turned, i + n + 1)
                    nc.vector.tensor_copy(flat[:, ds(i * (NP + P) + d * P, P)],
                                          lower[:, ds(((i + n) % SLOTS) * BANK, P)]).then_inc(low_put, 1)
                n += count
            for t in range(TILES):
                dve.wait_ge(diag_turned, t + 1)
                nc.vector.tensor_tensor(adj[:, t, t * P:(t + 1) * P], lower[:, t % 2 * BANK:t % 2 * BANK + P], g.identb[:, :],
                                        ALU.add).then_inc(diag_put, 1)
            dve.wait_ge(diag_put, TILES)


def split(step, nc, parts, value, rest):
    step(nc.vector.tensor_copy(parts(0), value))
    step(nc.vector.tensor_tensor(rest, value, parts(0), ALU.subtract))
    step(nc.vector.tensor_copy(parts(1), rest))
    return nc.vector.tensor_tensor(parts(2), rest, parts(1), ALU.subtract)


class Norm:

    def __init__(self, g, ctx):
        self.nc = g.nc
        self.stats = g.sbuf(ctx, "stats", [P, 6], F32)
        self.mv = g.sbuf(ctx, "mean_var", [P, 2], F32)
        self.eps = g.sbuf(ctx, "eps", [P, 1], F32)
        self.dev = g.sbuf(ctx, "deviation", [P, 1], F32)
        self.inv = g.sbuf(ctx, "inverse", [P, 1], F32)
        self.var_ready, self.dev_ready = g.sem(ctx, "var_ready"), g.sem(ctx, "dev_ready")
        self.tick = g.sem(ctx, "tick")

    def start(self, step):
        step(self.nc.vector.memset(self.eps[:, :], EPS))

    def vector(self, dve, step, out, value, n):
        nc = self.nc
        step(nc.vector.bn_stats(self.stats[:, :], value), self.tick)
        nc.vector.bn_aggr(self.mv[:, :], self.stats[:, :]).then_inc(self.var_ready, 1)
        dve.wait_ge(self.dev_ready, n)
        step(nc.vector.reciprocal(self.inv[:, :], self.dev[:, :]))
        return nc.vector.tensor_scalar(out, value, self.mv[:, 0:1], self.inv[:, :], ALU.subtract, ALU.mult)

    def scalar(self, act, n):
        act.wait_ge(self.var_ready, n)
        self.nc.scalar.activation(self.dev[:, :], self.mv[:, 1:2], ACT.Sqrt,
                                  bias=self.eps[:, :]).then_inc(self.dev_ready, 1)


def load_rows(eng, dram, tile, sem):
    eng.dma_start(tile[:, 0:FULL, :], dram[0:FULL * P, :].rearrange("(t p) d -> p t d", p=P)).then_inc(sem, 16)
    eng.dma_start(tile[0:REST, FULL, :], dram[FULL * P:NODES, :]).then_inc(sem, 16)


def propagate(g, adj, deg, x, x1):
    nc = g.nc
    UN, HOPS = 5, 3
    PW = PARTS * D
    with g.phase() as ctx:
        h = [g.sbuf(ctx, "hop_parts", [P, TILES, PW], BF16) for _ in range(2)]
        xin = h[1][:, :, :].rearrange("p t d -> p (t d)").bitcast(F32)[:, 0:TILES * D].rearrange(
            "p (t d) -> p t d", d=D)
        s1 = g.sbuf(ctx, "scale", [P, TILES], F32)
        s2 = g.sbuf(ctx, "scale_sq", [P, TILES], F32)
        val = g.sbuf(ctx, "val", [P, D], F32)
        rest = g.sbuf(ctx, "rest", [P, D], F32)
        xt = g.sbuf(ctx, "x_tile", [P, 2, D], F32)
        res = g.sbuf(ctx, "res", [P, 2, D], F32)
        norm = Norm(g, ctx)
        acc = [g.psum(ctx, "acc", [P, PW], F32) for _ in range(UN)]
        cleared, loaded, vec, root = g.sem(ctx, "cleared"), g.sem(ctx, "loaded"), g.sem(ctx, "vec"), g.sem(ctx, "root")
        parts_ready, summed, drained = g.sem(ctx, "parts_ready"), g.sem(ctx, "summed"), g.sem(ctx, "drained")
        xt_ready = [g.sem(ctx, "xt_ready") for _ in range(2)]
        stored = [g.sem(ctx, "stored") for _ in range(2)]
        xt_used, res_ready = g.sem(ctx, "xt_used"), g.sem(ctx, "res_ready")
        xt_clear = g.sem(ctx, "xt_clear")
        block = ctx.enter_context(nc.Block())

        @block.sync
        def _(sp):
            sp.wait_ge(cleared, 1)
            load_rows(sp, x, xin, loaded)
            sp.wait_ge(xt_clear, 1)
            for t in range(TILES):
                rows = min(NODES - t * P, P)
                if t >= 2:
                    sp.wait_ge(xt_used, t - 1)
                if t == FULL:
                    sp.wait_ge(xt_clear, 2)
                sp.dma_start(xt[0:rows, t % 2, :], x[t * P:t * P + rows, :]).then_inc(xt_ready[t % 2], 16)

        @block.tensor
        def _(pe):
            for hop in range(HOPS):
                pe.wait_ge(parts_ready, (hop + 1) * TILES)
                with pe.Fori(0, TILES // UN) as i:
                    for b in range(UN):
                        pe.wait_ge(drained, i * UN + b + hop * TILES + 1)
                        for k in range(TILES):
                            ins = nc.tensor.matmul(acc[b][:, :], adj[:, k, ds((i * UN + b) * P, P)],
                                                   h[hop % 2][:, k, :], start=(k == 0), stop=(k == TILES - 1))
                        ins.then_inc(summed, 1)

        @block.scalar
        def _(act):
            act.wait_ge(vec, 2)
            nc.scalar.activation(s1[:, :], deg[:, :], ACT.Sqrt).then_inc(root, 1)
            for t in range(TILES):
                norm.scalar(act, t + 1)
                if t >= 1:
                    act.wait_ge(res_ready, t)
                    act.dma_start(x1[(t - 1) * P:t * P, :], res[:, (t - 1) % 2, :]).then_inc(stored[(t - 1) % 2], 16)
            act.wait_ge(res_ready, TILES)
            act.dma_start(x1[(TILES - 1) * P:TILES * P, :], res[:, (TILES - 1) % 2, :])\
               .then_inc(stored[(TILES - 1) % 2], 16)
            act.wait_ge(stored[0], 16 * (TILES - TILES // 2))
            act.wait_ge(stored[1], 16 * (TILES // 2))

        @block.vector
        def _(dve):
            step = Steps(dve, vec)
            dve.sem_inc(drained, UN)
            nc.vector.memset(h[1][:, :, :].rearrange("p t d -> p (t d)").bitcast(U32)[:, FULL * D:TILES * D], 0)\
              .then_inc(cleared, 1)
            norm.start(step)
            step(nc.vector.memset(xt[:, :, :], 0.0))
            dve.sem_inc(xt_clear, 1)
            dve.wait_ge(root, 1)
            step(nc.vector.reciprocal(s1[:, :], s1[:, :]))
            step(nc.vector.tensor_tensor(s2[:, :], s1[:, :], s1[:, :], ALU.mult))
            dve.wait_ge(loaded, 32)
            with dve.Fori(0, TILES) as t:
                step.enter(t, 4)
                step(nc.vector.tensor_scalar(val[:, :], xin[:, ds(t, 1), :], s1[:, ds(t, 1)], None, ALU.mult))
                split(step, nc, lambda j: h[0][:, ds(t, 1), j * D:(j + 1) * D], val[:, :], rest[:, :])\
                    .then_inc(parts_ready, 1)
                step.leave(TILES)
                dve.wait_ge(parts_ready, t + 1)

            def total(hop, i, b):
                n = i * UN + b + hop * TILES
                dve.wait_ge(summed, n + 1)
                ins = nc.vector.tensor_reduce(val[:, :], acc[b][:, :].rearrange("p (j d) -> p d j", j=PARTS),
                                              AX.X, ALU.add)
                ins.then_inc(drained, 1)
                dve.wait_ge(drained, n + UN + 1)

            for hop in range(HOPS - 1):
                with dve.Fori(0, TILES // UN) as i:
                    step.enter(i, 4 * UN)
                    for b in range(UN):
                        t = i * UN + b
                        total(hop, i, b)
                        step(nc.vector.tensor_scalar(val[:, :], val[:, :], s2[:, ds(t, 1)], None, ALU.mult))
                        split(step, nc, lambda j: h[1 - hop % 2][:, ds(t, 1), j * D:(j + 1) * D], val[:, :],
                              rest[:, :]).then_inc(parts_ready, 1)
                        dve.wait_ge(parts_ready, t + (hop + 1) * TILES + 1)
                    step.leave(TILES // UN)
            for t in range(TILES):
                if t == FULL:
                    dve.wait_ge(xt_ready[t % 2], 16 * (t // 2))
                    step(nc.vector.memset(xt[:, t % 2, :], 0.0))
                    dve.sem_inc(xt_clear, 1)
                total(HOPS - 1, t // UN, t % UN)
                dve.wait_ge(xt_ready[t % 2], 16 * (t // 2 + 1))
                ins = nc.vector.scalar_tensor_tensor(val[:, :], val[:, :], s1[:, t:t + 1], xt[:, t % 2, :],
                                                     ALU.mult, ALU.add)
                ins.then_inc(xt_used, 1)
                dve.wait_ge(xt_used, t + 1)
                if t >= 2:
                    dve.wait_ge(stored[t % 2], 16 * (t // 2))
                norm.vector(dve, step, res[:, t % 2, :], val[:, :], t + 1).then_inc(res_ready, 1)
                dve.wait_ge(res_ready, t + 1)


ROW = CH + 1


class Attention:

    def __init__(self, g, ctx):
        dram = lambda name, shape: g.nc.dram_tensor(name, shape, F32, kind="Internal").ap()
        self.table = [dram(f"head_rows_{h}", [NP, ROW]) for h in range(HEADS)]
        self.scores = dram("neighbour_scores", [HEADS, NP])
        self.own = g.sbuf(ctx, "own_scores", [P, TILES, HEADS], F32)
        self.theirs = g.sbuf(ctx, "their_scores", [P, TILES, HEADS], F32)


def project(g, att, x1, w, a):
    nc = g.nc
    S = 2 * HEADS
    with g.phase() as ctx:
        wt = g.sbuf(ctx, "w", [P, D], F32)
        w_turned = g.sbuf(ctx, "w_turned", [P, D], F32)
        a_diag = g.sbuf(ctx, "a_diag", [P, S], F32)
        wa = g.sbuf(ctx, "wa", [P, S], F32)
        xt = g.sbuf(ctx, "x_tile", [P, 2, D], F32)
        x_turned = g.sbuf(ctx, "x_turned", [P, D], F32)
        rows = g.sbuf(ctx, "rows", [P, TILES, HEADS, ROW], F32)
        s_row = g.sbuf(ctx, "s_row", [S, NP], F32)
        ps_x, ps_h = g.psum(ctx, "ps_x", [P, D], F32), g.psum(ctx, "ps_h", [P, D], F32)
        ps_s, ps_c = g.psum(ctx, "ps_s", [S, P], F32), g.psum(ctx, "ps_c", [P, S], F32)
        cleared, w_loaded = g.sem(ctx, "cleared"), g.sem(ctx, "w_loaded")
        loaded = [g.sem(ctx, "loaded") for _ in range(2)]
        w_ps, w_sb = g.sem(ctx, "w_ps"), g.sem(ctx, "w_sb")
        x_ps, x_sb, h_ps, s_ps, s_sb, c_ps = (g.sem(ctx, n) for n in ("x_ps", "x_sb", "h_ps", "s_ps", "s_sb", "c_ps"))
        h_sb, c_sb = g.sem(ctx, "h_sb"), g.sem(ctx, "c_sb")
        stored = g.sem(ctx, "stored")
        block = ctx.enter_context(nc.Block())

        @block.sync
        def _(sp):
            sp.dma_start(wt[:, :], w).then_inc(w_loaded, 16)
            sp.wait_ge(cleared, 1)
            for h in range(HEADS):
                for half in range(2):
                    sp.dma_start(a_diag[h * CH:(h + 1) * CH, half * HEADS + h:half * HEADS + h + 1],
                                 a[h:h + 1, half * CH:(half + 1) * CH].rearrange("a c -> c a"),
                                 allow_slow_non_contiguous=True).then_inc(w_loaded, 16)
            for t in range(TILES):
                if t >= 2:
                    sp.wait_ge(x_ps, t - 1)
                sp.dma_start(xt[:, t % 2, :], x1[t * P:(t + 1) * P, :]).then_inc(loaded[t % 2], 16)
            sp.wait_ge(s_sb, TILES)
            sp.dma_start(att.scores, s_row[HEADS:S, :]).then_inc(stored, 16)
            sp.wait_ge(h_sb, TILES)
            sp.wait_ge(c_sb, 2 * TILES)
            for h in range(HEADS):
                sp.dma_start(att.table[h].rearrange("(t p) c -> p t c", p=P), rows[:, :, h, :]).then_inc(stored, 16)
            sp.wait_ge(stored, 16 * (1 + HEADS))

        @block.tensor
        def _(pe):
            pe.wait_ge(w_loaded, 16 * 9)
            nc.tensor.transpose(ps_x[:, :], wt[:, :], g.ident[:, :]).then_inc(w_ps, 1)
            pe.wait_ge(w_sb, 1)
            nc.tensor.matmul(ps_c[:, :], w_turned[:, :], a_diag[:, :], start=True, stop=True).then_inc(w_ps, 1)
            pe.wait_ge(w_sb, 2)
            for t in range(TILES):
                pe.wait_ge(loaded[t % 2], 16 * (t // 2 + 1))
                if t >= 1:
                    pe.wait_ge(x_sb, t)
                nc.tensor.transpose(ps_x[:, :], xt[:, t % 2, :], g.ident[:, :]).then_inc(x_ps, 1)
                pe.wait_ge(x_sb, t + 1)
                if t >= 1:
                    pe.wait_ge(s_sb, t)
                nc.tensor.matmul(ps_s[:, :], wa[:, :], x_turned[:, :], start=True, stop=True).then_inc(s_ps, 1)
                if t >= 1:
                    pe.wait_ge(h_sb, t)
                nc.tensor.matmul(ps_h[:, :], x_turned[:, :], wt[:, :], start=True, stop=True).then_inc(h_ps, 1)
                pe.wait_ge(s_sb, t + 1)
                if t >= 1:
                    pe.wait_ge(c_sb, 2 * t)
                nc.tensor.transpose(ps_c[:, :], s_row[:, t * P:(t + 1) * P], g.ident[0:S, 0:S]).then_inc(c_ps, 1)

        @block.scalar
        def _(act):
            for t in range(TILES):
                act.wait_ge(s_ps, t + 1)
                nc.scalar.copy(s_row[:, t * P:(t + 1) * P], ps_s[:, :]).then_inc(s_sb, 1)
                act.wait_ge(h_ps, t + 1)
                nc.scalar.copy(rows[:, t, :, 0:CH], ps_h[:, :].rearrange("p (h c) -> p h c", h=HEADS)).then_inc(h_sb, 1)

        @block.vector
        def _(dve):
            nc.vector.memset(a_diag[:, :], 0.0).then_inc(cleared, 1)
            dve.wait_ge(w_ps, 1)
            nc.vector.tensor_copy(w_turned[:, :], ps_x[:, :]).then_inc(w_sb, 1)
            dve.wait_ge(w_ps, 2)
            nc.vector.tensor_copy(wa[:, :], ps_c[:, :]).then_inc(w_sb, 1)
            for t in range(TILES):
                dve.wait_ge(x_ps, t + 1)
                if t >= 1:
                    dve.wait_ge(h_ps, t)
                nc.vector.tensor_copy(x_turned[:, :], ps_x[:, :]).then_inc(x_sb, 1)
                dve.wait_ge(c_ps, t + 1)
                nc.vector.tensor_copy(att.own[:, t, :], ps_c[:, 0:HEADS])
                nc.vector.tensor_copy(att.theirs[:, t, :], ps_c[:, HEADS:S]).then_inc(c_sb, 1)
                nc.vector.tensor_copy(rows[:, t, :, CH], ps_c[:, HEADS:S]).then_inc(c_sb, 1)


def rank(g, att, code):
    nc = g.nc
    HALF = [(0, 13), (13, TILES)]
    with g.phase() as ctx:
        score = g.sbuf(ctx, "score", [P, NP], F32)
        below = g.sbuf(ctx, "below", [P, 2, 13 * P], BF16)
        later = g.sbuf(ctx, "later", [P, P], BF16)
        ones = g.sbuf(ctx, "ones", [P, P], BF16)
        banks = [g.psum(ctx, "rank", [P, 512], F32) for _ in range(7)]
        made, loaded = g.sem(ctx, "made"), g.sem(ctx, "loaded")
        compared, summed, coded, diag = g.sem(ctx, "compared"), g.sem(ctx, "summed"), g.sem(ctx, "coded"), g.sem(ctx, "diag")
        read = g.sem(ctx, "read")
        block = ctx.enter_context(nc.Block())

        @block.gpsimd
        def _(pool):
            pool.memset(later[:, :], 1.0).then_inc(made, 1)
            pool.memset(ones[:, :], 1.0).then_inc(made, 1)
            pool.wait_ge(made, 2)
            pool.affine_select(out=later[:, :], in_=later[:, :], compare_op=ALU.is_gt, fill=0.0, base=0,
                               pattern=[[-1, P]], channel_multiplier=1).then_inc(made, 1)

        @block.sync
        def _(sp):
            for h in range(HEADS):
                if h >= 1:
                    sp.wait_ge(read, h)
                sp.dma_start(score[:, :], att.scores[h:h + 1, :].broadcast_to([P, NP])).then_inc(loaded, 16)

        def spans(lo, hi):
            first = 0 if lo == 0 else 4
            a = lo * P
            while a < hi * P:
                b = min(a + 512, hi * P)
                yield first + (a - lo * P) // 512, a, b
                a = b

        @block.vector
        def _(dve):
            dve.wait_ge(made, 3)
            n = nd = 0
            for h in range(HEADS):
                dve.wait_ge(loaded, 16 * (h + 1))
                for lo, hi in HALF:
                    for t in range(TILES):
                        if n >= 2:
                            dve.wait_ge(summed, n - 1)
                        buf, s = below[:, n % 2, :], att.theirs[:, t, h:h + 1]
                        left, right = min(max(t, lo), hi), min(max(t + 1, lo), hi)
                        if left > lo:
                            ins = nc.vector.tensor_scalar(buf[:, 0:(left - lo) * P], score[:, lo * P:left * P],
                                                          s, None, ALU.is_ge)
                        if hi > right:
                            ins = nc.vector.tensor_scalar(buf[:, (right - lo) * P:(hi - lo) * P],
                                                          score[:, right * P:hi * P], s, None, ALU.is_gt)
                        if left < right:
                            out, own = buf[:, (t - lo) * P:(t + 1 - lo) * P], score[:, t * P:(t + 1) * P]
                            nc.vector.scalar_tensor_tensor(out, own, s, later[:, :], ALU.is_ge, ALU.mult)\
                              .then_inc(diag, 1)
                            nd += 1
                            dve.wait_ge(diag, nd)
                            ins = nc.vector.scalar_tensor_tensor(out, own, s, out, ALU.is_gt, ALU.max)
                        ins.then_inc(compared, 1)
                        n += 1
                dve.wait_ge(compared, n)
                dve.sem_inc(read, 1)

        @block.tensor
        def _(pe):
            pe.wait_ge(made, 3)
            n = 0
            for h in range(HEADS):
                for k, (lo, hi) in enumerate(HALF):
                    if h >= 1:
                        pe.wait_ge(coded, 2 * (h - 1) + k + 1)
                    for t in range(TILES):
                        pe.wait_ge(compared, n + 1)
                        for bank, a, b in spans(lo, hi):
                            ins = nc.tensor.matmul(banks[bank][:, 0:b - a], ones[:, :],
                                                   below[:, n % 2, a - lo * P:b - lo * P],
                                                   start=(t == 0), stop=(t == TILES - 1))
                        ins.then_inc(summed, 1)
                        n += 1

        @block.scalar
        def _(act):
            for h in range(HEADS):
                for k, (lo, hi) in enumerate(HALF):
                    act.wait_ge(summed, (2 * h + k + 1) * TILES)
                    for bank, a, b in spans(lo, hi):
                        ins = nc.scalar.activation(code[:, h, a:b], banks[bank][:, 0:b - a], ACT.Copy,
                                                   bias=15.0, scale=16.0)
                    ins.then_inc(coded, 1)
            act.wait_ge(coded, 2 * HEADS)


def attend(g, att, adj, code, x1, x2):
    nc = g.nc
    HK = HEADS * TOPK
    BANK = 1024
    with g.phase() as ctx:
        mask = g.sbuf(ctx, "mask", [P, NP], I16)
        key = g.sbuf(ctx, "key", [P, NP], U16)
        best = g.sbuf(ctx, "best", [P, 2, HK], U32)
        where = g.sbuf(ctx, "where", [P, 2, HK], U32)
        rows = g.sbuf(ctx, "rows", [P, 2, HK, ROW], F32)
        xt = g.sbuf(ctx, "x_tile", [P, D], F32)
        res = g.sbuf(ctx, "res", [P, D], F32)
        low = g.sbuf(ctx, "low", [P, HK], U32)
        cnt, cum, kept = (g.sbuf(ctx, n, [P, HK], F32) for n in ("cnt", "cum", "kept"))
        again = g.sbuf(ctx, "again", [P, HK], F32)
        e, ez = g.sbuf(ctx, "e", [P, HK], F32), g.sbuf(ctx, "ez", [P, HK], F32)
        den = g.sbuf(ctx, "den", [P, HEADS], F32)
        o, neg = g.sbuf(ctx, "o", [P, D], F32), g.sbuf(ctx, "neg", [P, D], F32)
        norm = Norm(g, ctx)
        edges = [g.psum(ctx, "edges", [P, 4 * BANK], BF16) for _ in range(2)]
        vec, turned, masked, keyed = (g.sem(ctx, n) for n in ("vec", "turned", "masked", "keyed"))
        found, pool_tick = g.sem(ctx, "found"), g.sem(ctx, "pool_tick")
        gathered = [g.sem(ctx, "gathered") for _ in range(2)]
        used = g.sem(ctx, "used")
        e_ready, ez_ready, neg_ready, elu_ready = (g.sem(ctx, n) for n in ("e_ready", "ez_ready", "neg_ready", "elu_ready"))
        x_ready, x_used, res_ready, stored = (g.sem(ctx, n) for n in ("x_ready", "x_used", "res_ready", "stored"))
        block = ctx.enter_context(nc.Block())

        def over_tiles(eng, body, step=None, per=0):
            with eng.Fori(0, TILES // 2) as i:
                if step:
                    step.enter(i, 2 * per)
                for b in range(2):
                    body(i * 2 + b, b)
                if step:
                    step.leave(TILES // 2)
            body(TILES - 1, 0)

        @block.tensor
        def _(pe):
            def tile(q, b):
                pe.wait_ge(masked, q + 1)
                for k in range(TILES):
                    ins = nc.tensor.transpose(edges[b][:, k * P:(k + 1) * P],
                                              adj[:, k, ds(q * P, P)], g.identb[:, :])
                ins.then_inc(turned, 1)
            over_tiles(pe, tile)

        @block.gpsimd
        def _(pool):
            def tile(q, b):
                pool.wait_ge(used, q + 1)
                for h in range(HEADS):
                    pool.wait_ge(found, q * HEADS + h + 1)
                    pool.sem_inc(pool_tick, 1)
                    for k in range(TOPK):
                        j = h * TOPK + k
                        pool.indirect_dma_start(rows[:, b, j, :], None, att.table[h],
                                                bass.IndirectOffsetOnAxis(ap=where[:, b, j:j + 1], axis=0))\
                            .then_inc(gathered[b], 16)
            over_tiles(pool, tile)

        @block.sync
        def _(sp):
            with sp.Fori(0, TILES) as t:
                sp.wait_ge(x_used, t + 1)
                sp.dma_start(xt[:, :], x1[ds(t * P, P), :]).then_inc(x_ready, 16)
                sp.wait_ge(res_ready, t + 1)
                sp.dma_start(x2[ds(t * P, P), :], res[:, :]).then_inc(stored, 16)
            sp.wait_ge(stored, 16 * TILES + 16)

        @block.scalar
        def _(act):
            with act.Fori(0, TILES) as t:
                act.wait_ge(e_ready, t + 1)
                nc.scalar.activation(ez[:, :], e[:, :], ACT.Exp).then_inc(ez_ready, 1)
                act.wait_ge(neg_ready, t + 1)
                nc.scalar.activation(neg[:, :], neg[:, :], ACT.Exp).then_inc(elu_ready, 1)
                norm.scalar(act, t + 1)

        @block.vector
        def _(dve):
            step = Steps(dve, vec)
            dve.sem_inc(masked, 2)
            dve.sem_inc(used, 2)
            dve.sem_inc(x_used, 1)
            dve.sem_inc(stored, 16)
            norm.start(step)
            step(nc.vector.memset(again[:, :], 1.0))
            step(nc.vector.memset(again[:, :].rearrange("p (h k) -> p h k", k=TOPK)[:, :, 0:1], 0.0))
            heads = lambda t: t.rearrange("p (h k) -> p h k", k=TOPK)

            def search(q, b):
                dve.wait_ge(turned, q + 1)
                nc.vector.tensor_scalar(mask[:, :], edges[b][:, 0:NP], float(TOPK), -1.0, ALU.min, ALU.mult)\
                  .then_inc(masked, 1)
                dve.wait_ge(masked, q + 3)
                for h in range(HEADS):
                    step(nc.vector.tensor_tensor(key[:, :], code[:, h, :], mask[:, :].bitcast(U16),
                                                 ALU.bitwise_and), norm.tick)
                    at = slice(h * TOPK, (h + 1) * TOPK)
                    step(nc.vector.max(best[:, b, at], key[:, :]), norm.tick)
                    nc.vector.max_index(where[:, b, at], best[:, b, at], key[:, :]).then_inc(found, 1)
                    dve.wait_ge(found, q * HEADS + h + 1)

            def combine(q, b, uses):
                step(nc.vector.tensor_scalar(low[:, :], best[:, b, :], 15, None, ALU.bitwise_and))
                step(nc.vector.tensor_scalar(cnt[:, :], low[:, :], -1.0, 16.0, ALU.mult, ALU.add))
                step(nc.vector.scalar_tensor_tensor(cnt[:, :], best[:, b, :], 0.0, cnt[:, :], ALU.is_gt, ALU.mult))
                step(nc.vector.tensor_tensor_scan(cum[:, :], again[:, :], cnt[:, :], 0.0, ALU.mult, ALU.add))
                step(nc.vector.tensor_tensor(cum[:, :], cum[:, :], cnt[:, :], ALU.subtract))
                step(nc.vector.tensor_scalar(cum[:, :], cum[:, :], -1.0, float(TOPK), ALU.mult, ALU.add))
                step(nc.vector.scalar_tensor_tensor(kept[:, :], cum[:, :], 0.0, cnt[:, :], ALU.max, ALU.min))
                dve.wait_ge(gathered[b], uses * 16 * HK)
                step(nc.vector.tensor_tensor(heads(e[:, :]), heads(rows[:, b, :, CH]),
                                             att.own[:, ds(q, 1), :].rearrange("p a h -> p h a")
                                             .broadcast_to([P, HEADS, TOPK]), ALU.add))
                step(nc.vector.scalar_tensor_tensor(e[:, :], e[:, :], 0.2, e[:, :], ALU.mult, ALU.max))
                step(nc.vector.tensor_tensor(heads(cum[:, :]), heads(e[:, :]),
                                             heads(e[:, :])[:, :, 0:1].broadcast_to([P, HEADS, TOPK]), ALU.subtract))
                nc.vector.tensor_scalar(e[:, :], cum[:, :], 0.0, None, ALU.min).then_inc(e_ready, 1)
                dve.wait_ge(ez_ready, q + 1)
                step(nc.vector.tensor_tensor(ez[:, :], ez[:, :], kept[:, :], ALU.mult))
                step(nc.vector.tensor_reduce(den[:, :], heads(ez[:, :]), AX.X, ALU.add))
                step(nc.vector.reciprocal(den[:, :], den[:, :]))
                step(nc.vector.tensor_tensor(heads(ez[:, :]), heads(ez[:, :]),
                                             den[:, :].unsqueeze(2).broadcast_to([P, HEADS, TOPK]), ALU.mult))
                step(nc.vector.tensor_tensor(rows[:, b, :, 0:CH], rows[:, b, :, 0:CH],
                                             ez[:, :].unsqueeze(2).broadcast_to([P, HK, CH]), ALU.mult))
                nc.vector.tensor_reduce(o[:, :].rearrange("p (h c) -> p h c", h=HEADS),
                                        rows[:, b, :, 0:CH].rearrange("p (h k) c -> p h c k", k=TOPK),
                                        AX.X, ALU.add).then_inc(used, 1)
                dve.wait_ge(used, q + 3)
                nc.vector.tensor_scalar(neg[:, :], o[:, :], 0.0, None, ALU.min).then_inc(neg_ready, 1)
                dve.wait_ge(elu_ready, q + 1)
                step(nc.vector.scalar_tensor_tensor(o[:, :], o[:, :], 0.0, neg[:, :], ALU.max, ALU.add))
                dve.wait_ge(x_ready, q * 16 + 16)
                nc.vector.scalar_tensor_tensor(o[:, :], o[:, :], -1.0, xt[:, :], ALU.add, ALU.add).then_inc(x_used, 1)
                dve.wait_ge(x_used, q + 2)
                dve.wait_ge(stored, q * 16 + 16)
                norm.vector(dve, step, res[:, :], o[:, :], q + 1).then_inc(res_ready, 1)
                dve.wait_ge(res_ready, q + 1)

            per = 8 + 18
            search(0, 0)
            with dve.Fori(0, TILES // 2) as i:
                step.enter(i, 2 * per)
                search(i * 2 + 1, 1)
                combine(i * 2, 0, i + 1)
                search(i * 2 + 2, 0)
                combine(i * 2 + 1, 1, i + 1)
                step.leave(TILES // 2)
            combine(TILES - 1, 0, TILES // 2 + 1)


def gather_sum(g, cols, key, x, acc, width, weight=None):
    nc = g.nc
    UN = 3
    with g.phase() as ctx:
        spot = g.sbuf(ctx, "spot", [P, UN, CHUNKS], U32)
        rows = g.sbuf(ctx, "rows", [P, UN, CHUNKS, D], F32)
        hot = g.sbuf(ctx, "hot", [P, UN, CHUNKS, width], F32)
        sums = [g.psum(ctx, "sums", [P, width], F32) for _ in range(UN)]
        staged, hot_made, summed, added = (g.sem(ctx, n) for n in ("staged", "hot_made", "summed", "added"))
        tick = g.sem(ctx, "tick")
        gathered = [g.sem(ctx, "gathered") for _ in range(UN)]
        block = ctx.enter_context(nc.Block())

        @block.gpsimd
        def _(pool):
            with pool.Fori(0, GROUPS // UN) as i:
                for b in range(UN):
                    pool.wait_ge(summed, i * UN + b + 1)
                    nc.gpsimd.tensor_copy(spot[:, b, :], cols["source"][:, ds(i * UN + b, 1), :]).then_inc(staged, 1)
                    pool.wait_ge(staged, i * UN + b + 1)
                    pool.sem_inc(tick, 1)
                    for c in range(CHUNKS):
                        pool.indirect_dma_start(rows[:, b, c, :], None, x,
                                                bass.IndirectOffsetOnAxis(ap=spot[:, b, c:c + 1], axis=0))\
                            .then_inc(gathered[b], 16)

        @block.vector
        def _(dve):
            dve.sem_inc(summed, UN)
            dve.sem_inc(added, UN)
            with dve.Fori(0, GROUPS // UN) as i:
                def make(b):
                    dve.wait_ge(summed, i * UN + b + 1)
                    for c in range(CHUNKS):
                        at = cols[key][:, ds(i * UN + b, 1), c]
                        if weight:
                            ins = nc.vector.tensor_scalar(hot[:, b, c, :], g.keys_row[:, 0:width], at,
                                                          cols[weight][:, ds(i * UN + b, 1), c],
                                                          ALU.is_equal, ALU.mult)
                        else:
                            ins = nc.vector.tensor_scalar(hot[:, b, c, :], g.keys_row[:, 0:width], at, None,
                                                          ALU.is_equal)
                    ins.then_inc(hot_made, 1)

                def add(b):
                    base = nc.vector.value_load(g.base_row[0:1, ds(i * UN + b, 1)], min_val=0, max_val=NP - WIN)
                    dve.wait_ge(summed, i * UN + b + UN + 1)
                    dve.wait_ge(added, i * UN + b + UN)
                    nc.vector.tensor_tensor(acc[:, :, ds(base, WIN)], acc[:, :, ds(base, WIN)],
                                            sums[b][:, :].rearrange("p (r w) -> p r w", w=WIN),
                                            ALU.add).then_inc(added, 1)

                make(0)
                for b in range(1, UN):
                    make(b)
                    add(b - 1)
                add(UN - 1)

        @block.tensor
        def _(pe):
            with pe.Fori(0, GROUPS // UN) as i:
                for b in range(UN):
                    pe.wait_ge(hot_made, i * UN + b + 1)
                    pe.wait_ge(added, i * UN + b + 1)
                    pe.wait_ge(gathered[b], i * (16 * CHUNKS) + 16 * CHUNKS)
                    for c in range(CHUNKS):
                        ins = nc.tensor.matmul(sums[b][:, :], rows[:, b, c, :], hot[:, b, c, :],
                                               start=(c == 0), stop=(c == CHUNKS - 1))
                    ins.then_inc(summed, 1)


def combine_layer(g, acc, w_agg, w_self, self_turned, bias, x, out, in_deg):
    nc = g.nc
    R = w_agg.shape[0]
    with g.phase() as ctx:
        wt = g.sbuf(ctx, "w_agg", [P, R, D], F32)
        ws = g.sbuf(ctx, "w_self", [P, D], F32)
        ws_in = g.sbuf(ctx, "w_self_in", [P, D], F32)
        brow = g.sbuf(ctx, "bias_row", [1, D], F32)
        ones = g.sbuf(ctx, "ones", [1, P], F32)
        inv = g.sbuf(ctx, "inverse_degree", [P, TILES], F32)
        xt = g.sbuf(ctx, "x_tile", [P, 2, D], F32)
        x_turned = g.sbuf(ctx, "x_turned", [P, 2, D], F32)
        part = g.sbuf(ctx, "part", [P, D], F32)
        val = g.sbuf(ctx, "val", [P, D], F32)
        res = g.sbuf(ctx, "res", [P, 2, D], F32)
        norm = Norm(g, ctx)
        ps_x = g.psum(ctx, "ps_x", [P, D], F32)
        ps_a = [g.psum(ctx, "ps_agg", [P, D], F32) for _ in range(2)]
        ps_s = [g.psum(ctx, "ps_self", [P, D], F32) for _ in range(2)]
        w_loaded, vec, w_ps, w_sb = (g.sem(ctx, n) for n in ("w_loaded", "vec", "w_ps", "w_sb"))
        loaded = [g.sem(ctx, "loaded") for _ in range(2)]
        stored = [g.sem(ctx, "stored") for _ in range(2)]
        x_ps, x_sb, summed, part_made, used, res_ready = (
            g.sem(ctx, n) for n in ("x_ps", "x_sb", "summed", "part_made", "used", "res_ready"))
        block = ctx.enter_context(nc.Block())

        def store(sp, t):
            rows = min(out.shape[0] - t * P, P)
            sp.wait_ge(res_ready, t + 1)
            sp.dma_start(out[t * P:t * P + rows, :], res[0:rows, t % 2, :]).then_inc(stored[t % 2], 16)

        @block.sync
        def _(sp):
            sp.dma_start(wt[:, :, :], w_agg.rearrange("r i o -> i r o")).then_inc(w_loaded, 16)
            sp.dma_start(ws_in[:, :], w_self).then_inc(w_loaded, 16)
            sp.dma_start(brow[:, :], bias.rearrange("(a n) -> a n", a=1)).then_inc(w_loaded, 16)
            for t in range(TILES):
                if t >= 2:
                    sp.wait_ge(used, t - 1)
                sp.dma_start(xt[:, t % 2, :], x[t * P:(t + 1) * P, :]).then_inc(loaded[t % 2], 16)
                if t >= 1:
                    store(sp, t - 1)
            store(sp, TILES - 1)
            sp.wait_ge(stored[0], 16 * (TILES - TILES // 2))
            sp.wait_ge(stored[1], 16 * (TILES // 2))

        @block.tensor
        def _(pe):
            pe.wait_ge(w_loaded, 48)
            pe.wait_ge(vec, 1)
            if self_turned:
                nc.tensor.transpose(ps_x[:, :], ws_in[:, :], g.ident[:, :]).then_inc(w_ps, 1)
            pe.wait_ge(w_sb, 1)
            for t in range(TILES):
                b = t % 2
                pe.wait_ge(loaded[b], 16 * (t // 2 + 1))
                if t >= 1:
                    pe.wait_ge(x_sb, t)
                nc.tensor.transpose(ps_x[:, :], xt[:, b, :], g.ident[:, :]).then_inc(x_ps, 1)
                if t >= 2:
                    pe.wait_ge(used, t - 1)
                for r in range(R):
                    nc.tensor.matmul(ps_a[b][:, :], acc[:, r, t * P:(t + 1) * P], wt[:, r, :],
                                     start=(r == 0), stop=(r == R - 1))
                nc.tensor.matmul(ps_s[b][:, :], ones[:, :], brow[:, :], start=True, stop=False)
                pe.wait_ge(x_sb, t + 1)
                nc.tensor.matmul(ps_s[b][:, :], x_turned[:, b, :], ws[:, :], start=False, stop=True)\
                  .then_inc(summed, 1)

        @block.scalar
        def _(act):
            for t in range(TILES):
                act.wait_ge(summed, t + 1)
                if t >= 1:
                    act.wait_ge(used, t)
                if in_deg is None:
                    nc.scalar.copy(part[:, :], ps_a[t % 2][:, :]).then_inc(part_made, 1)
                else:
                    nc.scalar.activation(part[:, :], ps_a[t % 2][:, :], ACT.Copy, scale=inv[:, t:t + 1])\
                      .then_inc(part_made, 1)
                norm.scalar(act, t + 1)

        @block.vector
        def _(dve):
            step = Steps(dve, vec)
            step(nc.vector.memset(ones[:, :], 1.0))
            norm.start(step)
            if in_deg is not None:
                step(nc.vector.tensor_scalar(inv[:, :], in_deg, 1.0, None, ALU.max))
                step(nc.vector.reciprocal(inv[:, :], inv[:, :]))
            dve.wait_ge(w_loaded, 48)
            if self_turned:
                dve.wait_ge(w_ps, 1)
                nc.vector.tensor_copy(ws[:, :], ps_x[:, :]).then_inc(w_sb, 1)
            else:
                nc.vector.tensor_copy(ws[:, :], ws_in[:, :]).then_inc(w_sb, 1)
            for t in range(TILES):
                b = t % 2
                dve.wait_ge(x_ps, t + 1)
                if t >= 2:
                    dve.wait_ge(summed, t - 1)
                nc.vector.tensor_copy(x_turned[:, b, :], ps_x[:, :]).then_inc(x_sb, 1)
                dve.wait_ge(part_made, t + 1)
                step(nc.vector.tensor_tensor(val[:, :], part[:, :], ps_s[b][:, :], ALU.add))
                if in_deg is None:
                    ins = nc.vector.tensor_tensor(val[:, :], val[:, :], xt[:, b, :], ALU.add)
                else:
                    ins = nc.vector.scalar_tensor_tensor(val[:, :], val[:, :], 0.0, xt[:, b, :], ALU.max, ALU.add)
                ins.then_inc(used, 1)
                dve.wait_ge(used, t + 1)
                if t >= 2:
                    dve.wait_ge(stored[b], 16 * (t // 2))
                norm.vector(dve, step, res[:, b, :], val[:, :], t + 1).then_inc(res_ready, 1)
                dve.wait_ge(res_ready, t + 1)


def clear_tiles(g, tiles):
    nc = g.nc
    with g.phase() as ctx:
        zeroed = g.sem(ctx, "zeroed")
        block = ctx.enter_context(nc.Block())

        @block.vector
        def _(dve):
            for t in tiles:
                nc.vector.memset(t, 0).then_inc(zeroed, 1)
            dve.wait_ge(zeroed, len(tiles))


def gather_layer(g, kinds, key, width, weight, x, out, w_agg, w_self, self_turned, bias, in_deg):
    with ExitStack() as ctx:
        acc = g.sbuf(ctx, "acc", [P, width // WIN, NP], F32)
        clear_tiles(g, [acc[:, :, :].bitcast(U32), g.next_base[:, :].bitcast(U32)])

        def work():
            with ExitStack() as inner:
                cols = edge_columns(g, inner, kinds)
                gather_sum(g, cols, key, x, acc, width, weight)

        in_windows(g, work)
        combine_layer(g, acc, w_agg, w_self, self_turned, bias, x, out, in_deg)


def gnn(nc, x, src, dst, edge_type, edge_weight, att_w, att_a, w_neigh, w_self, b_self, w_rel, w_root, b_root, out):
    hidden = [nc.dram_tensor(f"x{n}", [NP, D], F32, kind="Internal").ap() for n in (1, 2, 3)]
    with ExitStack() as ctx:
        g = Graph(nc, ctx, src, dst, edge_type, edge_weight)
        out_deg, in_deg = g.sbuf(ctx, "out_deg", [P, TILES], F32), g.sbuf(ctx, "in_deg", [P, TILES], F32)
        constants(g)
        window_bases(g)
        with ExitStack() as mid:
            adj = g.sbuf(mid, "adj", [P, TILES, NP], BF16)
            clear_tiles(g, [adj[:, :, :].bitcast(U32)])

            def work():
                with ExitStack() as inner:
                    cols = edge_columns(g, inner, ("low", "key"))
                    add_edges(g, adj, cols["low"], cols["key"])

            in_windows(g, work)
            degrees(g, adj, in_deg)
            turn(g, adj)
            degrees(g, adj, out_deg)
            propagate(g, adj, out_deg, x, hidden[0])
            att = Attention(g, mid)
            project(g, att, hidden[0], att_w, att_a)
            code = g.sbuf(mid, "code", [P, HEADS, NP], U16)
            rank(g, att, code)
            attend(g, att, adj, code, hidden[0], hidden[1])
        gather_layer(g, ("place", "weight", "source"), "place", WIN, "weight", hidden[1], hidden[2],
                     w_neigh.rearrange("(r i) o -> r i o", r=1), w_self, False, b_self, None)
        gather_layer(g, ("typed", "source"), "typed", TYPES * WIN, None, hidden[2], out,
                     w_rel, w_root, True, b_root, in_deg[:, :])


_INS = ['x', 'src', 'dst', 'edge_type_8', 'edge_weight', 'L1_gnn_W', 'L1_gnn_att', 'L2_gnn_W_neigh',
        'L2_gnn_W_self', 'L2_gnn_b_self', 'L3_gnn_W_rel', 'L3_gnn_W_self_w', 'L3_gnn_W_self_b']


def kernel(**inputs):
    import numpy as np
    import concourse.bacc as bacc
    from concourse.bass_utils import run_bass_kernel_spmd

    nc = bacc.Bacc("TRN2", target_bir_lowering=False, num_devices=1)
    arrays, args = {}, []
    for name in _INS:
        a = np.ascontiguousarray(inputs[name])
        arrays[f"in_{name}"] = a
        args.append(nc.dram_tensor(f"in_{name}", a.shape, mybir.dt.from_np(a.dtype), kind="ExternalInput").ap())
    out = nc.dram_tensor("out", (NODES, D), F32, kind="ExternalOutput").ap()
    gnn(nc, *args, out)
    r = run_bass_kernel_spmd(nc, [arrays], core_ids=[0])
    return r.results[0]["out"]
```

```python
from contextlib import ExitStack

import concourse.bass as bass
from concourse import mybir

F32, BF16 = mybir.dt.float32, mybir.dt.bfloat16
I32, U32, U16, I16 = mybir.dt.int32, mybir.dt.uint32, mybir.dt.uint16, mybir.dt.int16
ALU, ACT, AX = mybir.AluOpType, mybir.ActivationFunctionType, mybir.AxisListType
ds = bass.ds

P = 128
NODES, D, EDGES, HEADS, CH, TOPK, TYPES = 3125, 128, 100000, 4, 32, 8, 8
TILES = -(-NODES // P)
NP = TILES * P
FULL, REST = NODES // P, NODES % P
CHUNKS = 3
GE = CHUNKS * P
GROUPS = -(-EDGES // GE)
GT = -(-GROUPS // P)
LOADS = EDGES // GE // P + 2
WIN = 18
WINDOWS = -(-NODES // WIN)
KEYS = TILES * WIN
OFF = 20000.0
EPS = 1e-5
PARTS = 3
BATCH, DENSE, SPAN = 9, 4, 80
BATCHES = GROUPS // BATCH


class Steps:

    def __init__(self, eng, sem):
        self.eng, self.sem, self.base, self.n = eng, sem, 0, 0

    def __call__(self, ins, tick=None):
        ins.then_inc(self.sem, 1)
        self.n += 1
        self.eng.wait_ge(self.sem, self.base + self.n)
        if tick is not None:
            self.eng.sem_inc(tick, 1)

    def enter(self, i, per):
        self.start, self.per = self.base + self.n, per
        self.base, self.n = self.start + i * per, 0

    def leave(self, count):
        assert self.n == self.per, (self.n, self.per)
        self.base, self.n = self.start + count * self.per, 0


class Graph:
    def __init__(self, nc, ctx, src, dst, etype, weight):
        self.nc, self.names = nc, 0
        self.src, self.dst, self.etype, self.weight = src, dst, etype, weight
        sb = lambda name, shape, dt: ctx.enter_context(nc.sbuf_tensor(name, shape, dt))
        self.ident = sb("ident", [P, P], F32)
        self.identb = sb("identb", [P, P], BF16)
        self.base = sb("base", [P, GT], F32)
        self.next_base = sb("next_base", [P, GT], F32)
        self.wide = sb("wide", [1, 1], I32)

    def phase(self):
        ctx = ExitStack()
        self.sems = []
        ctx.callback(self.clear, self.sems)
        return ctx

    def clear(self, sems):
        for sem in sems:
            self.nc.gpsimd.sem_clear(sem)
        if sems:
            self.nc.all_engine_barrier()

    def sem(self, ctx, name):
        self.names += 1
        self.sems.append(ctx.enter_context(self.nc.semaphore(f"{name}_{self.names}")))
        return self.sems[-1]

    def sbuf(self, ctx, name, shape, dt):
        self.names += 1
        return ctx.enter_context(self.nc.sbuf_tensor(f"{name}_{self.names}", shape, dt))

    def psum(self, ctx, name, shape, dt):
        self.names += 1
        return ctx.enter_context(self.nc.psum_tensor(f"{name}_{self.names}", shape, dt))


def load_edges(eng, dram, tile, sem):
    whole, full = EDGES // GE, EDGES // GE // P
    for t in range(full):
        eng.dma_start(tile[:, t, :], dram[t * P * GE:(t + 1) * P * GE].rearrange("(g e) -> g e", e=GE)).then_inc(sem, 16)
    eng.dma_start(tile[0:whole - full * P, full, :],
                  dram[full * P * GE:whole * GE].rearrange("(g e) -> g e", e=GE)).then_inc(sem, 16)
    eng.dma_start(tile[whole - full * P:whole - full * P + 1, full, 0:EDGES - whole * GE],
                  dram[whole * GE:EDGES].rearrange("(g e) -> g e", g=1)).then_inc(sem, 16)


def constants(g):
    nc = g.nc
    with g.phase() as ctx:
        zeroed, made = g.sem(ctx, "zeroed"), g.sem(ctx, "made")
        block = ctx.enter_context(nc.Block())

        @block.gpsimd
        def _(pool):
            pool.memset(g.ident[:, :], 0.0).then_inc(zeroed, 1)
            pool.memset(g.identb[:, :], 0.0).then_inc(zeroed, 1)
            pool.wait_ge(zeroed, 2)
            for m in (g.ident, g.identb):
                pool.affine_select(out=m[:, :], in_=m[:, :], compare_op=ALU.not_equal, fill=1.0, base=0,
                                   pattern=[[-1, P]], channel_multiplier=1).then_inc(made, 1)
            pool.wait_ge(made, 2)


def window_bases(g):
    nc = g.nc
    with g.phase() as ctx:
        dst_i = g.sbuf(ctx, "dst_i", [P, GT, GE], I32)
        dst_f = g.sbuf(ctx, "dst_f", [P, GT, GE], F32)
        dst_m = g.sbuf(ctx, "dst_m", [P, GT, GE], F32)
        hi = g.sbuf(ctx, "hi", [P, GT], F32)
        over = g.sbuf(ctx, "over", [P, 1], F32)
        ones = g.sbuf(ctx, "ones", [P, 1], F32)
        total = g.psum(ctx, "total", [1, 1], F32)
        turned = g.psum(ctx, "turned", [1, GT * P], F32)
        base_row = g.sbuf(ctx, "base_row", [1, GT * P], F32)
        ahead = g.sbuf(ctx, "ahead", [1, BATCHES], F32)
        filled, loaded, counted = g.sem(ctx, "filled"), g.sem(ctx, "loaded"), g.sem(ctx, "counted")
        vec = g.sem(ctx, "vec")
        block = ctx.enter_context(nc.Block())

        @block.sync
        def _(sp):
            sp.wait_ge(filled, 1)
            load_edges(sp, g.dst, dst_i, loaded)

        @block.vector
        def _(dve):
            step = Steps(dve, vec)
            nc.vector.memset(dst_i[:, :, :], int(OFF)).then_inc(filled, 1)
            step(nc.vector.memset(ones[:, :], 1.0))
            step(nc.vector.memset(g.next_base[:, :], 0.0))
            dve.wait_ge(loaded, 16 * LOADS)
            step(nc.vector.tensor_copy(dst_f[:, :, :], dst_i[:, :, :]))
            step(nc.vector.tensor_reduce(g.base[:, :], dst_f[:, :, :], AX.X, ALU.min))
            step(nc.vector.tensor_scalar(g.base[:, :], g.base[:, :], float(NODES - WIN), None, ALU.min))
            step(nc.vector.scalar_tensor_tensor(dst_m[:, :, :], dst_f[:, :, :], OFF, dst_f[:, :, :],
                                                ALU.is_lt, ALU.mult))
            step(nc.vector.tensor_reduce(hi[:, :], dst_m[:, :, :], AX.X, ALU.max))
            step(nc.vector.tensor_tensor(hi[:, :], hi[:, :], g.base[:, :], ALU.subtract))
            step(nc.vector.tensor_reduce(over[:, :], hi[:, :], AX.X, ALU.max))
            step(nc.vector.tensor_scalar(over[:, :], over[:, :], float(WIN), None, ALU.is_ge))
            dve.wait_ge(counted, 1)
            step(nc.vector.tensor_copy(base_row[:, :], turned[:, :]))
            batches = base_row[:, 0:GROUPS].rearrange("a (i b) -> a i b", b=BATCH)
            step(nc.vector.tensor_tensor(ahead[:, :], batches[:, :, DENSE - 1], batches[:, :, 0], ALU.subtract))
            step(nc.vector.tensor_reduce(base_row[:, 0:1], ahead[:, :], AX.X, ALU.max))
            step(nc.vector.tensor_scalar(base_row[:, 0:1], base_row[:, 0:1], float(SPAN - WIN), None, ALU.is_gt))
            step(nc.vector.tensor_tensor(base_row[:, 0:1], base_row[:, 0:1], total[:, :], ALU.add))
            step(nc.vector.tensor_scalar(g.wide[:, :], base_row[:, 0:1], 1.0, None, ALU.min))
            assert step.n == 16

        @block.tensor
        def _(pe):
            pe.wait_ge(vec, 10)
            for t in range(GT):
                nc.tensor.transpose(turned[:, t * P:(t + 1) * P], g.base[:, t:t + 1], g.ident[:, :])
            nc.tensor.matmul(total[:, :], over[:, :], ones[:, :], start=True, stop=True).then_inc(counted, 1)


def edge_columns(g, ctx, kinds):
    g.keys_row = g.sbuf(ctx, "keys_row", [P, 512], I16)
    g.base_row = g.sbuf(ctx, "base_row", [1, GT * P], I32)
    sel = {kind: g.sbuf(ctx, kind, [P, GROUPS, CHUNKS], U32 if kind == "source" else F32) for kind in kinds}
    group_keys(g, sel)
    return sel


def group_keys(g, sel):
    nc = g.nc
    with g.phase() as ctx:
        raw, val = {}, {}
        for name in ("dst", "src", "etype", "weight"):
            if name == "etype" and "typed" not in sel or name == "weight" and "weight" not in sel:
                continue
            raw[name] = g.sbuf(ctx, name + "_raw", [P, GT, GE], F32 if name == "weight" else I32)
        place = g.sbuf(ctx, "place", [P, GT, GE], F32)
        bad = g.sbuf(ctx, "bad", [P, GT, GE], F32)
        for kind in sel:
            if kind not in ("place", "weight"):
                val[kind] = g.sbuf(ctx, kind + "_val", [P, GT, GE], F32)
        val["place"] = place
        if "weight" in sel:
            val["weight"] = raw["weight"]
        ps = [g.psum(ctx, "turned", [P, GE], F32) for _ in range(2)]
        filled, loaded, vec = g.sem(ctx, "filled"), g.sem(ctx, "loaded"), g.sem(ctx, "vec")
        turned, copied = g.sem(ctx, "turned"), g.sem(ctx, "copied")
        based = g.sem(ctx, "based")
        base_ps = g.psum(ctx, "base_ps", [1, GT * P], F32)
        jobs = [(kind, t) for kind in sel for t in range(GT)]
        dram = dict(dst=g.dst, src=g.src, etype=g.etype, weight=g.weight)
        counted = g.sem(ctx, "counted")
        block = ctx.enter_context(nc.Block())

        @block.gpsimd
        def _(pool):
            pool.iota(g.keys_row[:, :], [[1, 512]], base=0, channel_multiplier=0).then_inc(counted, 1)
            pool.wait_ge(counted, 1)

        @block.sync
        def _(sp):
            sp.wait_ge(filled, len(raw))
            for name in raw:
                load_edges(sp, dram[name], raw[name], loaded)

        @block.vector
        def _(dve):
            step = Steps(dve, vec)
            for name in raw:
                nc.vector.memset(raw[name][:, :, :], int(OFF) if name == "dst" else 0).then_inc(filled, 1)
            dve.wait_ge(based, 1)
            step(nc.vector.tensor_copy(g.base_row[:, :], base_ps[:, :]))
            dve.wait_ge(loaded, 16 * LOADS * len(raw))
            step(nc.vector.tensor_copy(place[:, :, :], raw["dst"][:, :, :]))
            for t in range(GT):
                step(nc.vector.tensor_scalar(place[:, t, :], place[:, t, :], g.base[:, t:t + 1], None,
                                             ALU.subtract))
            step(nc.vector.tensor_scalar(bad[:, :, :], place[:, :, :], float(WIN), OFF, ALU.is_ge, ALU.mult))
            step(nc.vector.tensor_tensor(bad[:, :, :], bad[:, :, :], place[:, :, :], ALU.add))
            step(nc.vector.tensor_scalar(place[:, :, :], place[:, :, :], 0.0, OFF, ALU.is_lt, ALU.mult))
            step(nc.vector.tensor_tensor(place[:, :, :], place[:, :, :], bad[:, :, :], ALU.add))
            if "source" in sel:
                step(nc.vector.tensor_copy(val["source"][:, :, :], raw["src"][:, :, :]))
            if "typed" in sel:
                step(nc.vector.tensor_copy(val["typed"][:, :, :], raw["etype"][:, :, :]))
                step(nc.vector.scalar_tensor_tensor(val["typed"][:, :, :], val["typed"][:, :, :], float(WIN),
                                                    place[:, :, :], ALU.mult, ALU.add))
            if "low" in sel:
                low, high = raw["dst"], raw["src"]
                step(nc.vector.tensor_scalar(low[:, :, :], raw["src"][:, :, :], P - 1, None, ALU.bitwise_and))
                step(nc.vector.tensor_scalar(high[:, :, :], raw["src"][:, :, :], 7, None,
                                             ALU.arith_shift_right))
                step(nc.vector.tensor_copy(val["low"][:, :, :], low[:, :, :]))
                step(nc.vector.tensor_copy(bad[:, :, :], high[:, :, :]))
                step(nc.vector.scalar_tensor_tensor(val["key"][:, :, :], bad[:, :, :], float(WIN),
                                                    place[:, :, :], ALU.mult, ALU.add))
            for n, (kind, t) in enumerate(jobs):
                dve.wait_ge(turned, n + 1)
                rows = min(GROUPS - P * t, P)
                nc.vector.tensor_copy(
                    sel[kind][:, P * t:P * t + rows, :],
                    ps[n % 2][:, :].rearrange("p (c g) -> p g c", g=P)[:, 0:rows, :]).then_inc(copied, 1)
            dve.wait_ge(copied, len(jobs))

        @block.tensor
        def _(pe):
            for t in range(GT):
                ins = nc.tensor.transpose(base_ps[:, t * P:(t + 1) * P], g.base[:, t:t + 1], g.ident[:, :])
            ins.then_inc(based, 1)
            n_vec = 6 + GT + ("source" in sel) + 2 * ("typed" in sel) + 5 * ("low" in sel)
            pe.wait_ge(vec, n_vec)
            for n, (kind, t) in enumerate(jobs):
                if n >= 2:
                    pe.wait_ge(copied, n - 1)
                for c in range(CHUNKS):
                    ins = nc.tensor.transpose(ps[n % 2][:, c * P:(c + 1) * P],
                                              val[kind][:, t, c * P:(c + 1) * P], g.ident[:, :])
                ins.then_inc(turned, 1)


def add_edges(g, adj, low, key):
    nc = g.nc
    UN = 3
    with g.phase() as ctx:
        hot_key = g.sbuf(ctx, "hot_key", [P, UN, CHUNKS, KEYS], BF16)
        hot_low = g.sbuf(ctx, "hot_low", [P, UN, CHUNKS, P], BF16)
        count = [g.psum(ctx, "count", [P, KEYS], F32) for _ in range(UN)]
        hots_made, counted, put = g.sem(ctx, "hots_made"), g.sem(ctx, "counted"), g.sem(ctx, "put")
        block = ctx.enter_context(nc.Block())

        @block.vector
        def _(dve):
            dve.sem_inc(counted, UN)
            with dve.Fori(0, GROUPS // UN) as i:
                for b in range(UN):
                    dve.wait_ge(counted, i * UN + b + 1)
                    for c in range(CHUNKS):
                        nc.vector.tensor_scalar(hot_key[:, b, c, :], g.keys_row[:, 0:KEYS],
                                                key[:, ds(i * UN + b, 1), c], None, ALU.is_equal)
                        ins = nc.vector.tensor_scalar(hot_low[:, b, c, :], g.keys_row[:, 0:P],
                                                      low[:, ds(i * UN + b, 1), c], None, ALU.is_equal)
                    ins.then_inc(hots_made, 1)

        @block.tensor
        def _(pe):
            pe.sem_inc(put, UN)
            with pe.Fori(0, GROUPS // UN) as i:
                for b in range(UN):
                    base = nc.tensor.value_load(g.base_row[0:1, ds(i * UN + b, 1)], min_val=0, max_val=NP - WIN)
                    pe.wait_ge(hots_made, i * UN + b + 1)
                    pe.wait_ge(put, i * UN + b + 1)
                    for c in range(CHUNKS):
                        nc.tensor.matmul(count[b][:, :], hot_low[:, b, c, :], hot_key[:, b, c, :],
                                         start=(c == 0), stop=False)
                    pe.wait_ge(put, i * UN + b + UN)
                    nc.tensor.matmul(count[b][:, :], g.identb[:, :], adj[:, :, ds(base, WIN)],
                                     start=False, stop=True).then_inc(counted, 1)

        @block.scalar
        def _(act):
            nc.scalar.preload_act_table(ACT.Copy)
            with act.Fori(0, GROUPS // UN) as i:
                for b in range(UN):
                    base = nc.scalar.value_load(g.base_row[0:1, ds(i * UN + b, 1)], min_val=0, max_val=NP - WIN)
                    act.wait_ge(counted, i * UN + b + UN + 1)
                    nc.scalar.copy(adj[:, :, ds(base, WIN)], count[b][:, :].rearrange("p (t w) -> p t w", w=WIN))\
                      .then_inc(put, 1)


def in_windows(g, work):
    nc = g.nc
    flag = nc.values_load(g.wide[0:1, 0:1], min_val=0, max_val=1)
    with nc.If(flag):
        with nc.Fori(0, WINDOWS):
            with g.phase() as ctx:
                moved = g.sem(ctx, "moved")
                block = ctx.enter_context(nc.Block())

                @block.vector
                def _(dve):
                    nc.vector.tensor_copy(g.base[:, :], g.next_base[:, :]).then_inc(moved, 1)
                    dve.wait_ge(moved, 1)
                    nc.vector.tensor_scalar(g.next_base[:, :], g.next_base[:, :], float(WIN), None,
                                            ALU.add).then_inc(moved, 1)
                    dve.wait_ge(moved, 2)
            work()
    with nc.Else():
        work()


def out_degrees(g, adj, deg):
    nc = g.nc
    SHARE = 12
    with g.phase() as ctx:
        unused = g.sbuf(ctx, "unused", [P, NP], BF16)
        by_act, by_dve, whole = g.sem(ctx, "by_act"), g.sem(ctx, "by_dve"), g.sem(ctx, "whole")
        block = ctx.enter_context(nc.Block())

        @block.scalar
        def _(act):
            for k in range(SHARE):
                if k >= 1:
                    act.wait_ge(by_act, k)
                nc.scalar.activation(unused[:, :], adj[:, k, :], ACT.Copy, accum_out=deg[:, k:k + 1])\
                  .then_inc(by_act, 1)

        @block.vector
        def _(dve):
            nc.vector.tensor_reduce(deg[:, SHARE:TILES], adj[:, SHARE:TILES, :], AX.X, ALU.add).then_inc(by_dve, 1)
            dve.wait_ge(by_act, SHARE)
            dve.wait_ge(by_dve, 1)
            nc.vector.tensor_scalar(deg[:, :], deg[:, :], 1.0, None, ALU.add).then_inc(whole, 1)
            dve.wait_ge(whole, 1)


def turn(g, adj):
    nc = g.nc
    SIDE, SLOTS, BANK = 5, 4, 1024
    SQUARES = TILES // SIDE
    W = SIDE * P
    distances = [(d, SQUARES - d, sum(SQUARES - e for e in range(1, d))) for d in range(1, SQUARES)]
    BETWEEN = SQUARES * (SQUARES - 1) // 2 * SIDE
    with g.phase() as ctx:
        upper = g.psum(ctx, "upper", [P, SLOTS * BANK], BF16)
        lower = g.psum(ctx, "lower", [P, SLOTS * BANK], BF16)
        turned, up_put, low_put = g.sem(ctx, "turned"), g.sem(ctx, "up_put"), g.sem(ctx, "low_put")
        block = ctx.enter_context(nc.Block())

        def slot(n, width):
            return ds((n % SLOTS) * BANK, width)

        @block.tensor
        def _(pe):
            for d, count, before in distances:
                with pe.Fori(0, count) as a:
                    for i in range(SIDE):
                        n = (a + before) * SIDE + i
                        pe.wait_ge(up_put, n + 1)
                        pe.wait_ge(low_put, n + 1)
                        for j in range(SIDE):
                            nc.tensor.transpose(upper[:, ds((n % SLOTS) * BANK + j * P, P)],
                                                adj[:, ds(a * SIDE + i, 1), ds(a * W + d * W + j * P, P)],
                                                g.identb[:, :])
                            ins = nc.tensor.transpose(lower[:, ds((n % SLOTS) * BANK + j * P, P)],
                                                      adj[:, ds(a * SIDE + d * SIDE + j, 1), ds(a * W + i * P, P)],
                                                      g.identb[:, :])
                        ins.then_inc(turned, 1)
            with pe.Fori(0, SQUARES) as q:
                for r in range(SIDE - 1):
                    n = q * SIDE + BETWEEN + r
                    pe.wait_ge(up_put, n + 1)
                    pe.wait_ge(low_put, n + 1)
                    for j in range(r + 1, SIDE):
                        nc.tensor.transpose(upper[:, ds((n % SLOTS) * BANK + (j - r - 1) * P, P)],
                                            adj[:, ds(q * SIDE + r, 1), ds(q * W + j * P, P)], g.identb[:, :])
                        ins = nc.tensor.transpose(lower[:, ds((n % SLOTS) * BANK + (j - r - 1) * P, P)],
                                                  adj[:, ds(q * SIDE + j, 1), ds(q * W + r * P, P)],
                                                  g.identb[:, :])
                    ins.then_inc(turned, 1)
                n = q * SIDE + BETWEEN + SIDE - 1
                pe.wait_ge(low_put, n + 1)
                for j in range(SIDE):
                    ins = nc.tensor.transpose(lower[:, ds((n % SLOTS) * BANK + j * P, P)],
                                              adj[:, ds(q * SIDE + j, 1), ds(q * W + j * P, P)], g.identb[:, :])
                ins.then_inc(turned, 1)

        @block.scalar
        def _(act):
            act.sem_inc(up_put, SLOTS)
            nc.scalar.preload_act_table(ACT.Copy)
            for d, count, before in distances:
                with act.Fori(0, count) as a:
                    for i in range(SIDE):
                        n = (a + before) * SIDE + i
                        act.wait_ge(turned, n + 1)
                        nc.scalar.copy(adj[:, ds(a * SIDE + d * SIDE, SIDE), ds(a * W + i * P, P)],
                                       upper[:, slot(n, W)].rearrange("p (j c) -> p j c", c=P)).then_inc(up_put, 1)
            with act.Fori(0, SQUARES) as q:
                for r in range(SIDE - 1):
                    n = q * SIDE + BETWEEN + r
                    act.wait_ge(turned, n + 1)
                    nc.scalar.copy(adj[:, ds(q * SIDE + r + 1, SIDE - 1 - r), ds(q * W + r * P, P)],
                                   upper[:, slot(n, W - (r + 1) * P)].rearrange("p (j c) -> p j c", c=P))\
                      .then_inc(up_put, 1)
                act.wait_ge(up_put, q * SIDE + BETWEEN + SIDE - 1 + SLOTS)
                act.sem_inc(up_put, 1)

        @block.vector
        def _(dve):
            dve.sem_inc(low_put, SLOTS)
            for d, count, before in distances:
                with dve.Fori(0, count) as a:
                    for i in range(SIDE):
                        n = (a + before) * SIDE + i
                        dve.wait_ge(turned, n + 1)
                        nc.vector.tensor_copy(adj[:, ds(a * SIDE + i, 1), ds(a * W + d * W, W)],
                                              lower[:, slot(n, W)]).then_inc(low_put, 1)
            with dve.Fori(0, SQUARES) as q:
                for r in range(SIDE - 1):
                    n = q * SIDE + BETWEEN + r
                    dve.wait_ge(turned, n + 1)
                    nc.vector.tensor_copy(adj[:, ds(q * SIDE + r, 1), ds(q * W + (r + 1) * P, W - (r + 1) * P)],
                                          lower[:, slot(n, W - (r + 1) * P)]).then_inc(low_put, 1)
                n = q * SIDE + BETWEEN + SIDE - 1
                dve.wait_ge(turned, n + 1)
                for j in range(SIDE):
                    ins = nc.vector.tensor_tensor(adj[:, ds(q * SIDE + j, 1), ds(q * W + j * P, P)],
                                                  lower[:, ds((n % SLOTS) * BANK + j * P, P)], g.identb[:, :],
                                                  ALU.add)
                ins.then_inc(low_put, 1)
            dve.wait_ge(low_put, BETWEEN + SQUARES * SIDE + SLOTS)


def split(step, nc, parts, value, rest):
    step(nc.vector.tensor_copy(parts(0), value))
    step(nc.vector.tensor_tensor(rest, value, parts(0), ALU.subtract))
    step(nc.vector.tensor_copy(parts(1), rest))
    return nc.vector.tensor_tensor(parts(2), rest, parts(1), ALU.subtract)


class Norm:

    def __init__(self, g, ctx):
        self.nc = g.nc
        self.stats = g.sbuf(ctx, "stats", [P, 6], F32)
        self.mv = g.sbuf(ctx, "mean_var", [P, 2], F32)
        self.eps = g.sbuf(ctx, "eps", [P, 1], F32)
        self.dev = g.sbuf(ctx, "deviation", [P, 1], F32)
        self.inv = g.sbuf(ctx, "inverse", [P, 1], F32)
        self.var_ready, self.dev_ready = g.sem(ctx, "var_ready"), g.sem(ctx, "dev_ready")
        self.tick = g.sem(ctx, "tick")

    def start(self, step):
        step(self.nc.vector.memset(self.eps[:, :], EPS))

    def vector(self, dve, step, out, value, n):
        nc = self.nc
        step(nc.vector.bn_stats(self.stats[:, :], value), self.tick)
        nc.vector.bn_aggr(self.mv[:, :], self.stats[:, :]).then_inc(self.var_ready, 1)
        dve.wait_ge(self.dev_ready, n)
        step(nc.vector.reciprocal(self.inv[:, :], self.dev[:, :]))
        return nc.vector.tensor_scalar(out, value, self.mv[:, 0:1], self.inv[:, :], ALU.subtract, ALU.mult)

    def scalar(self, act, n):
        act.wait_ge(self.var_ready, n)
        self.nc.scalar.activation(self.dev[:, :], self.mv[:, 1:2], ACT.Sqrt,
                                  bias=self.eps[:, :]).then_inc(self.dev_ready, 1)


class AllNorm:

    def __init__(self, g, ctx):
        self.nc = g.nc
        self.stats = g.sbuf(ctx, "stats", [P, TILES, 6], F32)
        self.mv = g.sbuf(ctx, "mean_var", [P, TILES, 2], F32)
        self.eps = g.sbuf(ctx, "eps", [P, 1], F32)
        self.dev = g.sbuf(ctx, "deviation", [P, TILES], F32)
        self.inv = g.sbuf(ctx, "inverse", [P, TILES], F32)
        self.measured, self.var_ready, self.dev_ready = (
            g.sem(ctx, n) for n in ("measured", "var_ready", "dev_ready"))

    def start(self, step):
        step(self.nc.vector.memset(self.eps[:, :], EPS))

    def take(self, t, value):
        self.nc.vector.bn_stats(self.stats[:, t, :], value).then_inc(self.measured, 1)

    def finish(self, dve, step, rows, done):
        nc = self.nc
        dve.wait_ge(self.measured, TILES)
        for t in range(TILES):
            nc.vector.bn_aggr(self.mv[:, t, :], self.stats[:, t, :]).then_inc(self.var_ready, 1)
        dve.wait_ge(self.dev_ready, 1)
        step(nc.vector.reciprocal(self.inv[:, :], self.dev[:, :]))
        for t in range(TILES):
            nc.vector.tensor_scalar(rows[:, t, :], rows[:, t, :], self.mv[:, t, 0:1], self.inv[:, t:t + 1],
                                    ALU.subtract, ALU.mult).then_inc(done, 1)

    def scalar(self, act):
        act.wait_ge(self.var_ready, TILES)
        self.nc.scalar.activation(self.dev[:, :], self.mv[:, :, 1], ACT.Sqrt, bias=self.eps[:, :])\
            .then_inc(self.dev_ready, 1)


PIECE = 5


def load_pieces(eng, dram, rows, sems):
    for t in range(0, TILES, PIECE):
        eng.dma_start(rows[:, t:t + PIECE, :],
                      dram[t * P:(t + PIECE) * P, :].rearrange("(t p) d -> p t d", p=P)).then_inc(sems[t // PIECE], 16)


def store_pieces(eng, dram, rows, ready, sem):
    nodes, count = dram.shape[0], 0
    for t in range(0, TILES, PIECE):
        eng.wait_ge(ready, t + PIECE)
        full = min(PIECE, nodes // P - t)
        eng.dma_start(dram[t * P:(t + full) * P, :].rearrange("(t p) d -> p t d", p=P),
                      rows[:, t:t + full, :]).then_inc(sem, 16)
        count += 1
        if full < PIECE:
            eng.dma_start(dram[(t + full) * P:nodes, :], rows[0:nodes - (t + full) * P, t + full, :]).then_inc(sem, 16)
            count += 1
    eng.wait_ge(sem, 16 * count)


def load_rows(eng, dram, tile, sem):
    eng.dma_start(tile[:, 0:FULL, :], dram[0:FULL * P, :].rearrange("(t p) d -> p t d", p=P)).then_inc(sem, 16)
    eng.dma_start(tile[0:REST, FULL, :], dram[FULL * P:NODES, :]).then_inc(sem, 16)


def propagate(g, adj, deg, in_deg, x, x1):
    nc = g.nc
    UN, HOPS = 5, 3
    PW = PARTS * D
    with g.phase() as ctx:
        h = [g.sbuf(ctx, "hop_parts", [P, TILES, PW], BF16) for _ in range(2)]
        xin = h[1][:, :, :].rearrange("p t d -> p (t d)").bitcast(F32)[:, 0:TILES * D].rearrange(
            "p (t d) -> p t d", d=D)
        s1 = g.sbuf(ctx, "scale", [P, TILES], F32)
        s2 = g.sbuf(ctx, "scale_sq", [P, TILES], F32)
        val = g.sbuf(ctx, "val", [P, D], F32)
        rest = g.sbuf(ctx, "rest", [P, D], F32)
        unused = g.sbuf(ctx, "unused", [P, NP], BF16)
        norm = AllNorm(g, ctx)
        acc = [g.psum(ctx, "acc", [P, PW], F32) for _ in range(UN)]
        cleared, loaded, vec, root = g.sem(ctx, "cleared"), g.sem(ctx, "loaded"), g.sem(ctx, "vec"), g.sem(ctx, "root")
        parts_ready, summed, drained = g.sem(ctx, "parts_ready"), g.sem(ctx, "summed"), g.sem(ctx, "drained")
        degree, again, res_ready, stored = (g.sem(ctx, n) for n in ("degree", "again", "res_ready", "stored"))
        block = ctx.enter_context(nc.Block())

        @block.sync
        def _(sp):
            sp.wait_ge(cleared, 1)
            load_rows(sp, x, xin, loaded)
            sp.wait_ge(cleared, 2)
            load_rows(sp, x, xin, again)
            store_pieces(sp, x1, xin, res_ready, stored)

        @block.tensor
        def _(pe):
            for hop in range(HOPS):
                pe.wait_ge(parts_ready, hop * TILES + 1)
                with pe.Fori(0, TILES // UN) as i:
                    for b in range(UN):
                        pe.wait_ge(drained, i * UN + b + hop * TILES + 1)
                        for k in range(TILES):
                            ins = nc.tensor.matmul(acc[b][:, :], adj[:, k, ds((i * UN + b) * P, P)],
                                                   h[hop % 2][:, k, :], start=(k == 0), stop=(k == TILES - 1))
                        ins.then_inc(summed, 1)

        @block.scalar
        def _(act):
            nc.scalar.activation(s1[:, :], deg[:, :], ACT.Sqrt).then_inc(root, 1)
            for k in range(TILES):
                if k >= 1:
                    act.wait_ge(degree, k)
                nc.scalar.activation(unused[:, :], adj[:, k, :], ACT.Copy, accum_out=in_deg[:, k:k + 1])\
                  .then_inc(degree, 1)
            norm.scalar(act)

        @block.vector
        def _(dve):
            step = Steps(dve, vec)
            dve.sem_inc(drained, UN)
            nc.vector.memset(h[1][:, :, :].rearrange("p t d -> p (t d)").bitcast(U32)[:, FULL * D:TILES * D], 0)\
              .then_inc(cleared, 1)
            norm.start(step)
            dve.wait_ge(root, 1)
            step(nc.vector.reciprocal(s1[:, :], s1[:, :]))
            step(nc.vector.tensor_tensor(s2[:, :], s1[:, :], s1[:, :], ALU.mult))
            dve.wait_ge(loaded, 32)
            part = lambda j: h[0][:, :, j * D:(j + 1) * D]
            step(nc.vector.tensor_tensor(xin, xin, s1[:, :].unsqueeze(2).broadcast_to([P, TILES, D]), ALU.mult))
            split(step, nc, part, xin, xin).then_inc(parts_ready, 1)
            dve.wait_ge(parts_ready, 1)

            def total(hop, i, b):
                n = i * UN + b + hop * TILES
                dve.wait_ge(summed, n + 1)
                ins = nc.vector.tensor_reduce(val[:, :], acc[b][:, :].rearrange("p (j d) -> p d j", j=PARTS),
                                              AX.X, ALU.add)
                ins.then_inc(drained, 1)
                dve.wait_ge(drained, n + UN + 1)

            for hop in range(HOPS - 1):
                with dve.Fori(0, TILES // UN) as i:
                    step.enter(i, 4 * UN)
                    for b in range(UN):
                        t = i * UN + b
                        total(hop, i, b)
                        step(nc.vector.tensor_scalar(val[:, :], val[:, :], s2[:, ds(t, 1)], None, ALU.mult))
                        split(step, nc, lambda j: h[1 - hop % 2][:, ds(t, 1), j * D:(j + 1) * D], val[:, :],
                              rest[:, :]).then_inc(parts_ready, 1)
                        dve.wait_ge(parts_ready, t + hop * TILES + 2)
                    step.leave(TILES // UN)
            nc.vector.memset(h[1][:, :, :].rearrange("p t d -> p (t d)").bitcast(U32)[:, FULL * D:TILES * D], 0)\
              .then_inc(cleared, 1)
            for t in range(TILES):
                total(HOPS - 1, t // UN, t % UN)
                if t == 0:
                    dve.wait_ge(again, 32)
                step(nc.vector.scalar_tensor_tensor(xin[:, t, :], val[:, :], s1[:, t:t + 1], xin[:, t, :],
                                                    ALU.mult, ALU.add))
                norm.take(t, xin[:, t, :])
            norm.finish(dve, step, xin, res_ready)


ROW = CH + 1


class Attention:

    def __init__(self, g, ctx):
        dram = lambda name, shape: g.nc.dram_tensor(name, shape, F32, kind="Internal").ap()
        self.table = [dram(f"head_rows_{h}", [NP, ROW]) for h in range(HEADS)]
        self.ranked = [dram(f"ranked_rows_{h}", [NP, ROW]) for h in range(HEADS)]
        self.scores = dram("neighbour_scores", [HEADS, NP])
        self.own = g.sbuf(ctx, "own_scores", [P, TILES, HEADS], F32)
        self.theirs = g.sbuf(ctx, "their_scores", [P, TILES, HEADS], F32)


def project(g, att, x1, w, a):
    nc = g.nc
    S, ALL = 2 * HEADS, HEADS * ROW
    with g.phase() as ctx:
        wt = g.sbuf(ctx, "w", [P, D], F32)
        w_turned = g.sbuf(ctx, "w_turned", [P, D], F32)
        a_diag = g.sbuf(ctx, "a_diag", [P, S], F32)
        w_ext = g.sbuf(ctx, "w_ext", [P, ALL + HEADS], F32)
        xt = g.sbuf(ctx, "x_tiles", [P, TILES, D], F32)
        x_turned = g.sbuf(ctx, "x_turned", [P, 2, D], F32)
        rows = g.sbuf(ctx, "rows", [P, TILES, ALL], F32)
        s_row = g.sbuf(ctx, "s_row", [HEADS, NP], F32)
        ps_x = [g.psum(ctx, "ps_x", [P, D], F32) for _ in range(2)]
        ps_h = [g.psum(ctx, "ps_h", [P, ALL + HEADS], F32) for _ in range(2)]
        ps_s = [g.psum(ctx, "ps_s", [HEADS, P], F32) for _ in range(2)]
        cleared, w_loaded, a_loaded, w_ps, w_sb = (
            g.sem(ctx, n) for n in ("cleared", "w_loaded", "a_loaded", "w_ps", "w_sb"))
        loaded = [g.sem(ctx, "loaded") for _ in range(TILES // PIECE)]
        x_ps, x_sb, h_ps, h_sb, own_sb, s_ps, s_sb, stored, kept = (
            g.sem(ctx, n) for n in ("x_ps", "x_sb", "h_ps", "h_sb", "own_sb", "s_ps", "s_sb", "stored", "kept"))
        block = ctx.enter_context(nc.Block())
        by_head = lambda t: t.rearrange("p (h c) -> p h c", c=ROW)

        @block.sync
        def _(sp):
            sp.dma_start(wt[:, :], w).then_inc(w_loaded, 16)
            load_pieces(sp, x1, xt, loaded)
            sp.wait_ge(h_sb, TILES)
            for h in range(HEADS):
                sp.dma_start(att.table[h].rearrange("(t p) c -> p t c", p=P),
                             rows[:, :, h * ROW:(h + 1) * ROW]).then_inc(stored, 16)
            sp.wait_ge(s_sb, TILES)
            sp.dma_start(att.scores, s_row[:, :]).then_inc(stored, 16)
            sp.wait_ge(stored, 16 * (1 + HEADS))

        @block.gpsimd
        def _(pool):
            pool.memset(a_diag[:, :], 0.0).then_inc(cleared, 1)

        @block.tensor
        def _(pe):
            def turn_scores(t):
                pe.wait_ge(h_sb, t + 1)
                if t >= 2:
                    pe.wait_ge(s_sb, t - 1)
                nc.tensor.transpose(ps_s[t % 2][:, :], by_head(rows[:, t, :])[:, :, CH], g.ident[:, :])\
                  .then_inc(s_ps, 1)

            pe.wait_ge(w_loaded, 16)
            nc.tensor.transpose(ps_x[0][:, :], wt[:, :], g.ident[:, :]).then_inc(w_ps, 1)
            pe.wait_ge(w_sb, 1)
            pe.wait_ge(a_loaded, 16 * S)
            nc.tensor.matmul(ps_h[0][:, 0:S], w_turned[:, :], a_diag[:, :], start=True, stop=True).then_inc(w_ps, 1)
            pe.wait_ge(w_sb, 4)
            for t in range(TILES + 1):
                if t < TILES:
                    pe.wait_ge(loaded[t // PIECE], 16)
                    if t >= 2:
                        pe.wait_ge(x_sb, t - 1)
                    nc.tensor.transpose(ps_x[t % 2][:, :], xt[:, t, :], g.ident[:, :]).then_inc(x_ps, 1)
                if t >= 1:
                    pe.wait_ge(x_sb, t)
                    if t >= 3:
                        pe.wait_ge(h_sb, t - 2)
                        pe.wait_ge(own_sb, t - 2)
                    nc.tensor.matmul(ps_h[(t - 1) % 2][:, :], x_turned[:, (t - 1) % 2, :], w_ext[:, :],
                                     start=True, stop=True).then_inc(h_ps, 1)
                if t >= 2:
                    turn_scores(t - 2)
            turn_scores(TILES - 1)

        @block.scalar
        def _(act):
            act.wait_ge(cleared, 1)
            for h in range(HEADS):
                for half in range(2):
                    act.dma_start(a_diag[h * CH:(h + 1) * CH, half * HEADS + h:half * HEADS + h + 1],
                                  a[h:h + 1, half * CH:(half + 1) * CH].rearrange("a c -> c a"),
                                  allow_slow_non_contiguous=True).then_inc(a_loaded, 16)
            for t in range(TILES):
                act.wait_ge(h_ps, t + 1)
                nc.scalar.copy(rows[:, t, :], ps_h[t % 2][:, 0:ALL]).then_inc(h_sb, 1)
                nc.scalar.copy(att.own[:, t, :], ps_h[t % 2][:, ALL:ALL + HEADS]).then_inc(own_sb, 1)

        @block.vector
        def _(dve):
            dve.wait_ge(w_ps, 1)
            nc.vector.tensor_copy(w_turned[:, :], ps_x[0][:, :]).then_inc(w_sb, 1)
            nc.vector.tensor_copy(by_head(w_ext[:, 0:ALL])[:, :, 0:CH],
                                  wt[:, :].rearrange("p (h c) -> p h c", c=CH)).then_inc(w_sb, 1)
            dve.wait_ge(w_ps, 2)
            nc.vector.tensor_copy(w_ext[:, ALL:ALL + HEADS], ps_h[0][:, 0:HEADS]).then_inc(w_sb, 1)
            nc.vector.tensor_copy(by_head(w_ext[:, 0:ALL])[:, :, CH], ps_h[0][:, HEADS:S]).then_inc(w_sb, 1)
            for t in range(TILES + 2):
                if t < TILES:
                    dve.wait_ge(x_ps, t + 1)
                    if t >= 2:
                        dve.wait_ge(h_ps, t - 1)
                    nc.vector.tensor_copy(x_turned[:, t % 2, :], ps_x[t % 2][:, :]).then_inc(x_sb, 1)
                if t >= 2:
                    dve.wait_ge(s_ps, t - 1)
                    nc.vector.tensor_copy(s_row[:, (t - 2) * P:(t - 1) * P], ps_s[t % 2][:, :]).then_inc(s_sb, 1)
            dve.wait_ge(h_sb, TILES)
            nc.vector.tensor_copy(att.theirs[:, :, :],
                                  rows[:, :, :].rearrange("p t (h c) -> p t h c", c=ROW)[:, :, :, CH]).then_inc(kept, 1)
            dve.wait_ge(kept, 1)


def rank(g, att, code):
    nc = g.nc
    SIDE = 5
    HALF = [(0, 13), (13, TILES)]
    with g.phase() as ctx:
        score = g.sbuf(ctx, "score", [P, NP], F32)
        below = g.sbuf(ctx, "below", [P, 2, 13 * P], BF16)
        later = g.sbuf(ctx, "later", [P, P], BF16)
        ones = g.sbuf(ctx, "ones", [P, P], BF16)
        banks = [g.psum(ctx, "rank", [P, 512], F32) for _ in range(7)]
        rows = g.sbuf(ctx, "rows", [P, TILES, ROW], F32)
        diagonal = g.sbuf(ctx, "diagonal", [P, SIDE, P], U16)
        own_code = g.sbuf(ctx, "own_code", [P, TILES], F32)
        own_rank = g.sbuf(ctx, "own_rank", [P, TILES], U32)
        masked, added, ranked = g.sem(ctx, "masked"), g.sem(ctx, "added"), g.sem(ctx, "ranked")
        rows_loaded, scattered = g.sem(ctx, "rows_loaded"), g.sem(ctx, "scattered")
        made, loaded = g.sem(ctx, "made"), g.sem(ctx, "loaded")
        compared, summed, coded, diag = g.sem(ctx, "compared"), g.sem(ctx, "summed"), g.sem(ctx, "coded"), g.sem(ctx, "diag")
        read = g.sem(ctx, "read")
        block = ctx.enter_context(nc.Block())

        @block.gpsimd
        def _(pool):
            pool.memset(later[:, :], 1.0).then_inc(made, 1)
            pool.memset(ones[:, :], 1.0).then_inc(made, 1)
            pool.wait_ge(made, 2)
            pool.affine_select(out=later[:, :], in_=later[:, :], compare_op=ALU.is_gt, fill=0.0, base=0,
                               pattern=[[-1, P]], channel_multiplier=1).then_inc(made, 1)
            for h in range(HEADS):
                pool.wait_ge(coded, 2 * (h + 1))
                for n in range(TILES // SIDE):
                    if h + n >= 1:
                        pool.wait_ge(added, h * TILES + n * SIDE)
                    pool.affine_select(
                        out=diagonal[:, :, :].bitcast(I16),
                        in_=code[:, h, n * SIDE * P:(n + 1) * SIDE * P].rearrange("p (t c) -> p t c", c=P).bitcast(I16),
                        compare_op=ALU.is_equal, fill=0.0, base=0, pattern=[[0, SIDE], [-1, P]],
                        channel_multiplier=1).then_inc(masked, 1)
                pool.wait_ge(ranked, h + 1)
                pool.wait_ge(rows_loaded, 16 * (h + 1))
                for t in range(TILES):
                    pool.indirect_dma_start(att.ranked[h], bass.IndirectOffsetOnAxis(ap=own_rank[:, t:t + 1], axis=0),
                                            rows[:, t, :], None).then_inc(scattered, 16)
            pool.wait_ge(scattered, 16 * TILES * HEADS)

        @block.sync
        def _(sp):
            for h in range(HEADS):
                if h >= 1:
                    sp.wait_ge(read, h)
                sp.dma_start(score[:, :], att.scores[h:h + 1, :].broadcast_to([P, NP])).then_inc(loaded, 16)
                if h >= 1:
                    sp.wait_ge(scattered, 16 * TILES * h)
                sp.dma_start(rows[:, :, :], att.table[h].rearrange("(t p) c -> p t c", p=P)).then_inc(rows_loaded, 16)

        def spans(lo, hi):
            first = 0 if lo == 0 else 4
            a = lo * P
            while a < hi * P:
                b = min(a + 512, hi * P)
                yield first + (a - lo * P) // 512, a, b
                a = b

        @block.vector
        def _(dve):
            dve.wait_ge(made, 3)
            n = nd = 0
            for h in range(HEADS):
                dve.wait_ge(loaded, 16 * (h + 1))
                for lo, hi in HALF:
                    for t in range(TILES):
                        if n >= 2:
                            dve.wait_ge(summed, n - 1)
                        buf, s = below[:, n % 2, :], att.theirs[:, t, h:h + 1]
                        left, right = min(max(t, lo), hi), min(max(t + 1, lo), hi)
                        if left > lo:
                            ins = nc.vector.tensor_scalar(buf[:, 0:(left - lo) * P], score[:, lo * P:left * P],
                                                          s, None, ALU.is_ge)
                        if hi > right:
                            ins = nc.vector.tensor_scalar(buf[:, (right - lo) * P:(hi - lo) * P],
                                                          score[:, right * P:hi * P], s, None, ALU.is_gt)
                        if left < right:
                            out, own = buf[:, (t - lo) * P:(t + 1 - lo) * P], score[:, t * P:(t + 1) * P]
                            nc.vector.scalar_tensor_tensor(out, own, s, later[:, :], ALU.is_ge, ALU.mult)\
                              .then_inc(diag, 1)
                            nd += 1
                            dve.wait_ge(diag, nd)
                            ins = nc.vector.scalar_tensor_tensor(out, own, s, out, ALU.is_gt, ALU.max)
                        ins.then_inc(compared, 1)
                        n += 1
                dve.wait_ge(compared, n)
                dve.sem_inc(read, 1)

        @block.tensor
        def _(pe):
            pe.wait_ge(made, 3)
            n = 0
            for h in range(HEADS):
                for k, (lo, hi) in enumerate(HALF):
                    if h >= 1:
                        pe.wait_ge(coded, 2 * (h - 1) + k + 1)
                    for t in range(TILES):
                        pe.wait_ge(compared, n + 1)
                        for bank, a, b in spans(lo, hi):
                            ins = nc.tensor.matmul(banks[bank][:, 0:b - a], ones[:, :],
                                                   below[:, n % 2, a - lo * P:b - lo * P],
                                                   start=(t == 0), stop=(t == TILES - 1))
                        ins.then_inc(summed, 1)
                        n += 1

        @block.scalar
        def _(act):
            for h in range(HEADS):
                for k, (lo, hi) in enumerate(HALF):
                    act.wait_ge(summed, (2 * h + k + 1) * TILES)
                    for bank, a, b in spans(lo, hi):
                        ins = nc.scalar.activation(code[:, h, a:b], banks[bank][:, 0:b - a], ACT.Copy,
                                                   bias=15.0, scale=16.0)
                    ins.then_inc(coded, 1)
                for t in range(TILES):
                    if t % SIDE == 0:
                        act.wait_ge(masked, (h * TILES + t) // SIDE + 1)
                    nc.scalar.activation(diagonal[:, t % SIDE, :], diagonal[:, t % SIDE, :], ACT.Copy,
                                         accum_out=own_code[:, t:t + 1]).then_inc(added, 1)
                act.wait_ge(added, (h + 1) * TILES)
                if h >= 1:
                    act.wait_ge(scattered, 16 * TILES * h)
                nc.scalar.activation(own_rank[:, :], own_code[:, :], ACT.Copy, bias=-15.0 / 16, scale=1.0 / 16)\
                  .then_inc(ranked, 1)
            act.wait_ge(ranked, HEADS)


def attend(g, att, adj, code, x1, x2):
    nc = g.nc
    HK = HEADS * TOPK
    BANK = 1024
    with g.phase() as ctx:
        mask = g.sbuf(ctx, "mask", [P, NP], I16)
        key = g.sbuf(ctx, "key", [P, NP], U16)
        best = g.sbuf(ctx, "best", [P, 2, HK], U32)
        where = g.sbuf(ctx, "where", [P, 2, HK], U32)
        rows = g.sbuf(ctx, "rows", [P, 2, HK, ROW], F32)
        xt = g.sbuf(ctx, "x_tile", [P, D], F32)
        res = g.sbuf(ctx, "res", [P, D], F32)
        low = g.sbuf(ctx, "low", [P, HK], U32)
        cnt, cum, kept = (g.sbuf(ctx, n, [P, HK], F32) for n in ("cnt", "cum", "kept"))
        again = g.sbuf(ctx, "again", [P, HK], F32)
        e, ez = g.sbuf(ctx, "e", [P, HK], F32), g.sbuf(ctx, "ez", [P, HK], F32)
        den = g.sbuf(ctx, "den", [P, HEADS], F32)
        o, neg = g.sbuf(ctx, "o", [P, D], F32), g.sbuf(ctx, "neg", [P, D], F32)
        norm = Norm(g, ctx)
        edges = [g.psum(ctx, "edges", [P, 4 * BANK], BF16) for _ in range(2)]
        vec, turned, masked, keyed = (g.sem(ctx, n) for n in ("vec", "turned", "masked", "keyed"))
        found, pool_tick = g.sem(ctx, "found"), g.sem(ctx, "pool_tick")
        gathered = [g.sem(ctx, "gathered") for _ in range(2)]
        used = g.sem(ctx, "used")
        e_ready, ez_ready, neg_ready, elu_ready = (g.sem(ctx, n) for n in ("e_ready", "ez_ready", "neg_ready", "elu_ready"))
        x_ready, x_used, res_ready, stored = (g.sem(ctx, n) for n in ("x_ready", "x_used", "res_ready", "stored"))
        block = ctx.enter_context(nc.Block())

        def over_tiles(eng, body, step=None, per=0):
            with eng.Fori(0, TILES // 2) as i:
                if step:
                    step.enter(i, 2 * per)
                for b in range(2):
                    body(i * 2 + b, b)
                if step:
                    step.leave(TILES // 2)
            body(TILES - 1, 0)

        @block.tensor
        def _(pe):
            def tile(q, b):
                pe.wait_ge(masked, q + 1)
                for k in range(TILES):
                    ins = nc.tensor.transpose(edges[b][:, k * P:(k + 1) * P],
                                              adj[:, k, ds(q * P, P)], g.identb[:, :])
                ins.then_inc(turned, 1)
            over_tiles(pe, tile)

        @block.gpsimd
        def _(pool):
            def tile(q, b):
                pool.wait_ge(used, q + 1)
                for h in range(HEADS):
                    pool.wait_ge(found, q * HEADS + h + 1)
                    pool.sem_inc(pool_tick, 1)
                    for k in range(TOPK):
                        j = h * TOPK + k
                        pool.indirect_dma_start(rows[:, b, j, :], None, att.ranked[h],
                                                bass.IndirectOffsetOnAxis(ap=where[:, b, j:j + 1], axis=0))\
                            .then_inc(gathered[b], 16)
            over_tiles(pool, tile)

        @block.sync
        def _(sp):
            with sp.Fori(0, TILES) as t:
                sp.wait_ge(x_used, t + 1)
                sp.dma_start(xt[:, :], x1[ds(t * P, P), :]).then_inc(x_ready, 16)
                sp.wait_ge(res_ready, t + 1)
                sp.dma_start(x2[ds(t * P, P), :], res[:, :]).then_inc(stored, 16)
            sp.wait_ge(stored, 16 * TILES + 16)

        @block.scalar
        def _(act):
            with act.Fori(0, TILES) as t:
                act.wait_ge(e_ready, t + 1)
                nc.scalar.activation(ez[:, :], e[:, :], ACT.Exp).then_inc(ez_ready, 1)
                act.wait_ge(neg_ready, t + 1)
                nc.scalar.activation(neg[:, :], neg[:, :], ACT.Exp).then_inc(elu_ready, 1)
                norm.scalar(act, t + 1)

        @block.vector
        def _(dve):
            step = Steps(dve, vec)
            dve.sem_inc(masked, 2)
            dve.sem_inc(used, 2)
            dve.sem_inc(x_used, 1)
            dve.sem_inc(stored, 16)
            norm.start(step)
            step(nc.vector.memset(again[:, :], 1.0))
            step(nc.vector.memset(again[:, :].rearrange("p (h k) -> p h k", k=TOPK)[:, :, 0:1], 0.0))
            heads = lambda t: t.rearrange("p (h k) -> p h k", k=TOPK)

            def search(q, b):
                dve.wait_ge(turned, q + 1)
                nc.vector.tensor_scalar(mask[:, :], edges[b][:, 0:NP], float(TOPK), -1.0, ALU.min, ALU.mult)\
                  .then_inc(masked, 1)
                dve.wait_ge(masked, q + 3)
                for h in range(HEADS):
                    step(nc.vector.tensor_tensor(key[:, :], code[:, h, :], mask[:, :].bitcast(U16),
                                                 ALU.bitwise_and), norm.tick)
                    at = slice(h * TOPK, (h + 1) * TOPK)
                    step(nc.vector.max(best[:, b, at], key[:, :]), norm.tick)
                    nc.vector.tensor_scalar(where[:, b, at], best[:, b, at], 4, None, ALU.arith_shift_right)\
                      .then_inc(found, 1)
                    dve.wait_ge(found, q * HEADS + h + 1)

            def combine(q, b, uses):
                step(nc.vector.tensor_scalar(low[:, :], best[:, b, :], 15, None, ALU.bitwise_and))
                step(nc.vector.tensor_scalar(cnt[:, :], low[:, :], -1.0, 16.0, ALU.mult, ALU.add))
                step(nc.vector.scalar_tensor_tensor(cnt[:, :], best[:, b, :], 0.0, cnt[:, :], ALU.is_gt, ALU.mult))
                step(nc.vector.tensor_tensor_scan(cum[:, :], again[:, :], cnt[:, :], 0.0, ALU.mult, ALU.add))
                step(nc.vector.tensor_tensor(cum[:, :], cum[:, :], cnt[:, :], ALU.subtract))
                step(nc.vector.tensor_scalar(cum[:, :], cum[:, :], -1.0, float(TOPK), ALU.mult, ALU.add))
                step(nc.vector.scalar_tensor_tensor(kept[:, :], cum[:, :], 0.0, cnt[:, :], ALU.max, ALU.min))
                dve.wait_ge(gathered[b], uses * 16 * HK)
                step(nc.vector.tensor_tensor(heads(e[:, :]), heads(rows[:, b, :, CH]),
                                             att.own[:, ds(q, 1), :].rearrange("p a h -> p h a")
                                             .broadcast_to([P, HEADS, TOPK]), ALU.add))
                step(nc.vector.scalar_tensor_tensor(e[:, :], e[:, :], 0.2, e[:, :], ALU.mult, ALU.max))
                step(nc.vector.tensor_tensor(heads(cum[:, :]), heads(e[:, :]),
                                             heads(e[:, :])[:, :, 0:1].broadcast_to([P, HEADS, TOPK]), ALU.subtract))
                nc.vector.tensor_scalar(e[:, :], cum[:, :], 0.0, None, ALU.min).then_inc(e_ready, 1)
                dve.wait_ge(ez_ready, q + 1)
                step(nc.vector.tensor_tensor(ez[:, :], ez[:, :], kept[:, :], ALU.mult))
                step(nc.vector.tensor_reduce(den[:, :], heads(ez[:, :]), AX.X, ALU.add))
                step(nc.vector.reciprocal(den[:, :], den[:, :]))
                step(nc.vector.tensor_tensor(heads(ez[:, :]), heads(ez[:, :]),
                                             den[:, :].unsqueeze(2).broadcast_to([P, HEADS, TOPK]), ALU.mult))
                step(nc.vector.tensor_tensor(rows[:, b, :, 0:CH], rows[:, b, :, 0:CH],
                                             ez[:, :].unsqueeze(2).broadcast_to([P, HK, CH]), ALU.mult))
                nc.vector.tensor_reduce(o[:, :].rearrange("p (h c) -> p h c", h=HEADS),
                                        rows[:, b, :, 0:CH].rearrange("p (h k) c -> p h c k", k=TOPK),
                                        AX.X, ALU.add).then_inc(used, 1)
                dve.wait_ge(used, q + 3)
                nc.vector.tensor_scalar(neg[:, :], o[:, :], 0.0, None, ALU.min).then_inc(neg_ready, 1)
                dve.wait_ge(elu_ready, q + 1)
                step(nc.vector.scalar_tensor_tensor(o[:, :], o[:, :], 0.0, neg[:, :], ALU.max, ALU.add))
                dve.wait_ge(x_ready, q * 16 + 16)
                nc.vector.scalar_tensor_tensor(o[:, :], o[:, :], -1.0, xt[:, :], ALU.add, ALU.add).then_inc(x_used, 1)
                dve.wait_ge(x_used, q + 2)
                dve.wait_ge(stored, q * 16 + 16)
                norm.vector(dve, step, res[:, :], o[:, :], q + 1).then_inc(res_ready, 1)
                dve.wait_ge(res_ready, q + 1)

            per = 8 + 18
            search(0, 0)
            with dve.Fori(0, TILES // 2) as i:
                step.enter(i, 2 * per)
                search(i * 2 + 1, 1)
                combine(i * 2, 0, i + 1)
                search(i * 2 + 2, 0)
                combine(i * 2 + 1, 1, i + 1)
                step.leave(TILES // 2)
            combine(TILES - 1, 0, TILES // 2 + 1)


def gather_sum(g, cols, key, x, acc, width):
    nc = g.nc
    RING, UN = 9, 3
    with g.phase() as ctx:
        spot = g.sbuf(ctx, "spot", [P, RING, CHUNKS], U32)
        rows = g.sbuf(ctx, "rows", [P, RING, CHUNKS, D], F32)
        hot = g.sbuf(ctx, "hot", [P, UN, CHUNKS, width], F32)
        sums = [g.psum(ctx, "sums", [P, width], F32) for _ in range(UN)]
        staged, hot_made, summed, added = (g.sem(ctx, n) for n in ("staged", "hot_made", "summed", "added"))
        tick = g.sem(ctx, "tick")
        gathered = [g.sem(ctx, "gathered") for _ in range(RING)]
        block = ctx.enter_context(nc.Block())

        @block.scalar
        def _(act):
            nc.scalar.preload_act_table(ACT.Copy)
            with act.Fori(0, GROUPS // RING) as i:
                for b in range(RING):
                    act.wait_ge(summed, i * RING + b + 1)
                    nc.scalar.copy(spot[:, b, :], cols["source"][:, ds(i * RING + b, 1), :]).then_inc(staged, 1)

        @block.gpsimd
        def _(pool):
            with pool.Fori(0, GROUPS // RING) as i:
                for b in range(RING):
                    pool.wait_ge(staged, i * RING + b + 1)
                    pool.sem_inc(tick, 1)
                    for c in range(CHUNKS):
                        pool.indirect_dma_start(rows[:, b, c, :], None, x,
                                                bass.IndirectOffsetOnAxis(ap=spot[:, b, c:c + 1], axis=0))\
                            .then_inc(gathered[b], 16)

        @block.vector
        def _(dve):
            dve.sem_inc(summed, RING)
            dve.sem_inc(added, UN)
            with dve.Fori(0, GROUPS // UN) as i:
                def make(b):
                    dve.wait_ge(summed, i * UN + b + 1 + RING - UN)
                    for c in range(CHUNKS):
                        at = cols[key][:, ds(i * UN + b, 1), c]
                        ins = nc.vector.tensor_scalar(hot[:, b, c, :], g.keys_row[:, 0:width], at, None,
                                                      ALU.is_equal)
                    ins.then_inc(hot_made, 1)

                def add(b):
                    base = nc.vector.value_load(g.base_row[0:1, ds(i * UN + b, 1)], min_val=0, max_val=NP - WIN)
                    dve.wait_ge(summed, i * UN + b + RING + 1)
                    dve.wait_ge(added, i * UN + b + UN)
                    nc.vector.tensor_tensor(acc[:, :, ds(base, WIN)], acc[:, :, ds(base, WIN)],
                                            sums[b][:, :].rearrange("p (r w) -> p r w", w=WIN),
                                            ALU.add).then_inc(added, 1)

                make(0)
                for b in range(1, UN):
                    make(b)
                    add(b - 1)
                add(UN - 1)

        @block.tensor
        def _(pe):
            with pe.Fori(0, GROUPS // RING) as i:
                for b in range(RING):
                    pe.wait_ge(hot_made, i * RING + b + 1)
                    pe.wait_ge(added, i * RING + b + 1)
                    pe.wait_ge(gathered[b], i * (16 * CHUNKS) + 16 * CHUNKS)
                    for c in range(CHUNKS):
                        ins = nc.tensor.matmul(sums[b % UN][:, :], rows[:, b, c, :], hot[:, b % UN, c, :],
                                               start=(c == 0), stop=(c == CHUNKS - 1))
                    ins.then_inc(summed, 1)


def mixed_sum(g, cols, x, acc):
    nc = g.nc
    GATHER = BATCH - DENSE
    with g.phase() as ctx:
        rows_x = g.sbuf(ctx, "rows_x", [P, TILES, D], F32)
        weight_part = g.sbuf(ctx, "weight_part", [P, PARTS, GROUPS, CHUNKS], F32)
        rounded = g.sbuf(ctx, "rounded", [P, GROUPS, CHUNKS], BF16)
        batch_row = g.sbuf(ctx, "batch_row", [1, BATCHES], I32)
        ahead_row = g.sbuf(ctx, "ahead_row", [1, BATCHES, BATCH], I32)
        zeros = g.sbuf(ctx, "zeros", [P, SPAN], F32)
        hot_key = g.sbuf(ctx, "hot_key", [P, DENSE, CHUNKS, KEYS], BF16)
        hot_low = g.sbuf(ctx, "hot_low", [P, DENSE, CHUNKS, PARTS, P], BF16)
        dense = g.sbuf(ctx, "dense", [P, TILES, SPAN], F32)
        spot = g.sbuf(ctx, "spot", [P, GATHER, CHUNKS], U32)
        rows = g.sbuf(ctx, "rows", [P, GATHER, CHUNKS, D], F32)
        hot = g.sbuf(ctx, "hot", [P, GATHER, CHUNKS, WIN], F32)
        count = [g.psum(ctx, "count", [P, KEYS], F32) for _ in range(2)]
        sums = [g.psum(ctx, "sums", [P, WIN], F32) for _ in range(2)]
        product = g.psum(ctx, "product", [P, SPAN], F32)
        vec, x_loaded, ready = g.sem(ctx, "vec"), g.sem(ctx, "x_loaded"), g.sem(ctx, "ready")
        dense_made, dense_used = g.sem(ctx, "dense_made"), g.sem(ctx, "dense_used")
        put, multiplied = g.sem(ctx, "put"), g.sem(ctx, "multiplied")
        staged, hot_made, summed, added, tick = (
            g.sem(ctx, n) for n in ("staged", "hot_made", "summed", "added", "tick"))
        gathered = [g.sem(ctx, "gathered") for _ in range(GATHER)]
        block = ctx.enter_context(nc.Block())

        @block.sync
        def _(sp):
            sp.dma_start(rows_x[:, :, :], x.rearrange("(t p) d -> p t d", p=P)).then_inc(x_loaded, 16)

        @block.scalar
        def _(act):
            nc.scalar.preload_act_table(ACT.Copy)

            def stage(i, j):
                act.wait_ge(summed, i * GATHER + j + 1)
                nc.scalar.copy(spot[:, j, :], cols["source"][:, ds(i * BATCH + DENSE + j, 1), :])\
                  .then_inc(staged, 1)

            def batch(i, last):
                act.wait_ge(multiplied, i + 1)
                nc.scalar.copy(dense[:, :, :], zeros[:, :].unsqueeze(1).broadcast_to([P, TILES, SPAN])).then_inc(put, 1)
                for j in range(GATHER):
                    if j < DENSE:
                        ahead = nc.scalar.value_load(ahead_row[0:1, ds(i, 1), j], min_val=0, max_val=SPAN - WIN)
                        act.wait_ge(dense_used, i * DENSE + j + 1 + DENSE)
                        nc.scalar.copy(dense[:, :, ds(ahead, WIN)],
                                       count[j % 2][:, :].rearrange("p (t w) -> p t w", w=WIN)).then_inc(put, 1)
                    if not last:
                        stage(i + 1, j)

            for j in range(GATHER):
                stage(0, j)
            act.wait_ge(ready, 1)
            with act.Fori(0, BATCHES - 1) as i:
                batch(i, False)
            batch(BATCHES - 1, True)

        @block.gpsimd
        def _(pool):
            with pool.Fori(0, BATCHES) as i:
                for j in range(GATHER):
                    pool.wait_ge(staged, i * GATHER + j + 1)
                    pool.sem_inc(tick, 1)
                    for c in range(CHUNKS):
                        pool.indirect_dma_start(rows[:, j, c, :], None, x,
                                                bass.IndirectOffsetOnAxis(ap=spot[:, j, c:c + 1], axis=0))\
                            .then_inc(gathered[j], 16)

        @block.vector
        def _(dve):
            step = Steps(dve, vec)
            dve.sem_inc(summed, GATHER)
            dve.sem_inc(added, 2)
            dve.sem_inc(dense_used, DENSE)
            dve.sem_inc(put, 1)
            dve.sem_inc(multiplied, 1)
            step(nc.vector.memset(zeros[:, :], 0.0))
            groups = g.base_row[:, 0:GROUPS].rearrange("a (i b) -> a i b", b=BATCH)
            step(nc.vector.tensor_scalar(batch_row[:, :], groups[:, :, 0], float(NP - SPAN), None, ALU.min))
            step(nc.vector.tensor_tensor(ahead_row[:, :, :], groups,
                                         batch_row[:, :].unsqueeze(2).broadcast_to([1, BATCHES, BATCH]),
                                         ALU.subtract))
            rest = cols["weight"][:, :, :]
            for j in range(PARTS):
                step(nc.vector.tensor_copy(rounded[:, :, :], rest))
                step(nc.vector.tensor_copy(weight_part[:, j, :, :], rounded[:, :, :]))
                if j < PARTS - 1:
                    step(nc.vector.tensor_tensor(weight_part[:, PARTS - 1, :, :], rest, weight_part[:, j, :, :],
                                                 ALU.subtract))
                    rest = weight_part[:, PARTS - 1, :, :]
            dve.sem_inc(ready, 1)

            def make_dense(i, j):
                dve.wait_ge(dense_used, i * DENSE + j + 1)
                for c in range(CHUNKS):
                    nc.vector.tensor_scalar(hot_key[:, j, c, :], g.keys_row[:, 0:KEYS],
                                            cols["key"][:, ds(i * BATCH + j, 1), c], None, ALU.is_equal)
                    for part in range(PARTS):
                        ins = nc.vector.tensor_scalar(hot_low[:, j, c, part, :], g.keys_row[:, 0:P],
                                                      cols["low"][:, ds(i * BATCH + j, 1), c],
                                                      weight_part[:, part, ds(i * BATCH + j, 1), c],
                                                      ALU.is_equal, ALU.mult)
                ins.then_inc(dense_made, 1)

            def make_hot(i, j):
                dve.wait_ge(summed, i * GATHER + j + 1)
                for c in range(CHUNKS):
                    ins = nc.vector.tensor_scalar(hot[:, j, c, :], g.keys_row[:, 0:WIN],
                                                  cols["place"][:, ds(i * BATCH + DENSE + j, 1), c],
                                                  cols["weight"][:, ds(i * BATCH + DENSE + j, 1), c],
                                                  ALU.is_equal, ALU.mult)
                ins.then_inc(hot_made, 1)

            ADDS = GATHER + 1
            place_of = list(range(GATHER - 1)) + [GATHER]

            def add_sums(i, j):
                base = nc.vector.value_load(g.base_row[0:1, ds(i * BATCH + DENSE + j, 1)], min_val=0,
                                            max_val=NP - WIN)
                dve.wait_ge(summed, i * GATHER + j + GATHER + 1)
                dve.wait_ge(added, i * ADDS + place_of[j] + 2)
                nc.vector.tensor_tensor(acc[:, 0, ds(base, WIN)], acc[:, 0, ds(base, WIN)], sums[j % 2][:, :],
                                        ALU.add).then_inc(added, 1)

            def add_product(i):
                base = nc.vector.value_load(batch_row[0:1, ds(i, 1)], min_val=0, max_val=NP - SPAN)
                dve.wait_ge(multiplied, i + 2)
                dve.wait_ge(added, i * ADDS + GATHER + 1)
                nc.vector.tensor_tensor(acc[:, 0, ds(base, SPAN)], acc[:, 0, ds(base, SPAN)], product[:, :],
                                        ALU.add).then_inc(added, 1)

            def batch(i, last):
                for j in range(GATHER):
                    if j == GATHER - 1:
                        add_product(i)
                    add_sums(i, j)
                    if not last:
                        if j < DENSE:
                            make_dense(i + 1, j)
                        make_hot(i + 1, j)

            for j in range(GATHER):
                if j < DENSE:
                    make_dense(0, j)
                make_hot(0, j)
            with dve.Fori(0, BATCHES - 1) as i:
                batch(i, False)
            batch(BATCHES - 1, True)

        @block.tensor
        def _(pe):
            pe.wait_ge(ready, 1)
            pe.wait_ge(x_loaded, 16)
            with pe.Fori(0, BATCHES) as i:
                def count_edges(j):
                    ahead = nc.tensor.value_load(ahead_row[0:1, ds(i, 1), j], min_val=0, max_val=SPAN - WIN)
                    pe.wait_ge(dense_made, i * DENSE + j + 1)
                    pe.wait_ge(put, i * (DENSE + 1) + j + 1)
                    for c in range(CHUNKS):
                        for part in range(PARTS):
                            nc.tensor.matmul(count[j % 2][:, :], hot_low[:, j, c, part, :], hot_key[:, j, c, :],
                                             start=(c == 0 and part == 0), stop=False)
                    pe.wait_ge(put, i * (DENSE + 1) + j + 2)
                    nc.tensor.matmul(count[j % 2][:, :], g.ident[:, :], dense[:, :, ds(ahead, WIN)],
                                     start=False, stop=True).then_inc(dense_used, 1)

                def sum_rows(j):
                    pe.wait_ge(hot_made, i * GATHER + j + 1)
                    pe.wait_ge(added, i * (GATHER + 1) + max(j + 1, 2))
                    pe.wait_ge(gathered[j], i * (16 * CHUNKS) + 16 * CHUNKS)
                    for c in range(CHUNKS):
                        ins = nc.tensor.matmul(sums[j % 2][:, :], rows[:, j, c, :], hot[:, j, c, :],
                                               start=(c == 0), stop=(c == CHUNKS - 1))
                    ins.then_inc(summed, 1)

                for j in range(DENSE):
                    count_edges(j)
                    sum_rows(j)
                pe.wait_ge(put, i * (DENSE + 1) + DENSE + 2)
                pe.wait_ge(added, i * (GATHER + 1) + 2)
                for k in range(TILES):
                    ins = nc.tensor.matmul(product[:, :], rows_x[:, k, :], dense[:, k, :], start=(k == 0),
                                           stop=(k == TILES - 1))
                ins.then_inc(multiplied, 1)
                for j in range(DENSE, GATHER):
                    sum_rows(j)


def combine_layer(g, acc, w_agg, w_self, self_turned, bias, x, out, in_deg):
    nc = g.nc
    R = w_agg.shape[0]
    with g.phase() as ctx:
        wt = g.sbuf(ctx, "w_agg", [P, R, D], F32)
        ws = g.sbuf(ctx, "w_self", [P, D], F32)
        ws_in = g.sbuf(ctx, "w_self_in", [P, D], F32)
        brow = g.sbuf(ctx, "bias_row", [1, D], F32)
        ones = g.sbuf(ctx, "ones", [1, P], F32)
        inv = g.sbuf(ctx, "inverse_degree", [P, TILES], F32)
        rows = g.sbuf(ctx, "rows", [P, TILES, D], F32)
        x_turned = g.sbuf(ctx, "x_turned", [P, 2, D], F32)
        part = g.sbuf(ctx, "part", [P, 2, D], F32)
        val = g.sbuf(ctx, "val", [P, D], F32)
        norm = AllNorm(g, ctx)
        ps_x = [g.psum(ctx, "ps_x", [P, D], F32) for _ in range(2)]
        ps_a = [g.psum(ctx, "ps_agg", [P, D], F32) for _ in range(2)]
        ps_s = [g.psum(ctx, "ps_self", [P, D], F32) for _ in range(2)]
        w_loaded, vec, w_ps, w_sb = (g.sem(ctx, n) for n in ("w_loaded", "vec", "w_ps", "w_sb"))
        loaded = [g.sem(ctx, "loaded") for _ in range(TILES // PIECE)]
        x_ps, x_sb, summed, part_made, used, res_ready, stored = (
            g.sem(ctx, n) for n in ("x_ps", "x_sb", "summed", "part_made", "used", "res_ready", "stored"))
        block = ctx.enter_context(nc.Block())

        @block.sync
        def _(sp):
            sp.dma_start(ws_in[:, :], w_self).then_inc(w_loaded, 16)
            sp.dma_start(brow[:, :], bias.rearrange("(a n) -> a n", a=1)).then_inc(w_loaded, 16)
            sp.dma_start(wt[:, :, :], w_agg.rearrange("r i o -> i r o")).then_inc(w_loaded, 16)
            load_pieces(sp, x, rows, loaded)
            store_pieces(sp, out, rows, res_ready, stored)

        @block.tensor
        def _(pe):
            def turn_x(t):
                pe.wait_ge(loaded[t // PIECE], 16)
                if t >= 2:
                    pe.wait_ge(x_sb, t - 1)
                nc.tensor.transpose(ps_x[t % 2][:, :], rows[:, t, :], g.ident[:, :]).then_inc(x_ps, 1)

            pe.wait_ge(w_loaded, 48)
            pe.wait_ge(vec, 1)
            if self_turned:
                nc.tensor.transpose(ps_x[0][:, :], ws_in[:, :], g.ident[:, :]).then_inc(w_ps, 1)
            pe.wait_ge(w_sb, 1)
            turn_x(0)
            for t in range(TILES):
                b = t % 2
                if t + 1 < TILES:
                    turn_x(t + 1)
                if t >= 2:
                    pe.wait_ge(used, t - 1)
                for r in range(R):
                    nc.tensor.matmul(ps_a[b][:, :], acc[:, r, t * P:(t + 1) * P], wt[:, r, :],
                                     start=(r == 0), stop=(r == R - 1))
                nc.tensor.matmul(ps_s[b][:, :], ones[:, :], brow[:, :], start=True, stop=False)
                pe.wait_ge(x_sb, t + 1)
                nc.tensor.matmul(ps_s[b][:, :], x_turned[:, b, :], ws[:, :], start=False, stop=True)\
                  .then_inc(summed, 1)

        @block.scalar
        def _(act):
            for t in range(TILES + 1):
                if t < TILES:
                    act.wait_ge(x_ps, t + 1)
                    if t >= 2:
                        act.wait_ge(summed, t - 1)
                    nc.scalar.copy(x_turned[:, t % 2, :], ps_x[t % 2][:, :]).then_inc(x_sb, 1)
                if t >= 1:
                    b = (t - 1) % 2
                    act.wait_ge(summed, t)
                    if t >= 3:
                        act.wait_ge(used, t - 2)
                    if in_deg is None:
                        ins = nc.scalar.copy(part[:, b, :], ps_a[b][:, :])
                    else:
                        ins = nc.scalar.activation(part[:, b, :], ps_a[b][:, :], ACT.Copy, scale=inv[:, t - 1:t])
                    ins.then_inc(part_made, 1)
            norm.scalar(act)

        @block.vector
        def _(dve):
            step = Steps(dve, vec)
            step(nc.vector.memset(ones[:, :], 1.0))
            norm.start(step)
            if in_deg is not None:
                step(nc.vector.tensor_scalar(inv[:, :], in_deg, -1.0, 1.0, ALU.add, ALU.max))
                step(nc.vector.reciprocal(inv[:, :], inv[:, :]))
            dve.wait_ge(w_loaded, 48)
            if self_turned:
                dve.wait_ge(w_ps, 1)
                nc.vector.tensor_copy(ws[:, :], ps_x[0][:, :]).then_inc(w_sb, 1)
            else:
                nc.vector.tensor_copy(ws[:, :], ws_in[:, :]).then_inc(w_sb, 1)
            for t in range(TILES):
                b = t % 2
                dve.wait_ge(part_made, t + 1)
                step(nc.vector.tensor_tensor(val[:, :], part[:, b, :], ps_s[b][:, :], ALU.add))
                if in_deg is None:
                    ins = nc.vector.tensor_tensor(rows[:, t, :], val[:, :], rows[:, t, :], ALU.add)
                else:
                    ins = nc.vector.scalar_tensor_tensor(rows[:, t, :], val[:, :], 0.0, rows[:, t, :],
                                                         ALU.max, ALU.add)
                ins.then_inc(used, 1)
                dve.wait_ge(used, t + 1)
                norm.take(t, rows[:, t, :])
            norm.finish(dve, step, rows, res_ready)


def clear_tiles(g, tiles):
    nc = g.nc
    with g.phase() as ctx:
        zeroed = g.sem(ctx, "zeroed")
        block = ctx.enter_context(nc.Block())

        @block.vector
        def _(dve):
            for t in tiles:
                nc.vector.memset(t, 0).then_inc(zeroed, 1)
            dve.wait_ge(zeroed, len(tiles))


def gather_layer(g, kinds, key, width, x, out, w_agg, w_self, self_turned, bias, in_deg):
    with ExitStack() as ctx:
        acc = g.sbuf(ctx, "acc", [P, width // WIN, NP], F32)
        clear_tiles(g, [acc[:, :, :].bitcast(U32), g.next_base[:, :].bitcast(U32)])

        def work():
            with ExitStack() as inner:
                cols = edge_columns(g, inner, kinds)
                if "weight" in kinds:
                    mixed_sum(g, cols, x, acc)
                else:
                    gather_sum(g, cols, key, x, acc, width)

        in_windows(g, work)
        combine_layer(g, acc, w_agg, w_self, self_turned, bias, x, out, in_deg)


def gnn(nc, x, src, dst, edge_type, edge_weight, att_w, att_a, w_neigh, w_self, b_self, w_rel, w_root, b_root, out):
    hidden = [nc.dram_tensor(f"x{n}", [NP, D], F32, kind="Internal").ap() for n in (1, 2, 3)]
    with ExitStack() as ctx:
        g = Graph(nc, ctx, src, dst, edge_type, edge_weight)
        out_deg, in_deg = g.sbuf(ctx, "out_deg", [P, TILES], F32), g.sbuf(ctx, "in_deg", [P, TILES], F32)
        constants(g)
        window_bases(g)
        with ExitStack() as mid:
            adj = g.sbuf(mid, "adj", [P, TILES, NP], BF16)
            clear_tiles(g, [adj[:, :, :].bitcast(U32)])

            def work():
                with ExitStack() as inner:
                    cols = edge_columns(g, inner, ("low", "key"))
                    add_edges(g, adj, cols["low"], cols["key"])

            in_windows(g, work)
            out_degrees(g, adj, out_deg)
            turn(g, adj)
            propagate(g, adj, out_deg, in_deg, x, hidden[0])
            att = Attention(g, mid)
            project(g, att, hidden[0], att_w, att_a)
            code = g.sbuf(mid, "code", [P, HEADS, NP], U16)
            rank(g, att, code)
            attend(g, att, adj, code, hidden[0], hidden[1])
        gather_layer(g, ("low", "key", "place", "weight", "source"), "place", WIN, hidden[1], hidden[2],
                     w_neigh.rearrange("(r i) o -> r i o", r=1), w_self, False, b_self, None)
        gather_layer(g, ("typed", "source"), "typed", TYPES * WIN, hidden[2], out,
                     w_rel, w_root, True, b_root, in_deg[:, :])


_INS = ['x', 'src', 'dst', 'edge_type_8', 'edge_weight', 'L1_gnn_W', 'L1_gnn_att', 'L2_gnn_W_neigh',
        'L2_gnn_W_self', 'L2_gnn_b_self', 'L3_gnn_W_rel', 'L3_gnn_W_self_w', 'L3_gnn_W_self_b']


def kernel(**inputs):
    import numpy as np
    import concourse.bacc as bacc
    from concourse.bass_utils import run_bass_kernel_spmd

    nc = bacc.Bacc("TRN2", target_bir_lowering=False, num_devices=1)
    arrays, args = {}, []
    for name in _INS:
        a = np.ascontiguousarray(inputs[name])
        arrays[f"in_{name}"] = a
        args.append(nc.dram_tensor(f"in_{name}", a.shape, mybir.dt.from_np(a.dtype), kind="ExternalInput").ap())
    out = nc.dram_tensor("out", (NODES, D), F32, kind="ExternalOutput").ap()
    gnn(nc, *args, out)
    r = run_bass_kernel_spmd(nc, [arrays], core_ids=[0])
    return r.results[0]["out"]
```

```python
from contextlib import ExitStack

import concourse.bass as bass
from concourse import mybir

F32, BF16 = mybir.dt.float32, mybir.dt.bfloat16
I32, U32, U16, I16 = mybir.dt.int32, mybir.dt.uint32, mybir.dt.uint16, mybir.dt.int16
ALU, ACT, AX = mybir.AluOpType, mybir.ActivationFunctionType, mybir.AxisListType
ds = bass.ds

P = 128
NODES, D, EDGES, HEADS, CH, TOPK, TYPES = 3125, 128, 100000, 4, 32, 8, 8
TILES = -(-NODES // P)
NP = TILES * P
FULL, REST = NODES // P, NODES % P
CHUNKS = 3
GE = CHUNKS * P
GROUPS = -(-EDGES // GE)
GT = -(-GROUPS // P)
LOADS = EDGES // GE // P + 2
WIN = 18
WINDOWS = -(-NODES // WIN)
KEYS = TILES * WIN
OFF = 20000.0
EPS = 1e-5
PARTS = 3
BATCH, DENSE, SPAN = 18, 8, 120
BATCHES = -(-GROUPS // BATCH)
PADDED = BATCHES * BATCH


class Steps:

    def __init__(self, eng, sem):
        self.eng, self.sem, self.base, self.n = eng, sem, 0, 0

    def __call__(self, ins, tick=None):
        ins.then_inc(self.sem, 1)
        self.n += 1
        self.eng.wait_ge(self.sem, self.base + self.n)
        if tick is not None:
            self.eng.sem_inc(tick, 1)

    def enter(self, i, per):
        self.start, self.per = self.base + self.n, per
        self.base, self.n = self.start + i * per, 0

    def leave(self, count):
        assert self.n == self.per, (self.n, self.per)
        self.base, self.n = self.start + count * self.per, 0


class Graph:
    def __init__(self, nc, ctx, src, dst, etype, weight):
        self.nc, self.names = nc, 0
        self.src, self.dst, self.etype, self.weight = src, dst, etype, weight
        sb = lambda name, shape, dt: ctx.enter_context(nc.sbuf_tensor(name, shape, dt))
        self.ident = sb("ident", [P, P], F32)
        self.identb = sb("identb", [P, P], BF16)
        self.base = sb("base", [P, GT], F32)
        self.next_base = sb("next_base", [P, GT], F32)
        self.wide = sb("wide", [1, 1], I32)

    def phase(self, gpsimd_transfers=False):
        ctx = ExitStack()
        self.sems = []
        ctx.callback(self.clear, self.sems, gpsimd_transfers)
        return ctx

    def clear(self, sems, gpsimd_transfers):
        if gpsimd_transfers:
            self.nc.gpsimd.dma_reset()
        for sem in sems:
            self.nc.gpsimd.sem_clear(sem)
        if sems:
            self.nc.all_engine_barrier()

    def sem(self, ctx, name):
        self.names += 1
        self.sems.append(ctx.enter_context(self.nc.semaphore(f"{name}_{self.names}")))
        return self.sems[-1]

    def sbuf(self, ctx, name, shape, dt):
        self.names += 1
        return ctx.enter_context(self.nc.sbuf_tensor(f"{name}_{self.names}", shape, dt))

    def psum(self, ctx, name, shape, dt):
        self.names += 1
        return ctx.enter_context(self.nc.psum_tensor(f"{name}_{self.names}", shape, dt))


def load_edges(eng, dram, tile, sem):
    whole, full = EDGES // GE, EDGES // GE // P
    for t in range(full):
        eng.dma_start(tile[:, t, :], dram[t * P * GE:(t + 1) * P * GE].rearrange("(g e) -> g e", e=GE)).then_inc(sem, 16)
    eng.dma_start(tile[0:whole - full * P, full, :],
                  dram[full * P * GE:whole * GE].rearrange("(g e) -> g e", e=GE)).then_inc(sem, 16)
    eng.dma_start(tile[whole - full * P:whole - full * P + 1, full, 0:EDGES - whole * GE],
                  dram[whole * GE:EDGES].rearrange("(g e) -> g e", g=1)).then_inc(sem, 16)


def constants(g):
    nc = g.nc
    with g.phase() as ctx:
        zeroed, made = g.sem(ctx, "zeroed"), g.sem(ctx, "made")
        block = ctx.enter_context(nc.Block())

        @block.gpsimd
        def _(pool):
            pool.memset(g.ident[:, :], 0.0).then_inc(zeroed, 1)
            pool.memset(g.identb[:, :], 0.0).then_inc(zeroed, 1)
            pool.wait_ge(zeroed, 2)
            for m in (g.ident, g.identb):
                pool.affine_select(out=m[:, :], in_=m[:, :], compare_op=ALU.not_equal, fill=1.0, base=0,
                                   pattern=[[-1, P]], channel_multiplier=1).then_inc(made, 1)
            pool.wait_ge(made, 2)


def window_bases(g, clear):
    nc = g.nc
    with g.phase() as ctx:
        dst_i = g.sbuf(ctx, "dst_i", [P, GT, GE], I32)
        dst_f = g.sbuf(ctx, "dst_f", [P, GT, GE], F32)
        dst_m = g.sbuf(ctx, "dst_m", [P, GT, GE], F32)
        hi = g.sbuf(ctx, "hi", [P, GT], F32)
        over = g.sbuf(ctx, "over", [P, 1], F32)
        ones = g.sbuf(ctx, "ones", [P, 1], F32)
        total = g.psum(ctx, "total", [1, 1], F32)
        turned = g.psum(ctx, "turned", [1, GT * P], F32)
        base_row = g.sbuf(ctx, "base_row", [1, GT * P], F32)
        ahead = g.sbuf(ctx, "ahead", [1, BATCHES], F32)
        filled, loaded, counted = g.sem(ctx, "filled"), g.sem(ctx, "loaded"), g.sem(ctx, "counted")
        vec, zeroed = g.sem(ctx, "vec"), g.sem(ctx, "zeroed")
        zero = g.sbuf(ctx, "zero", [P, 1], F32)
        n = clear.shape[1]
        block = ctx.enter_context(nc.Block())

        @block.gpsimd
        def _(pool):
            pool.memset(zero[:, :], 0.0).then_inc(zeroed, 1)
            pool.memset(clear[:, 0:n // 2], 0.0).then_inc(zeroed, 1)
            pool.wait_ge(zeroed, 3)

        @block.scalar
        def _(act):
            act.wait_ge(zeroed, 1)
            nc.scalar.copy(clear[:, n // 2:n], zero[:, :].broadcast_to([P, n - n // 2])).then_inc(zeroed, 1)

        @block.sync
        def _(sp):
            sp.wait_ge(filled, 1)
            load_edges(sp, g.dst, dst_i, loaded)

        @block.vector
        def _(dve):
            step = Steps(dve, vec)
            nc.vector.memset(dst_i[:, :, :], int(OFF)).then_inc(filled, 1)
            step(nc.vector.memset(ones[:, :], 1.0))
            step(nc.vector.memset(g.next_base[:, :], 0.0))
            dve.wait_ge(loaded, 16 * LOADS)
            step(nc.vector.tensor_copy(dst_f[:, :, :], dst_i[:, :, :]))
            step(nc.vector.tensor_reduce(g.base[:, :], dst_f[:, :, :], AX.X, ALU.min))
            step(nc.vector.tensor_scalar(g.base[:, :], g.base[:, :], float(NODES - WIN), None, ALU.min))
            step(nc.vector.scalar_tensor_tensor(dst_m[:, :, :], dst_f[:, :, :], OFF, dst_f[:, :, :],
                                                ALU.is_lt, ALU.mult))
            step(nc.vector.tensor_reduce(hi[:, :], dst_m[:, :, :], AX.X, ALU.max))
            step(nc.vector.tensor_tensor(hi[:, :], hi[:, :], g.base[:, :], ALU.subtract))
            step(nc.vector.tensor_reduce(over[:, :], hi[:, :], AX.X, ALU.max))
            step(nc.vector.tensor_scalar(over[:, :], over[:, :], float(WIN), None, ALU.is_ge))
            dve.wait_ge(counted, 1)
            step(nc.vector.tensor_copy(base_row[:, :], turned[:, :]))
            batches = base_row[:, 0:PADDED].rearrange("a (i b) -> a i b", b=BATCH)
            step(nc.vector.tensor_tensor(ahead[:, :], batches[:, :, DENSE - 1], batches[:, :, 0], ALU.subtract))
            step(nc.vector.tensor_reduce(base_row[:, 0:1], ahead[:, :], AX.X, ALU.max))
            step(nc.vector.tensor_scalar(base_row[:, 0:1], base_row[:, 0:1], float(SPAN - WIN), None, ALU.is_gt))
            step(nc.vector.tensor_tensor(base_row[:, 0:1], base_row[:, 0:1], total[:, :], ALU.add))
            step(nc.vector.tensor_scalar(g.wide[:, :], base_row[:, 0:1], 1.0, None, ALU.min))
            assert step.n == 16

        @block.tensor
        def _(pe):
            pe.wait_ge(vec, 10)
            for t in range(GT):
                nc.tensor.transpose(turned[:, t * P:(t + 1) * P], g.base[:, t:t + 1], g.ident[:, :])
            nc.tensor.matmul(total[:, :], over[:, :], ones[:, :], start=True, stop=True).then_inc(counted, 1)


def edge_columns(g, ctx, kinds):
    g.keys_row = g.sbuf(ctx, "keys_row", [P, 512], I16)
    g.base_row = g.sbuf(ctx, "base_row", [1, GT * P], I32)
    sel = {kind: g.sbuf(ctx, kind, [P, PADDED, CHUNKS], U32 if kind == "source" else F32) for kind in kinds}
    return sel


def group_keys(g, sel):
    nc = g.nc
    with g.phase() as ctx:
        raw, val = {}, {}
        for name in ("dst", "src", "etype", "weight"):
            if name == "etype" and "typed" not in sel or name == "weight" and "weight" not in sel:
                continue
            raw[name] = g.sbuf(ctx, name + "_raw", [P, GT, GE], F32 if name == "weight" else I32)
        place = g.sbuf(ctx, "place", [P, GT, GE], F32)
        bad = g.sbuf(ctx, "bad", [P, GT, GE], F32)
        for kind in sel:
            if kind not in ("place", "weight"):
                val[kind] = g.sbuf(ctx, kind + "_val", [P, GT, GE], F32)
        val["place"] = place
        if "weight" in sel:
            val["weight"] = raw["weight"]
        ps = [g.psum(ctx, "turned", [P, GE], F32) for _ in range(2)]
        filled, loaded, vec = g.sem(ctx, "filled"), g.sem(ctx, "loaded"), g.sem(ctx, "vec")
        turned, copied = g.sem(ctx, "turned"), g.sem(ctx, "copied")
        based = g.sem(ctx, "based")
        base_ps = g.psum(ctx, "base_ps", [1, GT * P], F32)
        jobs = [(kind, t) for kind in sel for t in range(GT)]
        dram = dict(dst=g.dst, src=g.src, etype=g.etype, weight=g.weight)
        counted = g.sem(ctx, "counted")
        block = ctx.enter_context(nc.Block())

        @block.gpsimd
        def _(pool):
            pool.iota(g.keys_row[:, :], [[1, 512]], base=0, channel_multiplier=0).then_inc(counted, 1)
            pool.wait_ge(counted, 1)

        @block.sync
        def _(sp):
            sp.wait_ge(filled, len(raw))
            for name in raw:
                load_edges(sp, dram[name], raw[name], loaded)

        @block.vector
        def _(dve):
            step = Steps(dve, vec)
            for name in raw:
                nc.vector.memset(raw[name][:, :, :], int(OFF) if name == "dst" else 0).then_inc(filled, 1)
            dve.wait_ge(based, 1)
            step(nc.vector.tensor_copy(g.base_row[:, :], base_ps[:, :]))
            dve.wait_ge(loaded, 16 * LOADS * len(raw))
            step(nc.vector.tensor_copy(place[:, :, :], raw["dst"][:, :, :]))
            for t in range(GT):
                step(nc.vector.tensor_scalar(place[:, t, :], place[:, t, :], g.base[:, t:t + 1], None,
                                             ALU.subtract))
            step(nc.vector.tensor_scalar(bad[:, :, :], place[:, :, :], float(WIN), OFF, ALU.is_ge, ALU.mult))
            step(nc.vector.tensor_tensor(bad[:, :, :], bad[:, :, :], place[:, :, :], ALU.add))
            step(nc.vector.tensor_scalar(place[:, :, :], place[:, :, :], 0.0, OFF, ALU.is_lt, ALU.mult))
            step(nc.vector.tensor_tensor(place[:, :, :], place[:, :, :], bad[:, :, :], ALU.add))
            if "source" in sel:
                step(nc.vector.tensor_copy(val["source"][:, :, :], raw["src"][:, :, :]))
            if "typed" in sel:
                step(nc.vector.tensor_copy(val["typed"][:, :, :], raw["etype"][:, :, :]))
                step(nc.vector.scalar_tensor_tensor(val["typed"][:, :, :], val["typed"][:, :, :], float(WIN),
                                                    place[:, :, :], ALU.mult, ALU.add))
            if "low" in sel:
                low, high = raw["dst"], raw["src"]
                step(nc.vector.tensor_scalar(low[:, :, :], raw["src"][:, :, :], P - 1, None, ALU.bitwise_and))
                step(nc.vector.tensor_scalar(high[:, :, :], raw["src"][:, :, :], 7, None,
                                             ALU.arith_shift_right))
                step(nc.vector.tensor_copy(val["low"][:, :, :], low[:, :, :]))
                step(nc.vector.tensor_copy(bad[:, :, :], high[:, :, :]))
                step(nc.vector.scalar_tensor_tensor(val["key"][:, :, :], bad[:, :, :], float(WIN),
                                                    place[:, :, :], ALU.mult, ALU.add))
            for n, (kind, t) in enumerate(jobs):
                dve.wait_ge(turned, n + 1)
                rows = min(PADDED - P * t, P)
                nc.vector.tensor_copy(
                    sel[kind][:, P * t:P * t + rows, :],
                    ps[n % 2][:, :].rearrange("p (c g) -> p g c", g=P)[:, 0:rows, :]).then_inc(copied, 1)
            dve.wait_ge(copied, len(jobs))

        @block.tensor
        def _(pe):
            for t in range(GT):
                ins = nc.tensor.transpose(base_ps[:, t * P:(t + 1) * P], g.base[:, t:t + 1], g.ident[:, :])
            ins.then_inc(based, 1)
            n_vec = 6 + GT + ("source" in sel) + 2 * ("typed" in sel) + 5 * ("low" in sel)
            pe.wait_ge(vec, n_vec)
            for n, (kind, t) in enumerate(jobs):
                if n >= 2:
                    pe.wait_ge(copied, n - 1)
                for c in range(CHUNKS):
                    ins = nc.tensor.transpose(ps[n % 2][:, c * P:(c + 1) * P],
                                              val[kind][:, t, c * P:(c + 1) * P], g.ident[:, :])
                ins.then_inc(turned, 1)


def add_edges(g, adj, low, key):
    nc = g.nc
    UN, TURN = 3, 9
    with g.phase() as ctx:
        hot_key = g.sbuf(ctx, "hot_key", [P, UN, CHUNKS, KEYS], BF16)
        hot_low = g.sbuf(ctx, "hot_low", [P, UN, CHUNKS, P], BF16)
        count = [g.psum(ctx, "count", [P, KEYS], F32) for _ in range(UN)]
        hots_made, counted, put = g.sem(ctx, "hots_made"), g.sem(ctx, "counted"), g.sem(ctx, "put")
        block = ctx.enter_context(nc.Block())

        @block.vector
        def _(dve):
            dve.sem_inc(counted, UN)
            with dve.Fori(0, GROUPS // TURN) as i:
                for n in range(TURN):
                    b = n % UN
                    dve.wait_ge(counted, i * TURN + n + 1)
                    for c in range(CHUNKS):
                        nc.vector.tensor_scalar(hot_key[:, b, c, :], g.keys_row[:, 0:KEYS],
                                                key[:, ds(i * TURN + n, 1), c], None, ALU.is_equal)
                        ins = nc.vector.tensor_scalar(hot_low[:, b, c, :], g.keys_row[:, 0:P],
                                                      low[:, ds(i * TURN + n, 1), c], None, ALU.is_equal)
                    ins.then_inc(hots_made, 1)

        @block.tensor
        def _(pe):
            pe.sem_inc(put, UN)
            with pe.Fori(0, GROUPS // TURN) as i:
                for n in range(TURN):
                    b = n % UN
                    base = nc.tensor.value_load(g.base_row[0:1, ds(i * TURN + n, 1)], min_val=0, max_val=NP - WIN)
                    pe.wait_ge(hots_made, i * TURN + n + 1)
                    pe.wait_ge(put, i * TURN + n + 1)
                    for c in range(CHUNKS):
                        nc.tensor.matmul(count[b][:, :], hot_low[:, b, c, :], hot_key[:, b, c, :],
                                         start=(c == 0), stop=False)
                    pe.wait_ge(put, i * TURN + n + UN)
                    nc.tensor.matmul(count[b][:, :], g.identb[:, :], adj[:, :, ds(base, WIN)],
                                     start=False, stop=True).then_inc(counted, 1)

        @block.scalar
        def _(act):
            nc.scalar.preload_act_table(ACT.Copy)
            with act.Fori(0, GROUPS // TURN) as i:
                for n in range(TURN):
                    b = n % UN
                    base = nc.scalar.value_load(g.base_row[0:1, ds(i * TURN + n, 1)], min_val=0, max_val=NP - WIN)
                    act.wait_ge(counted, i * TURN + n + UN + 1)
                    nc.scalar.copy(adj[:, :, ds(base, WIN)], count[b][:, :].rearrange("p (t w) -> p t w", w=WIN))\
                      .then_inc(put, 1)


def in_windows(g, work, own=None):
    nc = g.nc
    flag = nc.values_load(g.wide[0:1, 0:1], min_val=0, max_val=1)
    with nc.If(flag):
        with nc.Fori(0, WINDOWS):
            with g.phase() as ctx:
                moved = g.sem(ctx, "moved")
                block = ctx.enter_context(nc.Block())

                @block.vector
                def _(dve):
                    nc.vector.tensor_copy(g.base[:, :], g.next_base[:, :]).then_inc(moved, 1)
                    dve.wait_ge(moved, 1)
                    nc.vector.tensor_scalar(g.next_base[:, :], g.next_base[:, :], float(WIN), None,
                                            ALU.add).then_inc(moved, 1)
                    dve.wait_ge(moved, 2)
            work()
    with nc.Else():
        (own or work)()


def out_degrees(g, adj, deg):
    nc = g.nc
    SHARE = 13
    with g.phase() as ctx:
        unused = g.sbuf(ctx, "unused", [P, NP], BF16)
        by_act, by_dve, whole = g.sem(ctx, "by_act"), g.sem(ctx, "by_dve"), g.sem(ctx, "whole")
        block = ctx.enter_context(nc.Block())

        @block.scalar
        def _(act):
            for k in range(SHARE):
                if k >= 1:
                    act.wait_ge(by_act, k)
                nc.scalar.activation(unused[:, :], adj[:, k, :], ACT.Copy, accum_out=deg[:, k:k + 1])\
                  .then_inc(by_act, 1)

        @block.vector
        def _(dve):
            nc.vector.tensor_reduce(deg[:, SHARE:TILES], adj[:, SHARE:TILES, :], AX.X, ALU.add).then_inc(by_dve, 1)
            dve.wait_ge(by_act, SHARE)
            dve.wait_ge(by_dve, 1)
            nc.vector.tensor_scalar(deg[:, :], deg[:, :], 1.0, None, ALU.add).then_inc(whole, 1)
            dve.wait_ge(whole, 1)


def turn(g, adj):
    nc = g.nc
    SIDE, SLOTS, BANK = 5, 4, 1024
    PLACE, SINCE = (0, 1, 2, 3, 1), (5, 2, 5, 5, 3)
    SQUARES = TILES // SIDE
    W = SIDE * P
    distances = [(d, SQUARES - d, sum(SQUARES - e for e in range(1, d))) for d in range(1, SQUARES)]
    BETWEEN = SQUARES * (SQUARES - 1) // 2 * SIDE
    with g.phase() as ctx:
        upper = g.psum(ctx, "upper", [P, SLOTS * BANK], BF16)
        lower = g.psum(ctx, "lower", [P, SLOTS * BANK], BF16)
        turned, up_put, low_put = g.sem(ctx, "turned"), g.sem(ctx, "up_put"), g.sem(ctx, "low_put")
        block = ctx.enter_context(nc.Block())

        def slot(i, width, start=0):
            return slice(PLACE[i] * BANK + start, PLACE[i] * BANK + start + width)

        def slot_free(pe, put, n, i):
            pe.wait_ge(put, n + 1 + SLOTS - min(SINCE[i], SLOTS))

        @block.tensor
        def _(pe):
            for d, count, before in distances:
                with pe.Fori(0, count) as a:
                    for i in range(SIDE):
                        n = (a + before) * SIDE + i
                        slot_free(pe, up_put, n, i)
                        slot_free(pe, low_put, n, i)
                        for j in range(SIDE):
                            nc.tensor.transpose(upper[:, slot(i, P, j * P)],
                                                adj[:, ds(a * SIDE + i, 1), ds(a * W + d * W + j * P, P)],
                                                g.identb[:, :])
                            ins = nc.tensor.transpose(lower[:, slot(i, P, j * P)],
                                                      adj[:, ds(a * SIDE + d * SIDE + j, 1), ds(a * W + i * P, P)],
                                                      g.identb[:, :])
                        ins.then_inc(turned, 1)
            with pe.Fori(0, SQUARES) as q:
                for r in range(SIDE - 1):
                    n = q * SIDE + BETWEEN + r
                    slot_free(pe, up_put, n, r)
                    slot_free(pe, low_put, n, r)
                    for j in range(r + 1, SIDE):
                        nc.tensor.transpose(upper[:, slot(r, P, (j - r - 1) * P)],
                                            adj[:, ds(q * SIDE + r, 1), ds(q * W + j * P, P)], g.identb[:, :])
                        ins = nc.tensor.transpose(lower[:, slot(r, P, (j - r - 1) * P)],
                                                  adj[:, ds(q * SIDE + j, 1), ds(q * W + r * P, P)],
                                                  g.identb[:, :])
                    ins.then_inc(turned, 1)
                n = q * SIDE + BETWEEN + SIDE - 1
                slot_free(pe, low_put, n, SIDE - 1)
                for j in range(SIDE):
                    ins = nc.tensor.transpose(lower[:, slot(SIDE - 1, P, j * P)],
                                              adj[:, ds(q * SIDE + j, 1), ds(q * W + j * P, P)], g.identb[:, :])
                ins.then_inc(turned, 1)

        @block.scalar
        def _(act):
            act.sem_inc(up_put, SLOTS)
            nc.scalar.preload_act_table(ACT.Copy)
            for d, count, before in distances:
                with act.Fori(0, count) as a:
                    for i in range(SIDE):
                        n = (a + before) * SIDE + i
                        act.wait_ge(turned, n + 1)
                        nc.scalar.copy(adj[:, ds(a * SIDE + d * SIDE, SIDE), ds(a * W + i * P, P)],
                                       upper[:, slot(i, W)].rearrange("p (j c) -> p j c", c=P)).then_inc(up_put, 1)
            with act.Fori(0, SQUARES) as q:
                for r in range(SIDE - 1):
                    n = q * SIDE + BETWEEN + r
                    act.wait_ge(turned, n + 1)
                    nc.scalar.copy(adj[:, ds(q * SIDE + r + 1, SIDE - 1 - r), ds(q * W + r * P, P)],
                                   upper[:, slot(r, W - (r + 1) * P)].rearrange("p (j c) -> p j c", c=P))\
                      .then_inc(up_put, 1)
                act.wait_ge(up_put, q * SIDE + BETWEEN + SIDE - 1 + SLOTS)
                act.sem_inc(up_put, 1)

        @block.vector
        def _(dve):
            dve.sem_inc(low_put, SLOTS)
            for d, count, before in distances:
                with dve.Fori(0, count) as a:
                    for i in range(SIDE):
                        n = (a + before) * SIDE + i
                        dve.wait_ge(turned, n + 1)
                        nc.vector.tensor_copy(adj[:, ds(a * SIDE + i, 1), ds(a * W + d * W, W)],
                                              lower[:, slot(i, W)]).then_inc(low_put, 1)
            with dve.Fori(0, SQUARES) as q:
                for r in range(SIDE - 1):
                    n = q * SIDE + BETWEEN + r
                    dve.wait_ge(turned, n + 1)
                    nc.vector.tensor_copy(adj[:, ds(q * SIDE + r, 1), ds(q * W + (r + 1) * P, W - (r + 1) * P)],
                                          lower[:, slot(r, W - (r + 1) * P)]).then_inc(low_put, 1)
                n = q * SIDE + BETWEEN + SIDE - 1
                dve.wait_ge(turned, n + 1)
                for j in range(SIDE):
                    ins = nc.vector.tensor_tensor(adj[:, ds(q * SIDE + j, 1), ds(q * W + j * P, P)],
                                                  lower[:, slot(SIDE - 1, P, j * P)], g.identb[:, :],
                                                  ALU.add)
                ins.then_inc(low_put, 1)
            dve.wait_ge(low_put, BETWEEN + SQUARES * SIDE + SLOTS)


def split(step, nc, parts, value, rest):
    step(nc.vector.tensor_copy(parts(0), value))
    step(nc.vector.tensor_tensor(rest, value, parts(0), ALU.subtract))
    step(nc.vector.tensor_copy(parts(1), rest))
    return nc.vector.tensor_tensor(parts(2), rest, parts(1), ALU.subtract)


class Norm:

    def __init__(self, g, ctx):
        self.nc = g.nc
        self.stats = g.sbuf(ctx, "stats", [P, 6], F32)
        self.mv = g.sbuf(ctx, "mean_var", [P, 2], F32)
        self.eps = g.sbuf(ctx, "eps", [P, 1], F32)
        self.dev = g.sbuf(ctx, "deviation", [P, 1], F32)
        self.inv = g.sbuf(ctx, "inverse", [P, 1], F32)
        self.var_ready, self.dev_ready = g.sem(ctx, "var_ready"), g.sem(ctx, "dev_ready")
        self.tick = g.sem(ctx, "tick")

    def start(self, step):
        step(self.nc.vector.memset(self.eps[:, :], EPS))

    def vector(self, dve, step, out, value, n):
        nc = self.nc
        step(nc.vector.bn_stats(self.stats[:, :], value), self.tick)
        nc.vector.bn_aggr(self.mv[:, :], self.stats[:, :]).then_inc(self.var_ready, 1)
        dve.wait_ge(self.dev_ready, n)
        step(nc.vector.reciprocal(self.inv[:, :], self.dev[:, :]))
        return nc.vector.tensor_scalar(out, value, self.mv[:, 0:1], self.inv[:, :], ALU.subtract, ALU.mult)

    def scalar(self, act, n):
        act.wait_ge(self.var_ready, n)
        self.nc.scalar.activation(self.dev[:, :], self.mv[:, 1:2], ACT.Sqrt,
                                  bias=self.eps[:, :]).then_inc(self.dev_ready, 1)


class AllNorm:

    def __init__(self, g, ctx):
        self.nc = g.nc
        self.stats = g.sbuf(ctx, "stats", [P, TILES, 6], F32)
        self.mv = g.sbuf(ctx, "mean_var", [P, TILES, 2], F32)
        self.eps = g.sbuf(ctx, "eps", [P, 1], F32)
        self.dev = g.sbuf(ctx, "deviation", [P, TILES], F32)
        self.inv = g.sbuf(ctx, "inverse", [P, TILES], F32)
        self.measured, self.var_ready, self.dev_ready = (
            g.sem(ctx, n) for n in ("measured", "var_ready", "dev_ready"))

    def start(self, step):
        step(self.nc.vector.memset(self.eps[:, :], EPS))

    def take(self, t, value):
        self.nc.vector.bn_stats(self.stats[:, t, :], value).then_inc(self.measured, 1)

    def finish(self, dve, step, rows, done):
        nc = self.nc
        dve.wait_ge(self.measured, TILES)
        for t in range(TILES):
            nc.vector.bn_aggr(self.mv[:, t, :], self.stats[:, t, :]).then_inc(self.var_ready, 1)
        dve.wait_ge(self.dev_ready, 1)
        step(nc.vector.reciprocal(self.inv[:, :], self.dev[:, :]))
        for t in range(TILES):
            nc.vector.tensor_scalar(rows[:, t, :], rows[:, t, :], self.mv[:, t, 0:1], self.inv[:, t:t + 1],
                                    ALU.subtract, ALU.mult).then_inc(done, 1)

    def scalar(self, act):
        act.wait_ge(self.var_ready, TILES)
        self.nc.scalar.activation(self.dev[:, :], self.mv[:, :, 1], ACT.Sqrt, bias=self.eps[:, :])\
            .then_inc(self.dev_ready, 1)


PIECE = 5


def load_pieces(eng, dram, rows, sems):
    for t in range(0, TILES, PIECE):
        eng.dma_start(rows[:, t:t + PIECE, :],
                      dram[t * P:(t + PIECE) * P, :].rearrange("(t p) d -> p t d", p=P)).then_inc(sems[t // PIECE], 16)


def store_pieces(eng, dram, rows, ready, sem):
    nodes, count = dram.shape[0], 0
    for t in range(0, TILES, PIECE):
        eng.wait_ge(ready, t + PIECE)
        full = min(PIECE, nodes // P - t)
        eng.dma_start(dram[t * P:(t + full) * P, :].rearrange("(t p) d -> p t d", p=P),
                      rows[:, t:t + full, :]).then_inc(sem, 16)
        count += 1
        if full < PIECE:
            eng.dma_start(dram[(t + full) * P:nodes, :], rows[0:nodes - (t + full) * P, t + full, :]).then_inc(sem, 16)
            count += 1
    eng.wait_ge(sem, 16 * count)


def load_rows(eng, dram, tile, sem):
    eng.dma_start(tile[:, 0:FULL, :], dram[0:FULL * P, :].rearrange("(t p) d -> p t d", p=P)).then_inc(sem, 16)
    eng.dma_start(tile[0:REST, FULL, :], dram[FULL * P:NODES, :]).then_inc(sem, 16)


def propagate(g, adj, deg, in_deg, x, x1):
    nc = g.nc
    UN, HOPS = 5, 3
    PIECES = TILES // PIECE
    PW = PARTS * D
    with g.phase() as ctx:
        h = [g.sbuf(ctx, "hop_parts", [P, TILES, PW], BF16) for _ in range(2)]
        xin = h[1][:, :, :].rearrange("p t d -> p (t d)").bitcast(F32)[:, 0:TILES * D].rearrange(
            "p (t d) -> p t d", d=D)
        s1 = g.sbuf(ctx, "scale", [P, TILES], F32)
        s2 = g.sbuf(ctx, "scale_sq", [P, TILES], F32)
        val = g.sbuf(ctx, "val", [P, D], F32)
        rest = g.sbuf(ctx, "rest", [P, D], F32)
        unused = g.sbuf(ctx, "unused", [P, NP], BF16)
        norm = AllNorm(g, ctx)
        acc = [g.psum(ctx, "acc", [P, PW], F32) for _ in range(UN)]
        cleared, vec, root = g.sem(ctx, "cleared"), g.sem(ctx, "vec"), g.sem(ctx, "root")
        loaded = [g.sem(ctx, "loaded") for _ in range(PIECES)]
        parts_ready, summed, drained = g.sem(ctx, "parts_ready"), g.sem(ctx, "summed"), g.sem(ctx, "drained")
        degree, again, res_ready, stored = (g.sem(ctx, n) for n in ("degree", "again", "res_ready", "stored"))
        block = ctx.enter_context(nc.Block())

        @block.sync
        def _(sp):
            for q in range(PIECES - 1):
                sp.dma_start(xin[:, q * PIECE:(q + 1) * PIECE, :],
                             x[q * PIECE * P:(q + 1) * PIECE * P, :].rearrange("(t p) d -> p t d", p=P))\
                  .then_inc(loaded[q], 16)
            sp.wait_ge(cleared, 1)
            last = (PIECES - 1) * PIECE
            sp.dma_start(xin[:, last:FULL, :], x[last * P:FULL * P, :].rearrange("(t p) d -> p t d", p=P))\
              .then_inc(loaded[PIECES - 1], 16)
            sp.dma_start(xin[0:REST, FULL, :], x[FULL * P:NODES, :]).then_inc(loaded[PIECES - 1], 16)
            sp.wait_ge(cleared, 2)
            load_rows(sp, x, xin, again)
            store_pieces(sp, x1, xin, res_ready, stored)

        @block.tensor
        def _(pe):
            for hop in range(HOPS):
                if hop >= 1:
                    pe.wait_ge(parts_ready, hop * TILES + PIECES)
                with pe.Fori(0, TILES // UN) as i:
                    for b in range(UN):
                        pe.wait_ge(drained, i * UN + b + hop * TILES + 1)
                        for k in range(TILES):
                            if hop == 0 and k % PIECE == 0:
                                pe.wait_ge(parts_ready, k // PIECE + 1)
                            ins = nc.tensor.matmul(acc[b][:, :], adj[:, k, ds((i * UN + b) * P, P)],
                                                   h[hop % 2][:, k, :], start=(k == 0), stop=(k == TILES - 1))
                        ins.then_inc(summed, 1)

        @block.scalar
        def _(act):
            nc.scalar.activation(s1[:, :], deg[:, :], ACT.Sqrt).then_inc(root, 1)
            for k in range(TILES):
                if k >= 1:
                    act.wait_ge(degree, k)
                nc.scalar.activation(unused[:, :], adj[:, k, :], ACT.Copy, accum_out=in_deg[:, k:k + 1])\
                  .then_inc(degree, 1)
            norm.scalar(act)

        @block.vector
        def _(dve):
            step = Steps(dve, vec)
            dve.sem_inc(drained, UN)
            nc.vector.memset(h[1][:, :, :].rearrange("p t d -> p (t d)").bitcast(U32)[:, FULL * D:TILES * D], 0)\
              .then_inc(cleared, 1)
            norm.start(step)
            dve.wait_ge(root, 1)
            step(nc.vector.reciprocal(s1[:, :], s1[:, :]))
            step(nc.vector.tensor_tensor(s2[:, :], s1[:, :], s1[:, :], ALU.mult))
            for q in range(PIECES):
                a, b = q * PIECE, (q + 1) * PIECE
                dve.wait_ge(loaded[q], 32 if q == PIECES - 1 else 16)
                step(nc.vector.tensor_tensor(xin[:, a:b, :], xin[:, a:b, :],
                                             s1[:, a:b].unsqueeze(2).broadcast_to([P, PIECE, D]), ALU.mult))
                split(step, nc, lambda j: h[0][:, a:b, j * D:(j + 1) * D], xin[:, a:b, :], xin[:, a:b, :])\
                    .then_inc(parts_ready, 1)
                dve.wait_ge(parts_ready, q + 1)

            def total(hop, i, b):
                n = i * UN + b + hop * TILES
                dve.wait_ge(summed, n + 1)
                ins = nc.vector.tensor_reduce(val[:, :], acc[b][:, :].rearrange("p (j d) -> p d j", j=PARTS),
                                              AX.X, ALU.add)
                ins.then_inc(drained, 1)
                dve.wait_ge(drained, n + UN + 1)

            for hop in range(HOPS - 1):
                with dve.Fori(0, TILES // UN) as i:
                    step.enter(i, 4 * UN)
                    for b in range(UN):
                        t = i * UN + b
                        total(hop, i, b)
                        step(nc.vector.tensor_scalar(val[:, :], val[:, :], s2[:, ds(t, 1)], None, ALU.mult))
                        split(step, nc, lambda j: h[1 - hop % 2][:, ds(t, 1), j * D:(j + 1) * D], val[:, :],
                              rest[:, :]).then_inc(parts_ready, 1)
                        dve.wait_ge(parts_ready, t + hop * TILES + PIECES + 1)
                    step.leave(TILES // UN)
            nc.vector.memset(h[1][:, :, :].rearrange("p t d -> p (t d)").bitcast(U32)[:, FULL * D:TILES * D], 0)\
              .then_inc(cleared, 1)
            for t in range(TILES):
                total(HOPS - 1, t // UN, t % UN)
                if t == 0:
                    dve.wait_ge(again, 32)
                step(nc.vector.scalar_tensor_tensor(xin[:, t, :], val[:, :], s1[:, t:t + 1], xin[:, t, :],
                                                    ALU.mult, ALU.add))
                norm.take(t, xin[:, t, :])
            norm.finish(dve, step, xin, res_ready)


ROW = CH + 1


class Attention:

    def __init__(self, g, ctx):
        dram = lambda name, shape: g.nc.dram_tensor(name, shape, F32, kind="Internal").ap()
        self.table = [dram(f"head_rows_{h}", [NP, ROW]) for h in range(HEADS)]
        self.ranked = [dram(f"ranked_rows_{h}", [NP, ROW]) for h in range(HEADS)]
        self.scores = dram("neighbour_scores", [HEADS, NP])
        self.own = g.sbuf(ctx, "own_scores", [P, TILES, HEADS], F32)
        self.theirs = g.sbuf(ctx, "their_scores", [P, TILES, HEADS], F32)


def project(g, att, x1, w, a):
    nc = g.nc
    S, ALL = 2 * HEADS, HEADS * ROW
    with g.phase() as ctx:
        wt = g.sbuf(ctx, "w", [P, D], F32)
        w_turned = g.sbuf(ctx, "w_turned", [P, D], F32)
        a_diag = g.sbuf(ctx, "a_diag", [P, S], F32)
        w_ext = g.sbuf(ctx, "w_ext", [P, ALL + HEADS], F32)
        xt = g.sbuf(ctx, "x_tiles", [P, TILES, D], F32)
        x_turned = g.sbuf(ctx, "x_turned", [P, 2, D], F32)
        rows = g.sbuf(ctx, "rows", [P, TILES, ALL], F32)
        s_row = g.sbuf(ctx, "s_row", [HEADS, NP], F32)
        ps_x = [g.psum(ctx, "ps_x", [P, D], F32) for _ in range(2)]
        ps_h = [g.psum(ctx, "ps_h", [P, ALL + HEADS], F32) for _ in range(2)]
        ps_s = [g.psum(ctx, "ps_s", [HEADS, P], F32) for _ in range(2)]
        cleared, w_loaded, a_loaded, w_ps, w_sb = (
            g.sem(ctx, n) for n in ("cleared", "w_loaded", "a_loaded", "w_ps", "w_sb"))
        loaded = [g.sem(ctx, "loaded") for _ in range(TILES // PIECE)]
        x_ps, x_sb, h_ps, h_sb, own_sb, s_ps, s_sb, stored, kept = (
            g.sem(ctx, n) for n in ("x_ps", "x_sb", "h_ps", "h_sb", "own_sb", "s_ps", "s_sb", "stored", "kept"))
        block = ctx.enter_context(nc.Block())
        by_head = lambda t: t.rearrange("p (h c) -> p h c", c=ROW)

        @block.sync
        def _(sp):
            sp.dma_start(wt[:, :], w).then_inc(w_loaded, 16)
            load_pieces(sp, x1, xt, loaded)
            sp.wait_ge(h_sb, TILES)
            for h in range(HEADS):
                sp.dma_start(att.table[h].rearrange("(t p) c -> p t c", p=P),
                             rows[:, :, h * ROW:(h + 1) * ROW]).then_inc(stored, 16)
            sp.wait_ge(s_sb, TILES)
            sp.dma_start(att.scores, s_row[:, :]).then_inc(stored, 16)
            sp.wait_ge(stored, 16 * (1 + HEADS))

        @block.gpsimd
        def _(pool):
            pool.memset(a_diag[:, :], 0.0).then_inc(cleared, 1)

        @block.tensor
        def _(pe):
            def turn_scores(t):
                pe.wait_ge(h_sb, t + 1)
                if t >= 2:
                    pe.wait_ge(s_sb, t - 1)
                nc.tensor.transpose(ps_s[t % 2][:, :], by_head(rows[:, t, :])[:, :, CH], g.ident[:, :])\
                  .then_inc(s_ps, 1)

            pe.wait_ge(w_loaded, 16)
            nc.tensor.transpose(ps_x[0][:, :], wt[:, :], g.ident[:, :]).then_inc(w_ps, 1)
            pe.wait_ge(w_sb, 1)
            pe.wait_ge(a_loaded, 16 * S)
            nc.tensor.matmul(ps_h[0][:, 0:S], w_turned[:, :], a_diag[:, :], start=True, stop=True).then_inc(w_ps, 1)
            pe.wait_ge(w_sb, 4)
            for t in range(TILES + 1):
                if t < TILES:
                    pe.wait_ge(loaded[t // PIECE], 16)
                    if t >= 2:
                        pe.wait_ge(x_sb, t - 1)
                    nc.tensor.transpose(ps_x[t % 2][:, :], xt[:, t, :], g.ident[:, :]).then_inc(x_ps, 1)
                if t >= 1:
                    pe.wait_ge(x_sb, t)
                    if t >= 3:
                        pe.wait_ge(h_sb, t - 2)
                        pe.wait_ge(own_sb, t - 2)
                    nc.tensor.matmul(ps_h[(t - 1) % 2][:, :], x_turned[:, (t - 1) % 2, :], w_ext[:, :],
                                     start=True, stop=True).then_inc(h_ps, 1)
                if t >= 2:
                    turn_scores(t - 2)
            turn_scores(TILES - 1)

        @block.scalar
        def _(act):
            act.wait_ge(cleared, 1)
            for h in range(HEADS):
                for half in range(2):
                    act.dma_start(a_diag[h * CH:(h + 1) * CH, half * HEADS + h:half * HEADS + h + 1],
                                  a[h:h + 1, half * CH:(half + 1) * CH].rearrange("a c -> c a"),
                                  allow_slow_non_contiguous=True).then_inc(a_loaded, 16)
            for t in range(TILES):
                act.wait_ge(h_ps, t + 1)
                nc.scalar.copy(rows[:, t, :], ps_h[t % 2][:, 0:ALL]).then_inc(h_sb, 1)
                nc.scalar.copy(att.own[:, t, :], ps_h[t % 2][:, ALL:ALL + HEADS]).then_inc(own_sb, 1)

        @block.vector
        def _(dve):
            dve.wait_ge(w_ps, 1)
            nc.vector.tensor_copy(w_turned[:, :], ps_x[0][:, :]).then_inc(w_sb, 1)
            nc.vector.tensor_copy(by_head(w_ext[:, 0:ALL])[:, :, 0:CH],
                                  wt[:, :].rearrange("p (h c) -> p h c", c=CH)).then_inc(w_sb, 1)
            dve.wait_ge(w_ps, 2)
            nc.vector.tensor_copy(w_ext[:, ALL:ALL + HEADS], ps_h[0][:, 0:HEADS]).then_inc(w_sb, 1)
            nc.vector.tensor_copy(by_head(w_ext[:, 0:ALL])[:, :, CH], ps_h[0][:, HEADS:S]).then_inc(w_sb, 1)
            for t in range(TILES + 2):
                if t < TILES:
                    dve.wait_ge(x_ps, t + 1)
                    if t >= 2:
                        dve.wait_ge(h_ps, t - 1)
                    nc.vector.tensor_copy(x_turned[:, t % 2, :], ps_x[t % 2][:, :]).then_inc(x_sb, 1)
                if t >= 2:
                    dve.wait_ge(s_ps, t - 1)
                    nc.vector.tensor_copy(s_row[:, (t - 2) * P:(t - 1) * P], ps_s[t % 2][:, :]).then_inc(s_sb, 1)
            dve.wait_ge(h_sb, TILES)
            nc.vector.tensor_copy(att.theirs[:, :, :],
                                  rows[:, :, :].rearrange("p t (h c) -> p t h c", c=ROW)[:, :, :, CH]).then_inc(kept, 1)
            dve.wait_ge(kept, 1)


def rank(g, att, code):
    nc = g.nc
    SIDE = 5
    HALF = [(0, 13), (13, TILES)]
    PIECES = [[(a, min(a + SIDE, hi)) for a in range(lo, hi, SIDE)] for lo, hi in HALF]
    with g.phase(gpsimd_transfers=True) as ctx:
        score = g.sbuf(ctx, "score", [P, NP], F32)
        below = g.sbuf(ctx, "below", [P, 2, 13 * P], BF16)
        later = g.sbuf(ctx, "later", [P, P], BF16)
        ones = g.sbuf(ctx, "ones", [P, P], BF16)
        banks = [g.psum(ctx, "rank", [P, 512], F32) for _ in range(7)]
        rows = g.sbuf(ctx, "rows", [P, TILES, ROW], F32)
        diagonal = g.sbuf(ctx, "diagonal", [P, SIDE, P], U16)
        own_code = g.sbuf(ctx, "own_code", [P, TILES], F32)
        own_rank = g.sbuf(ctx, "own_rank", [P, TILES], U32)
        masked, added, ranked = g.sem(ctx, "masked"), g.sem(ctx, "added"), g.sem(ctx, "ranked")
        rows_loaded, scattered = g.sem(ctx, "rows_loaded"), g.sem(ctx, "scattered")
        made = g.sem(ctx, "made")
        compared, summed, coded, diag = g.sem(ctx, "compared"), g.sem(ctx, "summed"), g.sem(ctx, "coded"), g.sem(ctx, "diag")
        loaded = [g.sem(ctx, "loaded") for _ in HALF]
        block = ctx.enter_context(nc.Block())

        @block.gpsimd
        def _(pool):
            pool.memset(later[:, :], 1.0).then_inc(made, 1)
            pool.memset(ones[:, :], 1.0).then_inc(made, 1)
            pool.wait_ge(made, 2)
            pool.affine_select(out=later[:, :], in_=later[:, :], compare_op=ALU.is_gt, fill=0.0, base=0,
                               pattern=[[-1, P]], channel_multiplier=1).then_inc(made, 1)
            for h in range(HEADS):
                for k, (lo, hi) in enumerate(HALF):
                    pool.wait_ge(coded, 2 * h + k + 1)
                    for a, b in PIECES[k]:
                        if h + a >= 1:
                            pool.wait_ge(added, h * TILES + a)
                        pool.affine_select(
                            out=diagonal[:, 0:b - a, :].bitcast(I16),
                            in_=code[:, h, a * P:b * P].rearrange("p (t c) -> p t c", c=P).bitcast(I16),
                            compare_op=ALU.is_equal, fill=0.0, base=0, pattern=[[0, b - a], [-1, P]],
                            channel_multiplier=1).then_inc(masked, 1)
                    pool.wait_ge(ranked, 2 * h + k + 1)
                    if k == 0:
                        pool.wait_ge(rows_loaded, 16 * (h + 1))
                    for t in range(lo, hi):
                        pool.indirect_dma_start(att.ranked[h],
                                                bass.IndirectOffsetOnAxis(ap=own_rank[:, t:t + 1], axis=0),
                                                rows[:, t, :], None).then_inc(scattered, 16)
            pool.wait_ge(scattered, 16 * TILES * HEADS)

        @block.sync
        def _(sp):
            for h in range(HEADS):
                for k, (lo, hi) in enumerate(HALF):
                    if h >= 1:
                        sp.wait_ge(compared, (2 * (h - 1) + k + 1) * TILES)
                    sp.dma_start(score[:, lo * P:hi * P],
                                 att.scores[h:h + 1, lo * P:hi * P].broadcast_to([P, (hi - lo) * P])).then_inc(loaded[k], 16)
                if h >= 1:
                    sp.wait_ge(scattered, 16 * TILES * h)
                sp.dma_start(rows[:, :, :], att.table[h].rearrange("(t p) c -> p t c", p=P)).then_inc(rows_loaded, 16)

        def spans(lo, hi):
            first = 0 if lo == 0 else 4
            a = lo * P
            while a < hi * P:
                b = min(a + 512, hi * P)
                yield first + (a - lo * P) // 512, a, b
                a = b

        @block.vector
        def _(dve):
            dve.wait_ge(made, 3)
            n = nd = 0
            for h in range(HEADS):
                for k, (lo, hi) in enumerate(HALF):
                    dve.wait_ge(loaded[k], 16 * (h + 1))
                    for t in range(TILES):
                        if n >= 2:
                            dve.wait_ge(summed, n - 1)
                        buf, s = below[:, n % 2, :], att.theirs[:, t, h:h + 1]
                        left, right = min(max(t, lo), hi), min(max(t + 1, lo), hi)
                        if left < right:
                            out, own = buf[:, (t - lo) * P:(t + 1 - lo) * P], score[:, t * P:(t + 1) * P]
                            nc.vector.scalar_tensor_tensor(out, own, s, later[:, :], ALU.is_ge, ALU.mult)\
                              .then_inc(diag, 1)
                            nd += 1
                        if left > lo:
                            ins = nc.vector.tensor_scalar(buf[:, 0:(left - lo) * P], score[:, lo * P:left * P],
                                                          s, None, ALU.is_ge)
                        if hi > right:
                            ins = nc.vector.tensor_scalar(buf[:, (right - lo) * P:(hi - lo) * P],
                                                          score[:, right * P:hi * P], s, None, ALU.is_gt)
                        if left < right:
                            dve.wait_ge(diag, nd)
                            ins = nc.vector.scalar_tensor_tensor(out, own, s, out, ALU.is_gt, ALU.max)
                        ins.then_inc(compared, 1)
                        n += 1

        @block.tensor
        def _(pe):
            pe.wait_ge(made, 3)
            n = 0
            for h in range(HEADS):
                for k, (lo, hi) in enumerate(HALF):
                    if h >= 1:
                        pe.wait_ge(coded, 2 * (h - 1) + k + 1)
                    for t in range(TILES):
                        pe.wait_ge(compared, n + 1)
                        for bank, a, b in spans(lo, hi):
                            ins = nc.tensor.matmul(banks[bank][:, 0:b - a], ones[:, :],
                                                   below[:, n % 2, a - lo * P:b - lo * P],
                                                   start=(t == 0), stop=(t == TILES - 1))
                        ins.then_inc(summed, 1)
                        n += 1

        @block.scalar
        def _(act):
            pieces = 0
            for h in range(HEADS):
                for k, (lo, hi) in enumerate(HALF):
                    act.wait_ge(summed, (2 * h + k + 1) * TILES)
                    for bank, a, b in spans(lo, hi):
                        ins = nc.scalar.activation(code[:, h, a:b], banks[bank][:, 0:b - a], ACT.Copy,
                                                   bias=15.0, scale=16.0)
                    ins.then_inc(coded, 1)
                    for a, b in PIECES[k]:
                        pieces += 1
                        act.wait_ge(masked, pieces)
                        for t in range(a, b):
                            nc.scalar.activation(diagonal[:, t - a, :], diagonal[:, t - a, :], ACT.Copy,
                                                 accum_out=own_code[:, t:t + 1]).then_inc(added, 1)
                    act.wait_ge(added, h * TILES + hi)
                    if h >= 1 and k == 0:
                        act.wait_ge(scattered, 16 * TILES * h)
                    nc.scalar.activation(own_rank[:, lo:hi], own_code[:, lo:hi], ACT.Copy, bias=-15.0 / 16,
                                         scale=1.0 / 16).then_inc(ranked, 1)
            act.wait_ge(ranked, 2 * HEADS)


def attend(g, att, adj, code, x1, x2):
    nc = g.nc
    HK = HEADS * TOPK
    BANK = 1024
    with g.phase(gpsimd_transfers=True) as ctx:
        mask = g.sbuf(ctx, "mask", [P, NP], I16)
        key = g.sbuf(ctx, "key", [P, NP], U16)
        best = g.sbuf(ctx, "best", [P, 2, HK], U32)
        where = g.sbuf(ctx, "where", [P, 2, HK], U32)
        rows = g.sbuf(ctx, "rows", [P, 2, HK, ROW], F32)
        xt = g.sbuf(ctx, "x_tile", [P, D], F32)
        res = g.sbuf(ctx, "res", [P, D], F32)
        low = g.sbuf(ctx, "low", [P, HK], U32)
        cnt, cum, kept = (g.sbuf(ctx, n, [P, HK], F32) for n in ("cnt", "cum", "kept"))
        again = g.sbuf(ctx, "again", [P, HK], F32)
        e, ez = g.sbuf(ctx, "e", [P, HK], F32), g.sbuf(ctx, "ez", [P, HK], F32)
        den = g.sbuf(ctx, "den", [P, HEADS], F32)
        o, neg = g.sbuf(ctx, "o", [P, D], F32), g.sbuf(ctx, "neg", [P, D], F32)
        norm = Norm(g, ctx)
        edges = [g.psum(ctx, "edges", [P, 4 * BANK], BF16) for _ in range(2)]
        vec, turned, masked, keyed = (g.sem(ctx, n) for n in ("vec", "turned", "masked", "keyed"))
        found, pool_tick = g.sem(ctx, "found"), g.sem(ctx, "pool_tick")
        gathered = [g.sem(ctx, "gathered") for _ in range(2)]
        used = g.sem(ctx, "used")
        e_ready, ez_ready, neg_ready, elu_ready = (g.sem(ctx, n) for n in ("e_ready", "ez_ready", "neg_ready", "elu_ready"))
        x_ready, x_used, res_ready, stored = (g.sem(ctx, n) for n in ("x_ready", "x_used", "res_ready", "stored"))
        block = ctx.enter_context(nc.Block())

        def over_tiles(eng, body, step=None, per=0):
            with eng.Fori(0, TILES // 2) as i:
                if step:
                    step.enter(i, 2 * per)
                for b in range(2):
                    body(i * 2 + b, b)
                if step:
                    step.leave(TILES // 2)
            body(TILES - 1, 0)

        @block.tensor
        def _(pe):
            def tile(q, b):
                pe.wait_ge(masked, q + 1)
                for k in range(TILES):
                    ins = nc.tensor.transpose(edges[b][:, k * P:(k + 1) * P],
                                              adj[:, k, ds(q * P, P)], g.identb[:, :])
                ins.then_inc(turned, 1)
            over_tiles(pe, tile)

        @block.gpsimd
        def _(pool):
            def tile(q, b):
                pool.wait_ge(used, q + 1)
                for h in range(HEADS):
                    pool.wait_ge(found, q * HEADS + h + 1)
                    pool.sem_inc(pool_tick, 1)
                    for k in range(TOPK):
                        j = h * TOPK + k
                        pool.indirect_dma_start(rows[:, b, j, :], None, att.ranked[h],
                                                bass.IndirectOffsetOnAxis(ap=where[:, b, j:j + 1], axis=0))\
                            .then_inc(gathered[b], 16)
            over_tiles(pool, tile)
            for b in range(2):
                pool.wait_ge(gathered[b], (TILES - b + 1) // 2 * HK * 16)

        @block.sync
        def _(sp):
            with sp.Fori(0, TILES) as t:
                sp.wait_ge(x_used, t + 1)
                sp.dma_start(xt[:, :], x1[ds(t * P, P), :]).then_inc(x_ready, 16)
                sp.wait_ge(res_ready, t + 1)
                sp.dma_start(x2[ds(t * P, P), :], res[:, :]).then_inc(stored, 16)
            sp.wait_ge(stored, 16 * TILES + 16)

        @block.scalar
        def _(act):
            with act.Fori(0, TILES) as t:
                act.wait_ge(e_ready, t + 1)
                nc.scalar.activation(ez[:, :], e[:, :], ACT.Exp).then_inc(ez_ready, 1)
                act.wait_ge(neg_ready, t + 1)
                nc.scalar.activation(neg[:, :], neg[:, :], ACT.Exp).then_inc(elu_ready, 1)
                norm.scalar(act, t + 1)

        @block.vector
        def _(dve):
            step = Steps(dve, vec)
            dve.sem_inc(masked, 2)
            dve.sem_inc(used, 2)
            dve.sem_inc(x_used, 1)
            dve.sem_inc(stored, 16)
            norm.start(step)
            step(nc.vector.memset(again[:, :], 1.0))
            step(nc.vector.memset(again[:, :].rearrange("p (h k) -> p h k", k=TOPK)[:, :, 0:1], 0.0))
            heads = lambda t: t.rearrange("p (h k) -> p h k", k=TOPK)

            def search(q, b):
                dve.wait_ge(turned, q + 1)
                nc.vector.tensor_scalar(mask[:, :], edges[b][:, 0:NP], float(TOPK), -1.0, ALU.min, ALU.mult)\
                  .then_inc(masked, 1)
                dve.wait_ge(masked, q + 3)
                for h in range(HEADS):
                    step(nc.vector.tensor_tensor(key[:, :], code[:, h, :], mask[:, :].bitcast(U16),
                                                 ALU.bitwise_and), norm.tick)
                    at = slice(h * TOPK, (h + 1) * TOPK)
                    step(nc.vector.max(best[:, b, at], key[:, :]), norm.tick)
                    nc.vector.tensor_scalar(where[:, b, at], best[:, b, at], 4, None, ALU.arith_shift_right)\
                      .then_inc(found, 1)
                    dve.wait_ge(found, q * HEADS + h + 1)

            def combine(q, b, uses):
                step(nc.vector.tensor_scalar(low[:, :], best[:, b, :], 15, None, ALU.bitwise_and))
                step(nc.vector.tensor_scalar(cnt[:, :], low[:, :], -1.0, 16.0, ALU.mult, ALU.add))
                step(nc.vector.scalar_tensor_tensor(cnt[:, :], best[:, b, :], 0.0, cnt[:, :], ALU.is_gt, ALU.mult))
                step(nc.vector.tensor_tensor_scan(cum[:, :], again[:, :], cnt[:, :], 0.0, ALU.mult, ALU.add))
                step(nc.vector.tensor_tensor(cum[:, :], cum[:, :], cnt[:, :], ALU.subtract))
                step(nc.vector.tensor_scalar(cum[:, :], cum[:, :], -1.0, float(TOPK), ALU.mult, ALU.add))
                step(nc.vector.scalar_tensor_tensor(kept[:, :], cum[:, :], 0.0, cnt[:, :], ALU.max, ALU.min))
                dve.wait_ge(gathered[b], uses * 16 * HK)
                step(nc.vector.tensor_tensor(heads(e[:, :]), heads(rows[:, b, :, CH]),
                                             att.own[:, ds(q, 1), :].rearrange("p a h -> p h a")
                                             .broadcast_to([P, HEADS, TOPK]), ALU.add))
                step(nc.vector.scalar_tensor_tensor(e[:, :], e[:, :], 0.2, e[:, :], ALU.mult, ALU.max))
                step(nc.vector.tensor_tensor(heads(cum[:, :]), heads(e[:, :]),
                                             heads(e[:, :])[:, :, 0:1].broadcast_to([P, HEADS, TOPK]), ALU.subtract))
                nc.vector.tensor_scalar(e[:, :], cum[:, :], 0.0, None, ALU.min).then_inc(e_ready, 1)
                dve.wait_ge(ez_ready, q + 1)
                step(nc.vector.tensor_tensor(ez[:, :], ez[:, :], kept[:, :], ALU.mult))
                step(nc.vector.tensor_reduce(den[:, :], heads(ez[:, :]), AX.X, ALU.add))
                step(nc.vector.reciprocal(den[:, :], den[:, :]))
                step(nc.vector.tensor_tensor(heads(ez[:, :]), heads(ez[:, :]),
                                             den[:, :].unsqueeze(2).broadcast_to([P, HEADS, TOPK]), ALU.mult))
                step(nc.vector.tensor_tensor(rows[:, b, :, 0:CH], rows[:, b, :, 0:CH],
                                             ez[:, :].unsqueeze(2).broadcast_to([P, HK, CH]), ALU.mult))
                nc.vector.tensor_reduce(o[:, :].rearrange("p (h c) -> p h c", h=HEADS),
                                        rows[:, b, :, 0:CH].rearrange("p (h k) c -> p h c k", k=TOPK),
                                        AX.X, ALU.add).then_inc(used, 1)
                dve.wait_ge(used, q + 3)
                nc.vector.tensor_scalar(neg[:, :], o[:, :], 0.0, None, ALU.min).then_inc(neg_ready, 1)
                dve.wait_ge(elu_ready, q + 1)
                step(nc.vector.scalar_tensor_tensor(o[:, :], o[:, :], 0.0, neg[:, :], ALU.max, ALU.add))
                dve.wait_ge(x_ready, q * 16 + 16)
                nc.vector.scalar_tensor_tensor(o[:, :], o[:, :], -1.0, xt[:, :], ALU.add, ALU.add).then_inc(x_used, 1)
                dve.wait_ge(x_used, q + 2)
                dve.wait_ge(stored, q * 16 + 16)
                norm.vector(dve, step, res[:, :], o[:, :], q + 1).then_inc(res_ready, 1)
                dve.wait_ge(res_ready, q + 1)

            per = 8 + 18
            search(0, 0)
            with dve.Fori(0, TILES // 2) as i:
                step.enter(i, 2 * per)
                search(i * 2 + 1, 1)
                combine(i * 2, 0, i + 1)
                search(i * 2 + 2, 0)
                combine(i * 2 + 1, 1, i + 1)
                step.leave(TILES // 2)
            combine(TILES - 1, 0, TILES // 2 + 1)


def gather_sum(g, cols, x, acc):
    width = TYPES * WIN
    nc = g.nc
    RING, UN = 9, 3
    with g.phase(gpsimd_transfers=True) as ctx:
        spot = g.sbuf(ctx, "spot", [P, RING, CHUNKS], U32)
        rows = g.sbuf(ctx, "rows", [P, RING, CHUNKS, D], F32)
        hot = g.sbuf(ctx, "hot", [P, UN, CHUNKS, width], F32)
        sums = [g.psum(ctx, "sums", [P, width], F32) for _ in range(UN)]
        staged, hot_made, summed, added = (g.sem(ctx, n) for n in ("staged", "hot_made", "summed", "added"))
        tick = g.sem(ctx, "tick")
        gathered = [g.sem(ctx, "gathered") for _ in range(RING)]
        block = ctx.enter_context(nc.Block())

        @block.scalar
        def _(act):
            nc.scalar.preload_act_table(ACT.Copy)
            with act.Fori(0, GROUPS // RING) as i:
                for b in range(RING):
                    act.wait_ge(summed, i * RING + b + 1)
                    nc.scalar.copy(spot[:, b, :], cols["source"][:, ds(i * RING + b, 1), :]).then_inc(staged, 1)

        @block.gpsimd
        def _(pool):
            with pool.Fori(0, GROUPS // RING) as i:
                for b in range(RING):
                    pool.wait_ge(staged, i * RING + b + 1)
                    pool.sem_inc(tick, 1)
                    for c in range(CHUNKS):
                        pool.indirect_dma_start(rows[:, b, c, :], None, x,
                                                bass.IndirectOffsetOnAxis(ap=spot[:, b, c:c + 1], axis=0))\
                            .then_inc(gathered[b], 16)
            for b in range(RING):
                pool.wait_ge(gathered[b], GROUPS // RING * CHUNKS * 16)

        @block.vector
        def _(dve):
            dve.sem_inc(summed, RING)
            dve.sem_inc(added, UN)
            with dve.Fori(0, GROUPS // UN) as i:
                def make(b):
                    dve.wait_ge(summed, i * UN + b + 1 + RING - UN)
                    for c in range(CHUNKS):
                        at = cols["typed"][:, ds(i * UN + b, 1), c]
                        ins = nc.vector.tensor_scalar(hot[:, b, c, :], g.keys_row[:, 0:width], at, None,
                                                      ALU.is_equal)
                    ins.then_inc(hot_made, 1)

                def add(b):
                    base = nc.vector.value_load(g.base_row[0:1, ds(i * UN + b, 1)], min_val=0, max_val=NP - WIN)
                    dve.wait_ge(summed, i * UN + b + RING + 1)
                    dve.wait_ge(added, i * UN + b + UN)
                    nc.vector.tensor_tensor(acc[:, :, ds(base, WIN)], acc[:, :, ds(base, WIN)],
                                            sums[b][:, :].rearrange("p (r w) -> p r w", w=WIN),
                                            ALU.add).then_inc(added, 1)

                make(0)
                for b in range(1, UN):
                    make(b)
                    add(b - 1)
                add(UN - 1)

        @block.tensor
        def _(pe):
            with pe.Fori(0, GROUPS // RING) as i:
                for b in range(RING):
                    pe.wait_ge(hot_made, i * RING + b + 1)
                    pe.wait_ge(added, i * RING + b + 1)
                    pe.wait_ge(gathered[b], i * (16 * CHUNKS) + 16 * CHUNKS)
                    for c in range(CHUNKS):
                        ins = nc.tensor.matmul(sums[b % UN][:, :], rows[:, b, c, :], hot[:, b % UN, c, :],
                                               start=(c == 0), stop=(c == CHUNKS - 1))
                    ins.then_inc(summed, 1)


def mixed_sum(g, cols, x, acc):
    nc = g.nc
    GATHER, PLACES = BATCH - DENSE, 4
    SHORT = GROUPS - (PADDED - BATCH)
    LAST_DENSE = min(SHORT // 2, DENSE)
    LAST = SHORT - LAST_DENSE
    ADDS = GATHER + 1
    with g.phase(gpsimd_transfers=True) as ctx:
        rows_x = g.sbuf(ctx, "rows_x", [P, TILES, D], F32)
        weight_part = g.sbuf(ctx, "weight_part", [P, PARTS, PADDED, CHUNKS], F32)
        rounded = g.sbuf(ctx, "rounded", [P, PADDED, CHUNKS], BF16)
        batch_row = g.sbuf(ctx, "batch_row", [1, BATCHES], I32)
        ahead_row = g.sbuf(ctx, "ahead_row", [1, BATCHES, BATCH], I32)
        zeros = g.sbuf(ctx, "zeros", [P, SPAN], F32)
        hot_key = g.sbuf(ctx, "hot_key", [P, PLACES, CHUNKS, KEYS], BF16)
        hot_low = g.sbuf(ctx, "hot_low", [P, PLACES, CHUNKS, PARTS, P], BF16)
        dense = g.sbuf(ctx, "dense", [P, TILES, SPAN], F32)
        spot = g.sbuf(ctx, "spot", [P, GATHER, CHUNKS], U32)
        rows = g.sbuf(ctx, "rows", [P, GATHER, CHUNKS, D], F32)
        hot = g.sbuf(ctx, "hot", [P, GATHER, CHUNKS, WIN], F32)
        count = [g.psum(ctx, "count", [P, KEYS], F32) for _ in range(2)]
        sums = [g.psum(ctx, "sums", [P, WIN], F32) for _ in range(2)]
        product = g.psum(ctx, "product", [P, SPAN], F32)
        vec, x_loaded, ready = g.sem(ctx, "vec"), g.sem(ctx, "x_loaded"), g.sem(ctx, "ready")
        dense_made, dense_used = g.sem(ctx, "dense_made"), g.sem(ctx, "dense_used")
        put, multiplied = g.sem(ctx, "put"), g.sem(ctx, "multiplied")
        staged, hot_made, summed, added, tick = (
            g.sem(ctx, n) for n in ("staged", "hot_made", "summed", "added", "tick"))
        gathered = [g.sem(ctx, "gathered") for _ in range(GATHER)]
        block = ctx.enter_context(nc.Block())

        @block.sync
        def _(sp):
            sp.dma_start(rows_x[:, :, :], x.rearrange("(t p) d -> p t d", p=P)).then_inc(x_loaded, 16)

        @block.scalar
        def _(act):
            nc.scalar.preload_act_table(ACT.Copy)

            def stage(i, j, dense_before):
                act.wait_ge(summed, i * GATHER + j + 1)
                nc.scalar.copy(spot[:, j, :], cols["source"][:, ds(i * BATCH + dense_before + j, 1), :])\
                  .then_inc(staged, 1)

            def batch(i, dense_groups, next_gathers, next_dense):
                act.wait_ge(multiplied, i + 1)
                nc.scalar.copy(dense[:, :, :], zeros[:, :].unsqueeze(1).broadcast_to([P, TILES, SPAN])).then_inc(put, 1)
                for j in range(max(dense_groups, next_gathers)):
                    if j < dense_groups:
                        ahead = nc.scalar.value_load(ahead_row[0:1, ds(i, 1), j], min_val=0, max_val=SPAN - WIN)
                        act.wait_ge(dense_used, i * DENSE + j + 1 + PLACES)
                        if j == 0:
                            act.wait_ge(put, i * (DENSE + 1) + 2)
                        nc.scalar.copy(dense[:, :, ds(ahead, WIN)],
                                       count[j % 2][:, :].rearrange("p (t w) -> p t w", w=WIN)).then_inc(put, 1)
                    if j < next_gathers:
                        stage(i + 1, j, next_dense)

            for j in range(GATHER):
                stage(0, j, DENSE)
            act.wait_ge(ready, 1)
            with act.Fori(0, BATCHES - 2) as i:
                batch(i, DENSE, GATHER, DENSE)
            batch(BATCHES - 2, DENSE, LAST, LAST_DENSE)
            batch(BATCHES - 1, LAST_DENSE, 0, 0)

        @block.gpsimd
        def _(pool):
            def gather(i, j):
                pool.wait_ge(staged, i * GATHER + j + 1)
                pool.sem_inc(tick, 1)
                for c in range(CHUNKS):
                    pool.indirect_dma_start(rows[:, j, c, :], None, x,
                                            bass.IndirectOffsetOnAxis(ap=spot[:, j, c:c + 1], axis=0))\
                        .then_inc(gathered[j], 16)

            with pool.Fori(0, BATCHES - 1) as i:
                for j in range(GATHER):
                    gather(i, j)
            for j in range(LAST):
                gather(BATCHES - 1, j)
            for j in range(GATHER):
                pool.wait_ge(gathered[j], (BATCHES - (j >= LAST)) * CHUNKS * 16)

        @block.vector
        def _(dve):
            step = Steps(dve, vec)
            dve.sem_inc(summed, GATHER)
            dve.sem_inc(added, 2)
            dve.sem_inc(dense_used, PLACES)
            dve.sem_inc(put, 1)
            dve.sem_inc(multiplied, 1)
            step(nc.vector.memset(zeros[:, :], 0.0))
            groups = g.base_row[:, 0:PADDED].rearrange("a (i b) -> a i b", b=BATCH)
            step(nc.vector.tensor_scalar(batch_row[:, :], groups[:, :, 0], float(NP - SPAN), None, ALU.min))
            step(nc.vector.tensor_tensor(ahead_row[:, :, :], groups,
                                         batch_row[:, :].unsqueeze(2).broadcast_to([1, BATCHES, BATCH]),
                                         ALU.subtract))
            rest = cols["weight"][:, :, :]
            for j in range(PARTS):
                step(nc.vector.tensor_copy(rounded[:, :, :], rest))
                step(nc.vector.tensor_copy(weight_part[:, j, :, :], rounded[:, :, :]))
                if j < PARTS - 1:
                    step(nc.vector.tensor_tensor(weight_part[:, PARTS - 1, :, :], rest, weight_part[:, j, :, :],
                                                 ALU.subtract))
                    rest = weight_part[:, PARTS - 1, :, :]
            dve.sem_inc(ready, 1)

            def make_dense(i, j):
                dve.wait_ge(dense_used, i * DENSE + j + 1)
                for c in range(CHUNKS):
                    nc.vector.tensor_scalar(hot_key[:, j % PLACES, c, :], g.keys_row[:, 0:KEYS],
                                            cols["key"][:, ds(i * BATCH + j, 1), c], None, ALU.is_equal)
                    for part in range(PARTS):
                        ins = nc.vector.tensor_scalar(hot_low[:, j % PLACES, c, part, :], g.keys_row[:, 0:P],
                                                      cols["low"][:, ds(i * BATCH + j, 1), c],
                                                      weight_part[:, part, ds(i * BATCH + j, 1), c],
                                                      ALU.is_equal, ALU.mult)
                ins.then_inc(dense_made, 1)

            def make_hot(i, j, dense_before):
                dve.wait_ge(summed, i * GATHER + j + 1)
                for c in range(CHUNKS):
                    ins = nc.vector.tensor_scalar(hot[:, j, c, :], g.keys_row[:, 0:WIN],
                                                  cols["place"][:, ds(i * BATCH + dense_before + j, 1), c],
                                                  cols["weight"][:, ds(i * BATCH + dense_before + j, 1), c],
                                                  ALU.is_equal, ALU.mult)
                ins.then_inc(hot_made, 1)

            def add_sums(i, j, dense_before, place):
                base = nc.vector.value_load(g.base_row[0:1, ds(i * BATCH + dense_before + j, 1)], min_val=0,
                                            max_val=NP - WIN)
                dve.wait_ge(summed, i * GATHER + j + GATHER + 1)
                dve.wait_ge(added, i * ADDS + place + 2)
                nc.vector.tensor_tensor(acc[:, 0, ds(base, WIN)], acc[:, 0, ds(base, WIN)], sums[j % 2][:, :],
                                        ALU.add).then_inc(added, 1)

            def add_product(i, place):
                base = nc.vector.value_load(batch_row[0:1, ds(i, 1)], min_val=0, max_val=NP - SPAN)
                dve.wait_ge(multiplied, i + 2)
                dve.wait_ge(added, i * ADDS + place + 2)
                nc.vector.tensor_tensor(acc[:, 0, ds(base, SPAN)], acc[:, 0, ds(base, SPAN)], product[:, :],
                                        ALU.add).then_inc(added, 1)

            def batch(i, dense_groups, gathers, next_dense, next_gathers):
                for j in range(max(dense_groups, gathers - 1)):
                    if j < gathers - 1:
                        add_sums(i, j, dense_groups, j)
                    if j + PLACES < dense_groups:
                        make_dense(i, j + PLACES)
                    elif j < dense_groups and j + PLACES - dense_groups < next_dense:
                        make_dense(i + 1, j + PLACES - dense_groups)
                    if j < next_gathers:
                        make_hot(i + 1, j, next_dense)
                add_product(i, gathers - 1)
                add_sums(i, gathers - 1, dense_groups, gathers)
                if gathers - 1 < next_gathers:
                    make_hot(i + 1, gathers - 1, next_dense)

            for j in range(GATHER):
                if j < PLACES:
                    make_dense(0, j)
                make_hot(0, j, DENSE)
            with dve.Fori(0, BATCHES - 2) as i:
                batch(i, DENSE, GATHER, DENSE, GATHER)
            batch(BATCHES - 2, DENSE, GATHER, LAST_DENSE, LAST)
            batch(BATCHES - 1, LAST_DENSE, LAST, 0, 0)

        @block.tensor
        def _(pe):
            pe.wait_ge(ready, 1)
            pe.wait_ge(x_loaded, 16)

            def count_edges(i, j):
                if j >= 1:
                    ahead = nc.tensor.value_load(ahead_row[0:1, ds(i, 1), j], min_val=0, max_val=SPAN - WIN)
                pe.wait_ge(dense_made, i * DENSE + j + 1)
                pe.wait_ge(put, i * (DENSE + 1) + (1 if j < 2 else j + 1))
                for c in range(CHUNKS):
                    for part in range(PARTS):
                        ins = nc.tensor.matmul(
                            count[j % 2][:, :], hot_low[:, j % PLACES, c, part, :], hot_key[:, j % PLACES, c, :],
                            start=(c == 0 and part == 0), stop=(j == 0 and c == CHUNKS - 1 and part == PARTS - 1))
                if j >= 1:
                    pe.wait_ge(put, i * (DENSE + 1) + j + 2)
                    ins = nc.tensor.matmul(count[j % 2][:, :], g.ident[:, :], dense[:, :, ds(ahead, WIN)],
                                           start=False, stop=True)
                ins.then_inc(dense_used, 1)

            def sum_rows(i, j):
                pe.wait_ge(hot_made, i * GATHER + j + 1)
                pe.wait_ge(added, i * ADDS + j + 1)
                pe.wait_ge(gathered[j], i * (16 * CHUNKS) + 16 * CHUNKS)
                for c in range(CHUNKS):
                    ins = nc.tensor.matmul(sums[j % 2][:, :], rows[:, j, c, :], hot[:, j, c, :],
                                           start=(c == 0), stop=(c == CHUNKS - 1))
                ins.then_inc(summed, 1)

            def batch(i, dense_groups, gathers):
                for j in range(max(dense_groups, gathers - 1)):
                    if j < dense_groups:
                        count_edges(i, j)
                    if j < gathers - 1:
                        sum_rows(i, j)
                pe.wait_ge(put, i * (DENSE + 1) + dense_groups + 2)
                pe.wait_ge(added, i * ADDS + 2)
                for k in range(TILES):
                    ins = nc.tensor.matmul(product[:, :], rows_x[:, k, :], dense[:, k, :], start=(k == 0),
                                           stop=(k == TILES - 1))
                ins.then_inc(multiplied, 1)
                sum_rows(i, gathers - 1)

            with pe.Fori(0, BATCHES - 1) as i:
                batch(i, DENSE, GATHER)
            batch(BATCHES - 1, LAST_DENSE, LAST)


def combine_layer(g, acc, w_agg, w_self, self_turned, bias, x, out, in_deg, clear):
    nc = g.nc
    R = w_agg.shape[0]
    with g.phase() as ctx:
        wt = g.sbuf(ctx, "w_agg", [P, R, D], F32)
        ws = g.sbuf(ctx, "w_self", [P, D], F32)
        ws_in = g.sbuf(ctx, "w_self_in", [P, D], F32)
        brow = g.sbuf(ctx, "bias_row", [1, D], F32)
        ones = g.sbuf(ctx, "ones", [1, P], F32)
        inv = g.sbuf(ctx, "inverse_degree", [P, TILES], F32)
        rows = g.sbuf(ctx, "rows", [P, TILES, D], F32)
        x_turned = g.sbuf(ctx, "x_turned", [P, 2, D], F32)
        part = g.sbuf(ctx, "part", [P, 2, D], F32)
        val = g.sbuf(ctx, "val", [P, D], F32)
        norm = AllNorm(g, ctx)
        ps_x = [g.psum(ctx, "ps_x", [P, D], F32) for _ in range(2)]
        ps_a = [g.psum(ctx, "ps_agg", [P, D], F32) for _ in range(2)]
        ps_s = [g.psum(ctx, "ps_self", [P, D], F32) for _ in range(2)]
        w_loaded, vec, w_ps, w_sb = (g.sem(ctx, n) for n in ("w_loaded", "vec", "w_ps", "w_sb"))
        loaded = [g.sem(ctx, "loaded") for _ in range(TILES // PIECE)]
        x_ps, x_sb, summed, part_made, used, res_ready, stored = (
            g.sem(ctx, n) for n in ("x_ps", "x_sb", "summed", "part_made", "used", "res_ready", "stored"))
        zeroed = g.sem(ctx, "zeroed")
        block = ctx.enter_context(nc.Block())

        @block.sync
        def _(sp):
            sp.dma_start(ws_in[:, :], w_self).then_inc(w_loaded, 16)
            sp.dma_start(brow[:, :], bias.rearrange("(a n) -> a n", a=1)).then_inc(w_loaded, 16)
            sp.dma_start(wt[:, :, :], w_agg.rearrange("r i o -> i r o")).then_inc(w_loaded, 16)
            load_pieces(sp, x, rows, loaded)
            store_pieces(sp, out, rows, res_ready, stored)

        @block.gpsimd
        def _(pool):
            for t in clear:
                pool.memset(t, 0.0).then_inc(zeroed, 1)
            if clear:
                pool.wait_ge(zeroed, len(clear))

        @block.tensor
        def _(pe):
            def turn_x(t):
                pe.wait_ge(loaded[t // PIECE], 16)
                if t >= 2:
                    pe.wait_ge(x_sb, t - 1)
                nc.tensor.transpose(ps_x[t % 2][:, :], rows[:, t, :], g.ident[:, :]).then_inc(x_ps, 1)

            pe.wait_ge(w_loaded, 48)
            pe.wait_ge(vec, 1)
            if self_turned:
                nc.tensor.transpose(ps_x[0][:, :], ws_in[:, :], g.ident[:, :]).then_inc(w_ps, 1)
            pe.wait_ge(w_sb, 1)
            turn_x(0)
            for t in range(TILES):
                b = t % 2
                if t + 1 < TILES:
                    turn_x(t + 1)
                if t >= 2:
                    pe.wait_ge(used, t - 1)
                for r in range(R):
                    nc.tensor.matmul(ps_a[b][:, :], acc[:, r, t * P:(t + 1) * P], wt[:, r, :],
                                     start=(r == 0), stop=(r == R - 1))
                nc.tensor.matmul(ps_s[b][:, :], ones[:, :], brow[:, :], start=True, stop=False)
                pe.wait_ge(x_sb, t + 1)
                nc.tensor.matmul(ps_s[b][:, :], x_turned[:, b, :], ws[:, :], start=False, stop=True)\
                  .then_inc(summed, 1)

        @block.scalar
        def _(act):
            for t in range(TILES + 1):
                if t < TILES:
                    act.wait_ge(x_ps, t + 1)
                    if t >= 2:
                        act.wait_ge(summed, t - 1)
                    nc.scalar.copy(x_turned[:, t % 2, :], ps_x[t % 2][:, :]).then_inc(x_sb, 1)
                if t >= 1:
                    b = (t - 1) % 2
                    act.wait_ge(summed, t)
                    if t >= 3:
                        act.wait_ge(used, t - 2)
                    if in_deg is None:
                        ins = nc.scalar.copy(part[:, b, :], ps_a[b][:, :])
                    else:
                        ins = nc.scalar.activation(part[:, b, :], ps_a[b][:, :], ACT.Copy, scale=inv[:, t - 1:t])
                    ins.then_inc(part_made, 1)
            norm.scalar(act)

        @block.vector
        def _(dve):
            step = Steps(dve, vec)
            step(nc.vector.memset(ones[:, :], 1.0))
            norm.start(step)
            if in_deg is not None:
                step(nc.vector.tensor_scalar(inv[:, :], in_deg, -1.0, 1.0, ALU.add, ALU.max))
                step(nc.vector.reciprocal(inv[:, :], inv[:, :]))
            dve.wait_ge(w_loaded, 48)
            if self_turned:
                dve.wait_ge(w_ps, 1)
                nc.vector.tensor_copy(ws[:, :], ps_x[0][:, :]).then_inc(w_sb, 1)
            else:
                nc.vector.tensor_copy(ws[:, :], ws_in[:, :]).then_inc(w_sb, 1)
            for t in range(TILES):
                b = t % 2
                dve.wait_ge(part_made, t + 1)
                step(nc.vector.tensor_tensor(val[:, :], part[:, b, :], ps_s[b][:, :], ALU.add))
                if in_deg is None:
                    ins = nc.vector.tensor_tensor(rows[:, t, :], val[:, :], rows[:, t, :], ALU.add)
                else:
                    ins = nc.vector.scalar_tensor_tensor(rows[:, t, :], val[:, :], 0.0, rows[:, t, :],
                                                         ALU.max, ALU.add)
                ins.then_inc(used, 1)
                dve.wait_ge(used, t + 1)
                norm.take(t, rows[:, t, :])
            norm.finish(dve, step, rows, res_ready)


def clear_tiles(g, tiles):
    nc = g.nc
    with g.phase() as ctx:
        zeroed = g.sem(ctx, "zeroed")
        block = ctx.enter_context(nc.Block())

        @block.vector
        def _(dve):
            for t in tiles:
                nc.vector.memset(t, 0).then_inc(zeroed, 1)
            dve.wait_ge(zeroed, len(tiles))


def gnn(nc, x, src, dst, edge_type, edge_weight, att_w, att_a, w_neigh, w_self, b_self, w_rel, w_root, b_root, out):
    hidden = [nc.dram_tensor(f"x{n}", [NP, D], F32, kind="Internal").ap() for n in (1, 2, 3)]
    with ExitStack() as ctx:
        g = Graph(nc, ctx, src, dst, edge_type, edge_weight)
        out_deg, in_deg = g.sbuf(ctx, "out_deg", [P, TILES], F32), g.sbuf(ctx, "in_deg", [P, TILES], F32)
        constants(g)
        with ExitStack() as mid:
            adj = g.sbuf(mid, "adj", [P, TILES, NP], BF16)
            window_bases(g, adj[:, :, :].rearrange("p k n -> p (k n)").bitcast(F32))

            def work():
                with ExitStack() as inner:
                    cols = edge_columns(g, inner, ("low", "key"))
                    group_keys(g, cols)
                    add_edges(g, adj, cols["low"], cols["key"])

            in_windows(g, work)
            out_degrees(g, adj, out_deg)
            turn(g, adj)
            propagate(g, adj, out_deg, in_deg, x, hidden[0])
            att = Attention(g, mid)
            project(g, att, hidden[0], att_w, att_a)
            code = g.sbuf(mid, "code", [P, HEADS, NP], U16)
            rank(g, att, code)
            attend(g, att, adj, code, hidden[0], hidden[1])
        cols = edge_columns(g, ctx, ("low", "key", "place", "weight", "source", "typed"))
        weighted = g.sbuf(ctx, "weighted", [P, 1, NP], F32)
        clear_tiles(g, [weighted[:, :, :].bitcast(U32), g.next_base[:, :].bitcast(U32)])

        def weigh():
            group_keys(g, cols)
            mixed_sum(g, cols, hidden[1], weighted)

        in_windows(g, weigh)
        by_type = g.sbuf(ctx, "by_type", [P, TYPES, NP], F32)
        combine_layer(g, weighted, w_neigh.rearrange("(r i) o -> r i o", r=1), w_self, False, b_self,
                      hidden[1], hidden[2], None, [by_type[:, :, :], g.next_base[:, :]])

        def gather():
            gather_sum(g, cols, hidden[2], by_type)

        def columns_and_gather():
            group_keys(g, {kind: cols[kind] for kind in ("typed", "source")})
            gather()

        in_windows(g, columns_and_gather, gather)
        combine_layer(g, by_type, w_rel, w_root, True, b_root, hidden[2], out, in_deg[:, :], [])


_INS = ['x', 'src', 'dst', 'edge_type_8', 'edge_weight', 'L1_gnn_W', 'L1_gnn_att', 'L2_gnn_W_neigh',
        'L2_gnn_W_self', 'L2_gnn_b_self', 'L3_gnn_W_rel', 'L3_gnn_W_self_w', 'L3_gnn_W_self_b']


def kernel(**inputs):
    import numpy as np
    import concourse.bacc as bacc
    from concourse.bass_utils import run_bass_kernel_spmd

    nc = bacc.Bacc("TRN2", target_bir_lowering=False, num_devices=1)
    arrays, args = {}, []
    for name in _INS:
        a = np.ascontiguousarray(inputs[name])
        arrays[f"in_{name}"] = a
        args.append(nc.dram_tensor(f"in_{name}", a.shape, mybir.dt.from_np(a.dtype), kind="ExternalInput").ap())
    out = nc.dram_tensor("out", (NODES, D), F32, kind="ExternalOutput").ap()
    gnn(nc, *args, out)
    r = run_bass_kernel_spmd(nc, [arrays], core_ids=[0])
    return r.results[0]["out"]
```
